# Optimizing a Trainium2 kernel written in Bass

```python
import numpy as np
import jax
import jax.numpy as jnp

def _softmax(x, axis=-1):
    return jax.nn.softmax(x, axis=axis)

def _gelu(x):
    return jax.nn.gelu(x, approximate=True)

def _silu(x):
    return jax.nn.silu(x)

def _sigmoid(x):
    return jax.nn.sigmoid(x)

def _layernorm(x, axis=-1, eps=1e-05):
    m = jnp.mean(x, axis=axis, keepdims=True)
    v = jnp.var(x, axis=axis, keepdims=True)
    return (x - m) / jnp.sqrt(v + eps)

def _scatter_add(tgt, idx, src, axis=0):
    return tgt.at[idx].add(src)

def _segment_sum(src, seg, n):
    return jax.ops.segment_sum(src, seg, n)
kernel_name = 'mk_early_fusion_d2_tok_img768_r4_7629ee'

def setup_inputs(seed: int=0):
    np.random.seed(seed)
    _w = jnp.asarray

    def _rec_inputs():
        import jax
        import jax.numpy as jnp
        _rk = jax.random.key(seed)
        x = -7.10856e-05 + 0.999911 * jax.random.normal(jax.random.fold_in(_rk, 1), (4, 32, 128, 128), jnp.float32)
        txt = -0.00271877 + 0.451779 * jax.random.normal(jax.random.fold_in(_rk, 2), (4, 32, 192), jnp.float32)
        return (x, txt)
    x, txt = _rec_inputs()

    def _L0_tok_setup():
        import jax, jax.numpy as jnp
        import numpy as np
        B, C, H, W = (8, 32, 128, 128)
        P = 8
        D = 128
        NH, DH = (8, 64)
        M = 512
        L = 2
        DOUT = 192
        INNER = NH * DH

        def _ln(x, g, b, eps=1e-05):
            mu = x.mean(-1, keepdims=True)
            xc = x - mu
            var = (xc * xc).mean(-1, keepdims=True)
            return xc * jax.lax.rsqrt(var + eps) * g + b

        def _forward(im, conv_w, conv_b, ln1_g, ln1_b, qkv_w, out_w, out_b, ln2_g, ln2_b, ff1_w, ff1_b, ff2_w, ff2_b, lnf_g, lnf_b, head_w, head_b):
            b, c, h, w = im.shape
            hp, wp = (h // P, w // P)
            patches = im.reshape(b, c, hp, P, wp, P)
            x = jnp.einsum('bchpwq,dcpq->bhwd', patches, conv_w)
            x = x.reshape(b, hp * wp, -1) + conv_b
            n = hp * wp
            scale = DH ** (-0.5)
            for i in range(ln1_g.shape[0]):
                y = _ln(x, ln1_g[i], ln1_b[i])
                qkv = y @ qkv_w[i]
                q, k, v = jnp.split(qkv, 3, axis=-1)
                to_heads = lambda t: t.reshape(b, n, NH, DH).transpose(0, 2, 1, 3)
                q, k, v = (to_heads(q), to_heads(k), to_heads(v))
                q = jax.nn.softmax(q, axis=-1) * scale
                k = jax.nn.softmax(k, axis=-2)
                ctx = jnp.einsum('bhnd,bhne->bhde', k, v)
                att = jnp.einsum('bhnd,bhde->bhne', q, ctx)
                att = att.transpose(0, 2, 1, 3).reshape(b, n, INNER)
                x = x + att @ out_w[i] + out_b[i]
                y = _ln(x, ln2_g[i], ln2_b[i])
                hdn = jax.nn.gelu(y @ ff1_w[i] + ff1_b[i], approximate=False)
                x = x + hdn @ ff2_w[i] + ff2_b[i]
            return _ln(x, lnf_g, lnf_b) @ head_w + head_b
        key = jax.random.key(seed)
        ks = iter(jax.random.split(key, 32))
        g = lambda shape, s=0.02: (jax.random.normal(next(ks), shape) * s).astype(jnp.float32)
        inp = {'im': jax.random.normal(next(ks), (B, C, H, W), dtype=jnp.float32), 'conv_w': g((D, C, P, P)), 'conv_b': jnp.zeros((D,), jnp.float32), 'ln1_g': jnp.ones((L, D), jnp.float32), 'ln1_b': jnp.zeros((L, D), jnp.float32), 'qkv_w': g((L, D, 3 * INNER)), 'out_w': g((L, INNER, D)), 'out_b': jnp.zeros((L, D), jnp.float32), 'ln2_g': jnp.ones((L, D), jnp.float32), 'ln2_b': jnp.zeros((L, D), jnp.float32), 'ff1_w': g((L, D, M)), 'ff1_b': jnp.zeros((L, M), jnp.float32), 'ff2_w': g((L, M, D)), 'ff2_b': jnp.zeros((L, D), jnp.float32), 'lnf_g': jnp.ones((D,), jnp.float32), 'lnf_b': jnp.zeros((D,), jnp.float32), 'head_w': g((D, DOUT)), 'head_b': jnp.zeros((DOUT,), jnp.float32)}
        return inp
    _L0_tok_all = _L0_tok_setup()
    _L0_tok_in = {k: v for k, v in _L0_tok_all.items() if k in ('conv_w', 'conv_b', 'ln1_g', 'ln1_b', 'qkv_w', 'out_w', 'out_b', 'ln2_g', 'ln2_b', 'ff1_w', 'ff1_b', 'ff2_w', 'ff2_b', 'lnf_g', 'lnf_b', 'head_w', 'head_b')}
    del _L0_tok_all

    def _L0_attn_setup():
        import jax, jax.numpy as jnp
        import numpy as np
        DIM, HEADS = (192, 12)
        key = jax.random.key(seed)
        ks = jax.random.split(key, 9)
        B, N, C, H = (4, 256, DIM, HEADS)
        s = 0.02
        return {'x': jax.random.normal(ks[0], (B, N, C), jnp.float32), 'W_qkv': jax.random.normal(ks[1], (C, 3 * C), jnp.float32) * s, 'W_proj': jax.random.normal(ks[2], (C, C), jnp.float32) * s, 'b_proj': jax.random.normal(ks[3], (C,), jnp.float32) * s, 'W_l': jax.random.normal(ks[4], (H, H), jnp.float32) * s, 'b_l': jax.random.normal(ks[5], (H,), jnp.float32) * s, 'W_w': jax.random.normal(ks[6], (H, H), jnp.float32) * s, 'b_w': jax.random.normal(ks[7], (H,), jnp.float32) * s, 'lamb': jax.random.normal(ks[8], (H,), jnp.float32) * 0.1}
    _L0_attn_all = _L0_attn_setup()
    _L0_attn_in = {k: v for k, v in _L0_attn_all.items() if k in ('W_qkv', 'W_proj', 'b_proj', 'W_l', 'b_l', 'W_w', 'b_w', 'lamb')}
    del _L0_attn_all

    def _L0_ffn_setup():
        import jax, jax.numpy as jnp
        import numpy as np
        B, N, DIM, HEADS = (4, 256, 192, 12)
        HIDDEN, E, TOPK = (768, 8, 2)
        EPS = 1e-05

        def _layernorm(x, g, b):
            mu = jnp.mean(x, axis=-1, keepdims=True)
            var = jnp.var(x, axis=-1, keepdims=True)
            return (x - mu) * jax.lax.rsqrt(var + EPS) * g + b
        key = jax.random.key(seed)
        ks = jax.random.split(key, 10)
        s = 0.02
        return {'x': jax.random.normal(ks[0], (B, N, DIM), dtype=jnp.float32), 'ln1_g': jnp.ones((DIM,), jnp.float32), 'ln1_b': jnp.zeros((DIM,), jnp.float32), 'qkv_w': jax.random.normal(ks[1], (3 * DIM, DIM), jnp.float32) * s, 'proj_w': jax.random.normal(ks[2], (DIM, DIM), jnp.float32) * s, 'proj_b': jnp.zeros((DIM,), jnp.float32), 'ln2_g': jnp.ones((DIM,), jnp.float32), 'ln2_b': jnp.zeros((DIM,), jnp.float32), 'gate_w': jax.random.normal(ks[3], (E, DIM), jnp.float32) * s, 'gate_b': jnp.zeros((E,), jnp.float32), 'w1': jax.random.normal(ks[4], (E, HIDDEN, DIM), jnp.float32) * s, 'b1': jnp.zeros((E, HIDDEN), jnp.float32), 'w2': jax.random.normal(ks[5], (E, DIM, HIDDEN), jnp.float32) * s, 'b2': jnp.zeros((E, DIM), jnp.float32)}
    _L0_ffn_all = _L0_ffn_setup()
    _L0_ffn_in = {k: v for k, v in _L0_ffn_all.items() if k in ('ln1_g', 'ln1_b', 'qkv_w', 'proj_w', 'proj_b', 'ln2_g', 'ln2_b', 'gate_w', 'gate_b', 'w1', 'b1', 'w2', 'b2')}
    del _L0_ffn_all

    def _L1_attn_setup():
        import jax, jax.numpy as jnp
        import numpy as np
        B, C, D = (8, 512, 192)
        EPS = 1e-05
        key = jax.random.key(seed)
        kx, kk, kq, kv = jax.random.split(key, 4)
        x = jax.random.normal(kx, (B, C, D), dtype=jnp.float32)
        s = 1.0 / np.sqrt(D)
        Wk = jax.random.uniform(kk, (D, D), dtype=jnp.float32, minval=-s, maxval=s)
        Wq = jax.random.uniform(kq, (D, D), dtype=jnp.float32, minval=-s, maxval=s)
        Wv = jax.random.uniform(kv, (D, D), dtype=jnp.float32, minval=-s, maxval=s)
        return {'x': x, 'Wk': Wk, 'Wq': Wq, 'Wv': Wv}
    _L1_attn_all = _L1_attn_setup()
    _L1_attn_in = {k: v for k, v in _L1_attn_all.items() if k in ('Wk', 'Wq', 'Wv')}
    del _L1_attn_all

    def _L1_ffn_setup():
        import jax, jax.numpy as jnp
        import numpy as np
        B, S, D, F, E = (2, 256, 192, 768, 8)
        key = jax.random.key(seed)
        k0, k1, k2, k3, k4, k5 = jax.random.split(key, 6)
        scale = 0.02
        return {'hidden_states': jax.random.normal(k0, (B, S, D), dtype=jnp.float32), 'Wg': jax.random.normal(k1, (D, E), dtype=jnp.float32) * scale, 'W1': jax.random.normal(k2, (E, D, F), dtype=jnp.float32) * scale, 'b1': jnp.zeros((E, F), dtype=jnp.float32), 'W2': jax.random.normal(k3, (E, F, D), dtype=jnp.float32) * scale, 'b2': jnp.zeros((E, D), dtype=jnp.float32)}
    _L1_ffn_all = _L1_ffn_setup()
    _L1_ffn_in = {k: v for k, v in _L1_ffn_all.items() if k in ('Wg', 'W1', 'b1', 'W2', 'b2')}
    del _L1_ffn_all
    return {'x': x, 'txt': txt, 'L0_tok_conv_w': _L0_tok_in['conv_w'], 'L0_tok_conv_b': _L0_tok_in['conv_b'], 'L0_tok_ln1_g': _L0_tok_in['ln1_g'], 'L0_tok_ln1_b': _L0_tok_in['ln1_b'], 'L0_tok_qkv_w': _L0_tok_in['qkv_w'], 'L0_tok_out_w': _L0_tok_in['out_w'], 'L0_tok_out_b': _L0_tok_in['out_b'], 'L0_tok_ln2_g': _L0_tok_in['ln2_g'], 'L0_tok_ln2_b': _L0_tok_in['ln2_b'], 'L0_tok_ff1_w': _L0_tok_in['ff1_w'], 'L0_tok_ff1_b': _L0_tok_in['ff1_b'], 'L0_tok_ff2_w': _L0_tok_in['ff2_w'], 'L0_tok_ff2_b': _L0_tok_in['ff2_b'], 'L0_tok_lnf_g': _L0_tok_in['lnf_g'], 'L0_tok_lnf_b': _L0_tok_in['lnf_b'], 'L0_tok_head_w': _L0_tok_in['head_w'], 'L0_tok_head_b': _L0_tok_in['head_b'], 'L0_attn_W_qkv': _L0_attn_in['W_qkv'], 'L0_attn_W_proj': _L0_attn_in['W_proj'], 'L0_attn_b_proj': _L0_attn_in['b_proj'], 'L0_attn_W_l': _L0_attn_in['W_l'], 'L0_attn_b_l': _L0_attn_in['b_l'], 'L0_attn_W_w': _L0_attn_in['W_w'], 'L0_attn_b_w': _L0_attn_in['b_w'], 'L0_attn_lamb': _L0_attn_in['lamb'], 'L0_ffn_ln1_g': _L0_ffn_in['ln1_g'], 'L0_ffn_ln1_b': _L0_ffn_in['ln1_b'], 'L0_ffn_qkv_w': _L0_ffn_in['qkv_w'], 'L0_ffn_proj_w': _L0_ffn_in['proj_w'], 'L0_ffn_proj_b': _L0_ffn_in['proj_b'], 'L0_ffn_ln2_g': _L0_ffn_in['ln2_g'], 'L0_ffn_ln2_b': _L0_ffn_in['ln2_b'], 'L0_ffn_gate_w': _L0_ffn_in['gate_w'], 'L0_ffn_gate_b': _L0_ffn_in['gate_b'], 'L0_ffn_w1': _L0_ffn_in['w1'], 'L0_ffn_b1': _L0_ffn_in['b1'], 'L0_ffn_w2': _L0_ffn_in['w2'], 'L0_ffn_b2': _L0_ffn_in['b2'], 'L1_attn_Wk': _L1_attn_in['Wk'], 'L1_attn_Wq': _L1_attn_in['Wq'], 'L1_attn_Wv': _L1_attn_in['Wv'], 'L1_ffn_Wg': _L1_ffn_in['Wg'], 'L1_ffn_W1': _L1_ffn_in['W1'], 'L1_ffn_b1': _L1_ffn_in['b1'], 'L1_ffn_W2': _L1_ffn_in['W2'], 'L1_ffn_b2': _L1_ffn_in['b2']}

def reference(x, txt, L0_tok_conv_w, L0_tok_conv_b, L0_tok_ln1_g, L0_tok_ln1_b, L0_tok_qkv_w, L0_tok_out_w, L0_tok_out_b, L0_tok_ln2_g, L0_tok_ln2_b, L0_tok_ff1_w, L0_tok_ff1_b, L0_tok_ff2_w, L0_tok_ff2_b, L0_tok_lnf_g, L0_tok_lnf_b, L0_tok_head_w, L0_tok_head_b, L0_attn_W_qkv, L0_attn_W_proj, L0_attn_b_proj, L0_attn_W_l, L0_attn_b_l, L0_attn_W_w, L0_attn_b_w, L0_attn_lamb, L0_ffn_ln1_g, L0_ffn_ln1_b, L0_ffn_qkv_w, L0_ffn_proj_w, L0_ffn_proj_b, L0_ffn_ln2_g, L0_ffn_ln2_b, L0_ffn_gate_w, L0_ffn_gate_b, L0_ffn_w1, L0_ffn_b1, L0_ffn_w2, L0_ffn_b2, L1_attn_Wk, L1_attn_Wq, L1_attn_Wv, L1_ffn_Wg, L1_ffn_W1, L1_ffn_b1, L1_ffn_W2, L1_ffn_b2):
    import jax
    import jax.numpy as jnp

    def _L0_tok_ref(im, conv_w, conv_b, ln1_g, ln1_b, qkv_w, out_w, out_b, ln2_g, ln2_b, ff1_w, ff1_b, ff2_w, ff2_b, lnf_g, lnf_b, head_w, head_b):
        import jax, jax.numpy as jnp
        import numpy as np
        B, C, H, W = (8, 32, 128, 128)
        P = 8
        D = 128
        NH, DH = (8, 64)
        M = 512
        L = 2
        DOUT = 192
        INNER = NH * DH

        def _ln(x, g, b, eps=1e-05):
            mu = x.mean(-1, keepdims=True)
            xc = x - mu
            var = (xc * xc).mean(-1, keepdims=True)
            return xc * jax.lax.rsqrt(var + eps) * g + b

        def _forward(im, conv_w, conv_b, ln1_g, ln1_b, qkv_w, out_w, out_b, ln2_g, ln2_b, ff1_w, ff1_b, ff2_w, ff2_b, lnf_g, lnf_b, head_w, head_b):
            b, c, h, w = im.shape
            hp, wp = (h // P, w // P)
            patches = im.reshape(b, c, hp, P, wp, P)
            x = jnp.einsum('bchpwq,dcpq->bhwd', patches, conv_w)
            x = x.reshape(b, hp * wp, -1) + conv_b
            n = hp * wp
            scale = DH ** (-0.5)
            for i in range(ln1_g.shape[0]):
                y = _ln(x, ln1_g[i], ln1_b[i])
                qkv = y @ qkv_w[i]
                q, k, v = jnp.split(qkv, 3, axis=-1)
                to_heads = lambda t: t.reshape(b, n, NH, DH).transpose(0, 2, 1, 3)
                q, k, v = (to_heads(q), to_heads(k), to_heads(v))
                q = jax.nn.softmax(q, axis=-1) * scale
                k = jax.nn.softmax(k, axis=-2)
                ctx = jnp.einsum('bhnd,bhne->bhde', k, v)
                att = jnp.einsum('bhnd,bhde->bhne', q, ctx)
                att = att.transpose(0, 2, 1, 3).reshape(b, n, INNER)
                x = x + att @ out_w[i] + out_b[i]
                y = _ln(x, ln2_g[i], ln2_b[i])
                hdn = jax.nn.gelu(y @ ff1_w[i] + ff1_b[i], approximate=False)
                x = x + hdn @ ff2_w[i] + ff2_b[i]
            return _ln(x, lnf_g, lnf_b) @ head_w + head_b
        return _forward(im, conv_w, conv_b, ln1_g, ln1_b, qkv_w, out_w, out_b, ln2_g, ln2_b, ff1_w, ff1_b, ff2_w, ff2_b, lnf_g, lnf_b, head_w, head_b)

    def _L0_attn_ref(x, W_qkv, W_proj, b_proj, W_l, b_l, W_w, b_w, lamb):
        import jax, jax.numpy as jnp
        import numpy as np
        DIM, HEADS = (192, 12)
        B, N, C = x.shape
        H = W_l.shape[0]
        d = C // H
        scale = d ** (-0.5)
        qkv = (x @ W_qkv).reshape(B, N, 3, H, d)
        q = qkv[:, :, 0].transpose(0, 2, 1, 3) * scale
        k = qkv[:, :, 1].transpose(0, 2, 1, 3)
        v = qkv[:, :, 2].transpose(0, 2, 1, 3)
        attn = jnp.einsum('bhnd,bhmd->bhnm', q, k)
        attn = jnp.einsum('bhnm,hg->bgnm', attn, W_l) + b_l[None, :, None, None]
        attn = jax.nn.softmax(attn, axis=-1)
        attn = jnp.einsum('bhnm,hg->bgnm', attn, W_w) + b_w[None, :, None, None]
        eye = jnp.eye(N, dtype=attn.dtype)
        reaction = 3.0 * jnp.einsum('bhnk,bhkm->bhnm', attn - eye, attn) + attn
        attn = attn + lamb[None, :, None, None] * reaction
        out = jnp.einsum('bhnm,bhmd->bhnd', attn, v)
        out = out.transpose(0, 2, 1, 3).reshape(B, N, C)
        return out @ W_proj + b_proj

    def _L0_ffn_ref(x, ln1_g, ln1_b, qkv_w, proj_w, proj_b, ln2_g, ln2_b, gate_w, gate_b, w1, b1, w2, b2):
        import jax, jax.numpy as jnp
        import numpy as np
        B, N, DIM, HEADS = (4, 256, 192, 12)
        HIDDEN, E, TOPK = (768, 8, 2)
        EPS = 1e-05

        def _layernorm(x, g, b):
            mu = jnp.mean(x, axis=-1, keepdims=True)
            var = jnp.var(x, axis=-1, keepdims=True)
            return (x - mu) * jax.lax.rsqrt(var + EPS) * g + b
        b, n, d = x.shape
        hd = d // HEADS
        scale = hd ** (-0.5)
        h = _layernorm(x, ln1_g, ln1_b)
        qkv = h @ qkv_w.T
        qkv = qkv.reshape(b, n, 3, HEADS, hd).transpose(2, 0, 3, 1, 4)
        q, k, v = (qkv[0], qkv[1], qkv[2])
        attn = jax.nn.softmax(jnp.einsum('bhnd,bhmd->bhnm', q, k) * scale, axis=-1)
        a = jnp.einsum('bhnm,bhmd->bhnd', attn, v)
        a = a.transpose(0, 2, 1, 3).reshape(b, n, d)
        a = a @ proj_w.T + proj_b
        x = x + a
        h2 = _layernorm(x, ln2_g, ln2_b)
        t = h2.reshape(-1, d)
        T = t.shape[0]
        logits = t @ gate_w.T + gate_b
        top_val, top_idx = jax.lax.top_k(logits, TOPK)
        score = jax.nn.softmax(top_val, axis=-1)
        cw = jnp.zeros((T, E), t.dtype).at[jnp.arange(T)[:, None], top_idx].add(score)
        out = jnp.zeros_like(t)
        for e in range(E):
            he = jax.nn.gelu(t @ w1[e].T + b1[e], approximate=False)
            ye = he @ w2[e].T + b2[e]
            out = out + cw[:, e:e + 1] * ye
        return x + out.reshape(b, n, d)

    def _L1_attn_ref(x, Wk, Wq, Wv):
        import jax, jax.numpy as jnp
        import numpy as np
        B, C, D = (8, 512, 192)
        EPS = 1e-05
        mean = jnp.mean(x, axis=(-2, -1), keepdims=True)
        var = jnp.mean(jnp.square(x - mean), axis=(-2, -1), keepdims=True)
        xn = (x - mean) * jax.lax.rsqrt(var + EPS)
        keys = jnp.einsum('bcd,od->bco', xn, Wk)
        queries = jnp.einsum('bcd,od->bco', xn, Wq)
        values = jnp.einsum('bcd,od->bco', xn, Wv)
        att = jax.nn.softmax(jnp.einsum('bid,bjd->bij', queries, keys), axis=-1)
        return jnp.einsum('bjd,bij->bid', values, att)

    def _L1_ffn_ref(hidden_states, Wg, W1, b1, W2, b2):
        import jax, jax.numpy as jnp
        import numpy as np
        B, S, D, F, E = (2, 256, 192, 768, 8)
        b, s, d = hidden_states.shape
        e = W1.shape[0]
        x = hidden_states.reshape(-1, d)
        logits = x @ Wg
        probs = jax.nn.softmax(logits, axis=-1)
        gate = jnp.max(probs, axis=-1)
        expert_idx = jnp.argmax(probs, axis=-1)
        h = jax.nn.silu(jnp.einsum('td,edf->etf', x, W1) + b1[:, None, :])
        y = jnp.einsum('etf,efd->etd', h, W2) + b2[:, None, :]
        combine = jax.nn.one_hot(expert_idx, e, dtype=x.dtype) * gate[:, None]
        out = jnp.einsum('te,etd->td', combine, y)
        return out.reshape(b, s, d)
    h = _L0_tok_ref(x, L0_tok_conv_w, L0_tok_conv_b, L0_tok_ln1_g, L0_tok_ln1_b, L0_tok_qkv_w, L0_tok_out_w, L0_tok_out_b, L0_tok_ln2_g, L0_tok_ln2_b, L0_tok_ff1_w, L0_tok_ff1_b, L0_tok_ff2_w, L0_tok_ff2_b, L0_tok_lnf_g, L0_tok_lnf_b, L0_tok_head_w, L0_tok_head_b)
    h = jnp.concatenate([h, txt], axis=1)
    h = h + _L0_attn_ref(_layernorm(h, axis=-1), L0_attn_W_qkv, L0_attn_W_proj, L0_attn_b_proj, L0_attn_W_l, L0_attn_b_l, L0_attn_W_w, L0_attn_b_w, L0_attn_lamb)
    h = h + _L0_ffn_ref(_layernorm(h, axis=-1), L0_ffn_ln1_g, L0_ffn_ln1_b, L0_ffn_qkv_w, L0_ffn_proj_w, L0_ffn_proj_b, L0_ffn_ln2_g, L0_ffn_ln2_b, L0_ffn_gate_w, L0_ffn_gate_b, L0_ffn_w1, L0_ffn_b1, L0_ffn_w2, L0_ffn_b2)
    h = h + _L1_attn_ref(_layernorm(h, axis=-1), L1_attn_Wk, L1_attn_Wq, L1_attn_Wv)
    h = h + _L1_ffn_ref(_layernorm(h, axis=-1), L1_ffn_Wg, L1_ffn_W1, L1_ffn_b1, L1_ffn_W2, L1_ffn_b2)
    return h

_drawn_inputs = setup_inputs


def setup_inputs(seed=0):
    import zlib

    import numpy as np

    out = dict(_drawn_inputs(seed))
    spreads = {'L0_tok_conv_b': (0.0, 0.1),
     'L0_tok_ln1_g': (1.0, 0.6),
     'L0_tok_ln1_b': (0.0, 0.8),
     'L0_tok_out_b': (0.0, 0.1),
     'L0_tok_ln2_g': (1.0, 0.6),
     'L0_tok_ln2_b': (0.0, 0.425),
     'L0_tok_ff1_b': (0.0, 0.1),
     'L0_tok_ff2_b': (0.0, 0.1),
     'L0_tok_lnf_g': (1.0, 0.2),
     'L0_tok_lnf_b': (0.0, 0.1),
     'L0_tok_head_b': (0.0, 0.1),
     'L0_ffn_ln1_g': (1.0, 0.6),
     'L0_ffn_ln1_b': (0.0, 0.8),
     'L0_ffn_proj_b': (0.0, 0.1),
     'L0_ffn_ln2_g': (1.0, 0.6),
     'L0_ffn_ln2_b': (0.0, 0.572),
     'L0_ffn_gate_b': (0.0, 0.1),
     'L0_ffn_b1': (0.0, 0.536),
     'L0_ffn_b2': (0.0, 0.1),
     'L1_ffn_b1': (0.0, 0.8),
     'L1_ffn_b2': (0.0, 0.708)}
    factors = {'L0_tok_qkv_w': 5.698,
     'L0_tok_out_w': 7.533,
     'L0_attn_W_l': 8.0,
     'L0_attn_b_l': 8.0,
     'L0_attn_W_w': 8.0,
     'L1_ffn_Wg': 4.083,
     'L1_ffn_W1': 6.313,
     'L1_ffn_W2': 6.145}
    for name, (base, spread) in spreads.items():
        noise = np.random.default_rng([zlib.crc32(name.encode()), seed]).standard_normal(out[name].shape)
        drawn = base * np.exp(spread * noise) if base else spread * noise
        out[name] = jnp.asarray(drawn.astype(out[name].dtype))
    for name, factor in factors.items():
        out[name] = (out[name] * factor).astype(out[name].dtype)
    return out
```

```python
from contextlib import ExitStack

import concourse.bass as bass
from concourse import mybir

F32 = mybir.dt.float32
U32 = mybir.dt.uint32
ACT = mybir.ActivationFunctionType
ALU = mybir.AluOpType
AX = mybir.AxisListType

B = 4
D = 128
KC = 16
NI = 256
TI = B * NI
VT = TI // 128
L = 2
NH, DH = 8, 64
INNER = NH * DH
M = 512
NC4 = INNER // 128
C = 192
CP = 96
CK = C // CP
N = 288
NT = N // CP
T = B * N
TT = B * NT
H = 12
HD = 16
HP = 32
HG = H // 4
RT = 9
MR = H * RT
JT = N // RT
EX = 8
F = 768
FC = F // 128
TG = 384
GT = TG // CP
NG = T // TG
EPS = 1e-5
POWER = [0, 1, 2, 3, 4, 5, 6, 7, 8, 9, None, 10]

V_CONV, V_G1, V_B1, V_G2, V_B2, V_GF, V_BF, V_F1 = 0, 1, 3, 5, 7, 9, 10, 11
V_END = V_F1 + L * NC4
R_OUT = 0
R_FF2 = R_OUT + L * D
R_HEAD = R_FF2 + L * D
R_P0 = R_HEAD + C
R_P1 = R_P0 + C
R_LAM = R_P1 + C
R_GB = R_LAM + H
R_END = R_GB + EX

LD_FUSED = 16 * (3 + 4 + 4 + 2 + 6)


def build(nc, a, out):
    with ExitStack() as ctx:
        def sb(name, shape, dt=F32):
            return ctx.enter_context(nc.sbuf_tensor(name, shape, dt))

        def sem(name):
            return ctx.enter_context(nc.semaphore(name))

        bank = [ctx.enter_context(nc.psum_tensor(f"bank{i}", [128, 512], F32)) for i in range(8)]

        ident = sb("ident", [128, 128])
        ones = sb("ones", [128, 128])
        vec = sb("vec", [128, V_END])
        row = sb("row", [128, R_END])
        big = sb("big", [128, 16384])
        patches = big[:, :].rearrange("p (k t) -> p k t", k=KC)
        expkT = big[:, 0:4096].rearrange("p (c t) -> p c t", c=NC4)
        expk = big[:, 4096:8192].rearrange("p (t c) -> p t c", t=VT)
        v_v = big[:, 8192:12288].rearrange("p (t c) -> p t c", t=VT)
        qT_v = big[:, 12288:16384].rearrange("p (c t) -> p c t", c=NC4)
        gmat = big[:, 0:2048].rearrange("p (b c d) -> p b c d", b=B, c=NC4)
        low = sb("low", [128, 14848])
        at = [0]

        def low_part(n):
            at[0] += n
            assert at[0] <= 14848, at[0]
            return low[:, at[0] - n:at[0]]

        convw = low_part(KC * D).rearrange("p (k d) -> p k d", k=KC)
        ctxT = convw.rearrange("p (b c) d -> p b c d", b=B)
        wqkv = [low_part(3 * INNER) for _ in range(L)]
        wout = [low_part(NC4 * D).rearrange("p (c d) -> p c d", c=NC4) for _ in range(L)]
        wff1 = [low_part(M) for _ in range(L)]
        wff2 = [low_part(NC4 * D).rearrange("p (c d) -> p c d", c=NC4) for _ in range(L)]
        x = low_part(TI).rearrange("p (t d) -> p t d", t=VT)
        xT = low_part(TI)
        q_v = low_part(VT * INNER).rearrange("p (t c) -> p t c", t=VT)
        hid_v = q_v.rearrange("p t c -> p (t c)").rearrange("p (c t) -> p c t", c=NC4)
        at[0] = 0
        qT = low_part(CK * T).rearrange("p (c t) -> p c t", c=CK)
        kT = low_part(CK * T).rearrange("p (c t) -> p c t", c=CK)
        y = sb("y", [128, TT * C])
        yT = sb("yT", [128, CK * T])
        uT = y[:, 0:HG * N].rearrange("p (g n) -> p g n", g=HG)
        zT = y[:, HG * N:2 * HG * N].rearrange("p (g n) -> p g n", g=HG)
        oT = yT[:, 0:HG * N].rearrange("p (g n) -> p g n", g=HG)
        znat = yT[0:CP, HG * N:HG * N + NT * H * HP].rearrange("p (c h d) -> p c h d", c=NT, h=H)
        vpad = low_part(TT * H * HP).rearrange("p (t h d) -> p t h d", t=TT, h=H)
        experts = [low_part(CK * F + FC * C + FC) for _ in range(2)]
        ew1 = [e[0:CP, 0:CK * F].rearrange("p (k f) -> p k f", k=CK) for e in experts]
        ew2 = [e[:, CK * F:CK * F + FC * C].rearrange("p (f c) -> p f c", f=FC) for e in experts]
        eb1 = [e[:, CK * F + FC * C:] for e in experts]
        AT = big[0:CP, 0:NT * H * N].rearrange("p (c h n) -> p c h n", c=NT, h=H)
        P4 = [big[0:CP, NT * N * j:NT * N * (j + 1)].rearrange("p (i n) -> p i n", i=NT) for j in range(8)]
        qh4 = [big[0:CP, 8 * NT * N + N * j:8 * NT * N + N * (j + 1)] for j in range(4)]
        vh4 = [big[0:CP, 8 * NT * N + 4 * N + NT * HP * j:8 * NT * N + 4 * N + NT * HP * (j + 1)]
               .rearrange("p (c d) -> p c d", c=NT) for j in range(4)]
        oT4 = big[:, 8448:8448 + B * HG * N].rearrange("p (b g n) -> p b g n", b=B, g=HG)
        P1 = big[0:CP, 0:TT * N].rearrange("p (t n) -> p t n", t=TT)
        PT1 = big[0:CP, TT * N:2 * TT * N].rearrange("p (t n) -> p t n", t=TT)
        v1 = vpad.rearrange("p t h d -> p (t h d)")[0:CP, 0:TT * C].rearrange("p (t c) -> p t c", t=TT)
        hid2 = [big[:, FC * TG * j:FC * TG * (j + 1)].rearrange("p (f t) -> p f t", f=FC) for j in range(2)]

        y_v = y[:, 0:TI].rearrange("p (t d) -> p t d", t=VT)
        y96 = y[0:CP, :].rearrange("p (t c) -> p t c", t=TT)
        yT_v = yT[:, 0:TI]
        yT96 = yT[0:CP, :].rearrange("p (c t) -> p c t", c=CK)
        h = sb("h", [CP, TT, C])
        z = sb("z", [CP, TT, C])
        headw = sb("headw", [128, C])
        wqkv96 = [sb(f"wqkv96_{i}", [CP, CK, 3 * C]) for i in range(3)]
        wproj = [sb(f"wproj{i}", [128, HG, C]) for i in range(2)]
        wlT = sb("wlT", [CP, CK, H])
        wmix = sb("wmix", [MR + 1, MR])
        wdelta = sb("wdelta", [MR + 1, MR])
        lam = sb("lam", [128, HG])
        lam_a = sb("lam_a", [128, HG])
        lam_b = sb("lam_b", [128, HG])
        qg = [sb(f"qg{i}", [CP + 1, CK, MR]) for i in range(4)]
        pt = [sb(f"pt{i}", [MR + 1, N]) for i in range(4)]
        wms = [sb(f"wms{i}", [MR + 1, MR]) for i in range(4)]
        rs = [sb(f"rs{i}", [MR + 1, 1]) for i in range(4)]
        sums = [sb(f"sums{i}", [128, 1]) for i in range(4)]
        nm = [sb(f"nm{i}", [128, 1]) for i in range(4)]
        hmask = sb("hmask", [CP, CK, H // CK])
        vec96 = sb("vec96", [CP, 4, CK])
        gate_w = [sb(f"gate_w{i}", [CP, CK, EX]) for i in range(2)]
        b2 = [sb(f"b2_{i}", [EX, C]) for i in range(2)]
        lg = sb("lg", [CP, TT, EX])
        oh = sb("oh", [CP, TT, EX])
        cw = sb("cw", [CP, TT, EX])
        top = sb("top", [CP, TT, EX])
        topi = sb("topi", [CP, TT, EX], U32)
        iota8 = sb("iota8", [CP, EX])
        s12 = sb("s12", [CP, TT])
        s12b = sb("s12b", [CP, TT])
        cwT = sb("cwT", [EX, T])
        nmh = sb("nmh", [CP, 4, NT])
        sumh = sb("sumh", [CP, 4, NT])
        rsh = sb("rsh", [CP, 4, NT])
        ms = sb("ms", [CP, 2 * B])
        msm = sb("msm", [CP, 2 * B])
        bstat = sb("bstat", [CP, B, 2])
        bve = sb("bve", [CP, B])
        brs = sb("brs", [CP, B])
        nm1 = sb("smax1", [CP, TT])
        sum1 = sb("sum1", [CP, TT])
        rec1 = sb("rec1", [CP, TT])
        st = sb("st", [128, TT, 6])
        mv = sb("mv", [128, TT, 2])
        ve = sb("ve", [128, TT])
        rstd = sb("rstd", [128, TT])
        mhalf = sb("mhalf", [128, TT])
        nkmax = sb("nkmax", [128, 16])
        ksum = sb("ksum", [128, 16])
        krec = sb("krec", [128, 16])
        qmax = sb("qmax", [128, 8, NH])
        qsum = sb("qsum", [128, 8, NH])
        qrec = sb("qrec", [128, 8, NH])

        ld_row = sem("ld_row")
        ld_conv = sem("ld_conv")
        ld_patch = [sem(f"ld_patch{i}") for i in range(8)]
        ld_layer = [sem(f"ld_layer{i}") for i in range(L)]
        ld_head = sem("ld_head")
        consts_ready = sem("consts_ready")
        mm_act = sem("mm_act")
        mm_dve = sem("mm_dve")
        act_evac = sem("act_evac")
        dve_evac = sem("dve_evac")
        ln_var = sem("ln_var")
        ln_rstd = sem("ln_rstd")
        ln_y = sem("ln_y")
        dve_step = sem("dve_step")
        kmax_ready = sem("kmax_ready")
        q_exp = sem("q_exp")
        q_norm = sem("q_norm")
        ctx_zeroed = sem("ctx_zeroed")
        pool_step = sem("pool_step")
        ld_fused = sem("ld_fused")
        fused_consts = sem("fused_consts")
        wmix_ready = sem("wmix_ready")
        tk_q = sem("tk_q")
        tk_s = sem("tk_s")
        tk_max = sem("tk_max")
        tk_exp = sem("tk_exp")
        tk_r = sem("tk_r")
        tk_w = sem("tk_w")
        tk_mix = sem("tk_mix")
        tk_at = sem("tk_at")
        z_ready = sem("z_ready")
        o_ready = sem("o_ready")
        mh_q = sem("mh_q")
        mh_s = sem("mh_s")
        mh_v = sem("mh_v")
        mh_max = sem("mh_max")
        mh_exp = sem("mh_exp")
        mh_r = sem("mh_r")
        mh_p = sem("mh_p")
        mh_t = sem("mh_t")
        mh_pt = sem("mh_pt")
        mh_o = sem("mh_o")
        mh_oT = sem("mh_oT")
        sa_max = sem("sa_max")
        sa_exp = sem("sa_exp")
        bn_stat = sem("bn_stat")
        bn_var = sem("bn_var")
        bn_rstd = sem("bn_rstd")
        gate_e = sem("gate_e")
        gate_x = sem("gate_x")
        cw_ready = sem("cw_ready")
        ld_exp = [sem(f"ld_exp{i}") for i in range(2)]
        ex_hid = [sem(f"ex_hid{i}") for i in range(2)]
        ex_act = [sem(f"ex_act{i}") for i in range(2)]
        ex_y = [sem(f"ex_y{i}") for i in range(2)]
        ex_add = [sem(f"ex_add{i}") for i in range(2)]
        stored = sem("stored")

        block = ctx.enter_context(nc.Block())

        made = {"act": 0, "dve": 0}
        read = {"act": 0, "dve": 0}
        ready_at, free_at, lies_in = {}, {}, {}
        holder = [None] * 8
        evac = {"act": act_evac, "dve": dve_evac}
        mm_ready = {"act": mm_act, "dve": mm_dve}

        @block.tensor
        def _(pe):
            turn = [0]

            def claim(key, reader, last=None):
                i = turn[0] % 8
                turn[0] += 1
                if holder[i]:
                    pe.wait_ge(evac[holder[i][0]], holder[i][1])
                last = last or reader
                made[reader] += 1
                read[last] += 1
                ready_at[key], free_at[key], lies_in[key] = made[reader], read[last], i
                holder[i] = (last, read[last])
                return bank[i]

            def done(mm, reader):
                mm.then_inc(mm_ready[reader], 1)

            pe.wait_ge(ld_conv, 16)
            halves = [claim(("conv", i), "act") for i in range(2)]
            for k in range(KC):
                if k % 2 == 0:
                    pe.wait_ge(ld_patch[k // 2], 16)
                for i in range(2):
                    mm = pe.matmul(halves[i][:, :], convw[:, k, :], patches[:, k, 512 * i:512 * i + 512],
                                   start=(k == 0), stop=(k == KC - 1))
                    if k == KC - 1:
                        done(mm, "act")
            pe.wait_ge(consts_ready, 1)
            for b in range(B):
                pe.wait_ge(act_evac, free_at[("conv", b // 2)])
                ps = claim(("x", b), "dve")
                for i in range(2):
                    t = 2 * b + i
                    mm = pe.transpose(ps[:, 128 * i:128 * i + 128], xT[:, 128 * t:128 * t + 128], ident[:, :])
                done(mm, "dve")

            def turn_tokens(n):
                for b in range(B):
                    pe.wait_ge(ln_y, B * n + b + 1)
                    ps = claim(("yT", n, b), "act")
                    for i in range(2):
                        mm = pe.transpose(ps[:, 128 * i:128 * i + 128], y_v[:, 2 * b + i, :], ident[:, :])
                    done(mm, "act")

            for l in range(L):
                turn_tokens(2 * l)
                pe.wait_ge(ld_layer[l], 64)
                w = wqkv[l]
                for b in range(B):
                    pe.wait_ge(act_evac, free_at[("yT", 2 * l, b)])
                    for p in range(2):
                        ps = claim(("k", l, b, p), "dve", "act")
                        for i in range(2):
                            c = 2 * p + i
                            mm = pe.matmul(ps[:, NI * i:NI * i + NI], w[:, INNER + 128 * c:INNER + 128 * c + 128],
                                           yT_v[:, NI * b:NI * b + NI], start=True, stop=True)
                        done(mm, "dve")
                for t in range(VT):
                    ps = claim(("q", l, t), "dve")
                    done(pe.matmul(ps[:, :], yT_v[:, 128 * t:128 * t + 128], w[:, 0:INNER],
                                   start=True, stop=True), "dve")
                    ps = claim(("v", l, t), "act")
                    done(pe.matmul(ps[:, :], yT_v[:, 128 * t:128 * t + 128], w[:, 2 * INNER:3 * INNER],
                                   start=True, stop=True), "act")
                for t in range(VT):
                    pe.wait_ge(act_evac, free_at[("k", l, t // 2, 1)])
                    ps = claim(("kt", l, t), "act")
                    for c in range(NC4):
                        mm = pe.transpose(ps[:, 128 * c:128 * c + 128], expkT[:, c, 128 * t:128 * t + 128],
                                          ident[:, :])
                    done(mm, "act")
                for b in range(B):
                    pe.wait_ge(act_evac, free_at[("kt", l, 2 * b + 1)])
                    ps = claim(("ctx", l, b), "dve")
                    for c in range(NC4):
                        for i in range(2):
                            t = 2 * b + i
                            mm = pe.matmul(ps[:, 128 * c:128 * c + 128], v_v[:, t, 128 * c:128 * c + 128],
                                           expk[:, t, 128 * c:128 * c + 128], start=(i == 0), stop=(i == 1))
                    done(mm, "dve")
                for t in range(VT):
                    pe.wait_ge(q_norm, VT * l + t + 1)
                    ps = claim(("qT", l, t), "act")
                    for c in range(NC4):
                        mm = pe.transpose(ps[:, 128 * c:128 * c + 128], q_v[:, t, 128 * c:128 * c + 128],
                                          ident[:, :])
                    done(mm, "act")
                for b in range(B):
                    pe.wait_ge(dve_evac, free_at[("ctx", l, b)])
                    ps = claim(("g", l, b), "dve")
                    for c in range(NC4):
                        mm = pe.matmul(ps[:, 128 * c:128 * c + 128], ctxT[:, b, c, :], wout[l][:, c, :],
                                       start=True, stop=True)
                    done(mm, "dve")
                for b in range(B):
                    pe.wait_ge(dve_evac, free_at[("g", l, b)])
                    ps = claim(("o", l, b), "dve")
                    for i in range(2):
                        t = 2 * b + i
                        pe.wait_ge(act_evac, free_at[("qT", l, t)])
                        for c in range(NC4):
                            mm = pe.matmul(ps[:, 128 * i:128 * i + 128], qT_v[:, c, 128 * t:128 * t + 128],
                                           gmat[:, b, c, :], start=(c == 0), stop=(c == NC4 - 1))
                    done(mm, "dve")
                turn_tokens(2 * l + 1)
                for b in range(B):
                    pe.wait_ge(act_evac, free_at[("yT", 2 * l + 1, b)])
                    for p in range(2):
                        ps = claim(("f1", l, b, p), "act")
                        for i in range(2):
                            c = 2 * p + i
                            mm = pe.matmul(ps[:, NI * i:NI * i + NI], wff1[l][:, 128 * c:128 * c + 128],
                                           yT_v[:, NI * b:NI * b + NI], start=True, stop=True)
                        done(mm, "act")
                for b in range(B):
                    pe.wait_ge(act_evac, free_at[("f1", l, b, 1)])
                    ps = claim(("f2", l, b), "dve")
                    for i in range(2):
                        t = 2 * b + i
                        for c in range(NC4):
                            mm = pe.matmul(ps[:, 128 * i:128 * i + 128], hid_v[:, c, 128 * t:128 * t + 128],
                                           wff2[l][:, c, :], start=(c == 0), stop=(c == NC4 - 1))
                    done(mm, "dve")
            turn_tokens(2 * L)
            pe.wait_ge(ld_head, 16 * (1 + B))
            for b in range(B):
                pe.wait_ge(act_evac, free_at[("yT", 2 * L, b)])
                for i in range(NT):
                    n = min(CP, NI - CP * i)
                    ps = claim(("h", b, i), "dve")
                    done(pe.matmul(ps[0:n, 0:C], yT_v[:, NI * b + CP * i:NI * b + CP * i + n], headw[:, :],
                                   start=True, stop=True), "dve")
            
            def turn96(n):
                for b in range(B):
                    pe.wait_ge(ln_y, B * n + b + 1)
                    for c in range(CK):
                        ps = claim(("yT", n, b, c), "act")
                        for i in range(NT):
                            mm = pe.transpose(ps[0:CP, CP * i:CP * i + CP],
                                              y96[:, NT * b + i, CP * c:CP * c + CP], ident[0:CP, 0:CP])
                        done(mm, "act")

            def qkv96(n, w):
                for b in range(B):
                    pe.wait_ge(act_evac, free_at[("yT", n, b, CK - 1)])
                    for j, reader in ((0, "act"), (1, "dve")):
                        for o in range(CK):
                            ps = claim(("qk", n, b, j, o), reader)
                            for k in range(CK):
                                mm = pe.matmul(ps[0:CP, 0:N], w[:, k, C * j + CP * o:C * j + CP * o + CP],
                                               yT96[:, k, N * b:N * b + N], start=(k == 0), stop=(k == CK - 1))
                            done(mm, reader)
                    for i in range(NT):
                        t = NT * b + i
                        ps = claim(("v", n, t), "dve")
                        for k in range(CK):
                            mm = pe.matmul(ps[0:CP, 0:C], yT96[:, k, CP * t:CP * t + CP],
                                           w[:, k, 2 * C:3 * C], start=(k == 0), stop=(k == CK - 1))
                        done(mm, "dve")

            def project(b, oT, w, r):
                for i in range(NT):
                    ps = claim(("proj", r, b, i), "dve")
                    pe.matmul(ps[0:CP, 0:C], ones[0:1, 0:CP], row[0:1, r:r + C], start=True, stop=False)
                    for g in range(HG):
                        mm = pe.matmul(ps[0:CP, 0:C], oT[:, g, CP * i:CP * i + CP], w[:, g, :],
                                       start=False, stop=(g == HG - 1))
                    done(mm, "dve")

            def free_banks():
                for i in range(8):
                    if holder[i]:
                        pe.wait_ge(evac[holder[i][0]], holder[i][1])
                        holder[i] = None

            pe.wait_ge(fused_consts, 1)
            turn96(5)
            pe.wait_ge(ld_fused, LD_FUSED)
            qkv96(5, wqkv96[0])
            free_banks()
            for b in range(B):
                with pe.Fori(0, JT // 4) as it:
                    def scores(u):
                        pe.wait_ge(tk_q, it * 4 + (JT * b + u + 1))
                        for k in range(CK):
                            r = CP + k
                            mm = pe.matmul(bank[u][0:MR, 0:N], qg[u][0:r, k, :], kT[0:r, k, N * b:N * b + N],
                                           start=(k == 0), stop=(k == CK - 1))
                        mm.then_inc(tk_s, 1)

                    def mix(u):
                        pe.wait_ge(tk_w, it * 4 + (JT * b + u + 1))
                        for c in range(NT):
                            mm = pe.matmul(bank[4 + u][0:CP, MR * c:MR * c + MR], pt[u][:, CP * c:CP * c + CP],
                                           wms[u][:, :], start=True, stop=True)
                        mm.then_inc(tk_mix, 1)

                    scores(0)
                    scores(1)
                    scores(2)
                    mix(0)
                    scores(3)
                    mix(1)
                    mix(2)
                    mix(3)
                pe.wait_ge(tk_at, JT * (b + 1))
                for g in range(HG):
                    ps = claim(("u", b, g), "act")
                    for c in range(NT):
                        for j in range(4):
                            mm = pe.matmul(ps[HP * j:HP * j + HP, 0:N], vpad[0:CP, NT * b + c, 4 * g + j, :],
                                           AT[:, c, 4 * g + j, :], start=(c == 0), stop=(c == NT - 1))
                    done(mm, "act")
                for i in range(NT):
                    pe.wait_ge(z_ready, b + 1)
                    ps = claim(("z", b, i), "act")
                    for g in range(HG):
                        mm = pe.transpose(ps[0:CP, 128 * g:128 * g + 128], zT[:, g, CP * i:CP * i + CP],
                                          ident[:, :])
                    done(mm, "act")
                for g in range(HG):
                    pe.wait_ge(act_evac, free_at[("z", b, NT - 1)])
                    ps = claim(("w", b, g), "dve")
                    for c in range(NT):
                        for j in range(4):
                            mm = pe.matmul(ps[HP * j:HP * j + HP, 0:N], znat[:, c, 4 * g + j, :],
                                           AT[:, c, 4 * g + j, :], start=(c == 0), stop=(c == NT - 1))
                    done(mm, "dve")
                pe.wait_ge(dve_evac, free_at[("w", b, HG - 1)])
                project(b, oT, wproj[0], R_P0)
                free_banks()

            turn96(7)
            qkv96(7, wqkv96[1])
            free_banks()

            def flip(k, j):
                pe.wait_ge(mh_p, k * 4 + (j + 1))
                for c in range(NT):
                    if j:
                        pe.wait_ge(mh_pt, k * 12 + (NT * j + c - 2))
                    for i in range(NT):
                        mm = pe.transpose(bank[(4, 5, 7)[c]][0:CP, CP * i:CP * i + CP],
                                          P4[j][:, i, CP * c:CP * c + CP], ident[0:CP, 0:CP])
                    mm.then_inc(mh_t, 1)

            for G in range(HG):
                with pe.Fori(0, B) as b:
                    k = b + B * G
                    for j in range(4):
                        o = (4 * G + j) // (H // CK)
                        pe.wait_ge(mh_q, k * 4 + (j + 1))
                        for i in range(NT):
                            s = NT * j + i
                            if s >= 4:
                                pe.wait_ge(mh_exp, k * 12 + (s - 3))
                            pe.matmul(bank[s % 4][0:CP, 0:N], qh4[j][:, CP * i:CP * i + CP],
                                      kT[0:CP, o, bass.ds(b * N, N)], start=True, stop=True).then_inc(mh_s, 1)
                        if j:
                            flip(k, j - 1)
                    flip(k, 3)
                    pe.wait_ge(mh_v, k + 1)
                    pe.wait_ge(mh_pt, k * 12 + 12)
                    for c in range(NT):
                        for j in range(4):
                            mm = pe.matmul(bank[6][HP * j:HP * j + HP, 0:N], vh4[j][:, c, :], P4[4 + j][:, c, :],
                                           start=(c == 0), stop=(c == NT - 1))
                    mm.then_inc(mh_o, 1)
            pe.wait_ge(mh_oT, B * HG)
            for b in range(B):
                project(b, oT4[:, b, :, :], wproj[1], R_P1)

            def mixture(s, n):
                for b in range(B):
                    pe.wait_ge(act_evac, free_at[("yT", n, b, CK - 1)])
                    ps = claim(("gate", s, b), "dve")
                    for i in range(NT):
                        t = NT * b + i
                        for k in range(CK):
                            mm = pe.matmul(ps[0:CP, EX * i:EX * i + EX], yT96[:, k, CP * t:CP * t + CP],
                                           gate_w[s][:, k, :], start=(k == 0), stop=(k == CK - 1))
                    done(mm, "dve")
                pe.wait_ge(cw_ready, s + 1)
                for b in range(B):
                    ps = claim(("cwT", s, b), "act")
                    for i in range(NT):
                        mm = pe.transpose(ps[0:EX, CP * i:CP * i + CP], cw[:, NT * b + i, :], ident[0:CP, 0:CP])
                    done(mm, "act")
                free_banks()
                for t in range(TT):
                    if t >= 4:
                        pe.wait_ge(ex_add[s], t - 3)
                    pe.matmul(bank[4 + t % 4][0:CP, 0:C], cwT[:, CP * t:CP * t + CP], b2[s][:, :],
                              start=True, stop=True).then_inc(ex_y[s], 1)
                with pe.Fori(0, EX // 2) as it:
                    def hidden(k):
                        p, g = divmod(k, NG)
                        if g == 0:
                            pe.wait_ge(ld_exp[p], it * 32 + (32 * (EX // 2) * s + 32))
                        for f in range(FC):
                            m = FC * k + f
                            if m >= 4:
                                pe.wait_ge(ex_act[s], it * (2 * NG * FC) + (m - 3))
                            for c in range(CK):
                                mm = pe.matmul(bank[m % 4][:, 0:TG], ew1[p][:, c, 128 * f:128 * f + 128],
                                               yT96[:, c, TG * g:TG * g + TG], start=(c == 0), stop=(c == CK - 1))
                            mm.then_inc(ex_hid[s], 1)

                    def output(k):
                        p = k // NG
                        pe.wait_ge(ex_act[s], it * (2 * NG * FC) + FC * (k + 1))
                        for i in range(GT):
                            pe.wait_ge(ex_add[s], it * (2 * TT) + (TT + GT * k + i - 3))
                            for f in range(FC):
                                mm = pe.matmul(bank[4 + i][0:CP, 0:C], hid2[k % 2][:, f, CP * i:CP * i + CP],
                                               ew2[p][:, f, :], start=(f == 0), stop=(f == FC - 1))
                            mm.then_inc(ex_y[s], 1)

                    hidden(0)
                    for k in range(1, 2 * NG):
                        hidden(k)
                        output(k - 1)
                    output(2 * NG - 1)

            turn96(8)
            mixture(0, 8)
            pe.wait_ge(ex_add[0], TT * (EX + 1))
            pe.wait_ge(bn_stat, 1)
            ps = claim(("moments",), "dve")
            done(pe.matmul(ps[0:CP, 0:2 * B], ones[0:CP, 0:CP], ms[:, :], start=True, stop=True), "dve")
            turn96(10)
            qkv96(10, wqkv96[2])
            for b in range(B):
                pe.wait_ge(act_evac, free_at[("qk", 10, b, 0, CK - 1)])
                pe.wait_ge(dve_evac, free_at[("v", 10, NT * b + NT - 1)])
                for i in range(NT):
                    t = NT * b + i
                    ps = claim(("s", t), "dve", "act")
                    for k in range(CK):
                        mm = pe.matmul(ps[0:CP, 0:N], qT[0:CP, k, CP * t:CP * t + CP],
                                       kT[0:CP, k, N * b:N * b + N], start=(k == 0), stop=(k == CK - 1))
                    done(mm, "dve")
            for b in range(B):
                pe.wait_ge(act_evac, free_at[("s", NT * b + NT - 1)])
                for c in range(NT):
                    ps = claim(("pT", b, c), "act")
                    for i in range(NT):
                        mm = pe.transpose(ps[0:CP, CP * i:CP * i + CP], P1[:, NT * b + i, CP * c:CP * c + CP],
                                          ident[0:CP, 0:CP])
                    done(mm, "act")
            for b in range(B):
                pe.wait_ge(act_evac, free_at[("pT", b, NT - 1)])
                for i in range(NT):
                    ps = claim(("a", NT * b + i), "dve")
                    for c in range(NT):
                        mm = pe.matmul(ps[0:CP, 0:C], PT1[:, NT * b + c, CP * i:CP * i + CP], v1[:, NT * b + c, :],
                                       start=(c == 0), stop=(c == NT - 1))
                    done(mm, "dve")
            turn96(11)
            mixture(1, 11)

        @block.scalar
        def _(act):
            def take(key):
                act.wait_ge(mm_act, ready_at[key])
                return bank[lies_in[key]]

            act.wait_ge(ld_row, 32)
            for i in range(2):
                ps = take(("conv", i))
                act.activation(xT[:, 512 * i:512 * i + 512], ps[:, :], ACT.Identity,
                               bias=vec[:, V_CONV:V_CONV + 1]).then_inc(act_evac, 1)

            def gain_shift(n, g, s):
                for b in range(B):
                    ps = take(("yT", n, b))
                    act.activation(yT_v[:, NI * b:NI * b + NI], ps[:, 0:NI], ACT.Identity,
                                   scale=vec[:, g:g + 1], bias=vec[:, s:s + 1]).then_inc(act_evac, 1)

            for l in range(L):
                gain_shift(2 * l, V_G1 + l, V_B1 + l)
                for b in range(B):
                    for p in range(2):
                        act.wait_ge(kmax_ready, 2 * (B * l + b) + p + 1)
                        ps = bank[lies_in[("k", l, b, p)]]
                        for i in range(2):
                            c = 2 * p + i
                            s = NC4 * b + c
                            ins = act.activation(expkT[:, c, NI * b:NI * b + NI], ps[:, NI * i:NI * i + NI],
                                                 ACT.Exp, bias=nkmax[:, s:s + 1], accum_out=ksum[:, s:s + 1])
                        ins.then_inc(act_evac, 1)
                for t in range(VT):
                    act.wait_ge(dve_evac, free_at[("q", l, t)])
                    act.activation(q_v[:, t, :], q_v[:, t, :], ACT.Exp).then_inc(q_exp, 1)
                    ps = take(("v", l, t))
                    act.activation(v_v[:, t, :], ps[:, :], ACT.Copy).then_inc(act_evac, 1)
                for t in range(VT):
                    ps = take(("kt", l, t))
                    act.activation(expk[:, t, :], ps[:, :], ACT.Copy).then_inc(act_evac, 1)
                for t in range(VT):
                    ps = take(("qT", l, t))
                    act.activation(qT_v[:, :, 128 * t:128 * t + 128],
                                   ps[:, :].rearrange("p (c t) -> p c t", c=NC4), ACT.Copy).then_inc(act_evac, 1)
                gain_shift(2 * l + 1, V_G2 + l, V_B2 + l)
                for b in range(B):
                    for p in range(2):
                        ps = take(("f1", l, b, p))
                        for i in range(2):
                            c = 2 * p + i
                            ins = act.activation(hid_v[:, c, NI * b:NI * b + NI], ps[:, NI * i:NI * i + NI],
                                                 ACT.Gelu, bias=vec[:, V_F1 + NC4 * l + c:V_F1 + NC4 * l + c + 1])
                        ins.then_inc(act_evac, 1)
            gain_shift(2 * L, V_GF, V_BF)
            
            def evac96(n, g=None, s=None):
                for b in range(B):
                    for c in range(CK):
                        ps = take(("yT", n, b, c))
                        if g is None:
                            ins = act.activation(yT96[:, c, N * b:N * b + N], ps[0:CP, 0:N], ACT.Copy)
                        else:
                            ins = act.activation(yT96[:, c, N * b:N * b + N], ps[0:CP, 0:N], ACT.Identity,
                                                 scale=vec96[:, g, c:c + 1], bias=vec96[:, s, c:c + 1])
                        ins.then_inc(act_evac, 1)

            def queries(n, scale):
                for b in range(B):
                    for o in range(CK):
                        ps = take(("qk", n, b, 0, o))
                        act.activation(qT[0:CP, o, N * b:N * b + N], ps[0:CP, 0:N], ACT.Copy, scale=scale)\
                            .then_inc(act_evac, 1)

            evac96(5)
            queries(5, HD ** -0.5)
            for b in range(B):
                with act.Fori(0, JT // 4) as it:
                    def softmax(u):
                        act.wait_ge(tk_max, it * 4 + (JT * b + u + 1))
                        act.activation(pt[u][0:MR, :], bank[u][0:MR, 0:N], ACT.Exp, bias=nm[u][0:MR, :],
                                       accum_out=sums[u][0:MR, :]).then_inc(tk_exp, 1)

                    def keep(u):
                        act.wait_ge(tk_mix, it * 4 + (JT * b + u + 1))
                        act.activation(AT[:, :, :, bass.ds(it * (4 * RT) + RT * u, RT)],
                                       bank[4 + u][0:CP, 0:NT * MR]
                                       .rearrange("p (c h n) -> p c h n", c=NT, h=H), ACT.Copy).then_inc(tk_at, 1)

                    softmax(0)
                    softmax(1)
                    softmax(2)
                    keep(0)
                    softmax(3)
                    keep(1)
                    keep(2)
                    keep(3)
                for g in range(HG):
                    ps = take(("u", b, g))
                    act.activation(uT[:, g, :], ps[:, 0:N], ACT.Copy).then_inc(act_evac, 1)
                for i in range(NT):
                    ps = take(("z", b, i))
                    act.activation(znat[:, i, :, :], ps[0:CP, 0:H * HP].rearrange("p (h d) -> p h d", h=H),
                                   ACT.Copy).then_inc(act_evac, 1)
            evac96(7, 0, 1)
            queries(7, HD ** -0.5)
            for G in range(HG):
                with act.Fori(0, B) as b:
                    k = b + B * G

                    def keep_flipped(j):
                        for c in range(NT):
                            act.wait_ge(mh_t, k * 12 + (NT * j + c + 1))
                            act.activation(P4[4 + j][:, c, :], bank[(4, 5, 7)[c]][0:CP, 0:N], ACT.Copy)\
                                .then_inc(mh_pt, 1)

                    for j in range(4):
                        for i in range(NT):
                            s = NT * j + i
                            act.wait_ge(mh_max, k * 12 + (s + 1))
                            act.activation(P4[j][:, i, :], bank[s % 4][0:CP, 0:N], ACT.Exp,
                                           bias=nmh[:, j, i:i + 1], accum_out=sumh[:, j, i:i + 1])\
                                .then_inc(mh_exp, 1)
                        if j:
                            keep_flipped(j - 1)
                    keep_flipped(3)

            def mixture(s, func):
                for b in range(B):
                    ps = take(("cwT", s, b))
                    act.activation(cwT[:, N * b:N * b + N], ps[0:EX, 0:N], ACT.Copy).then_inc(act_evac, 1)
                with act.Fori(0, EX // 2) as it:
                    for k in range(2 * NG):
                        for f in range(FC):
                            m = FC * k + f
                            act.wait_ge(ex_hid[s], it * (2 * NG * FC) + (m + 1))
                            act.activation(hid2[k % 2][:, f, :], bank[m % 4][:, 0:TG], func,
                                           bias=eb1[k // NG][:, f:f + 1]).then_inc(ex_act[s], 1)

            evac96(8, 2, 3)
            act.wait_ge(gate_e, 1)
            act.activation(s12[:, :], s12[:, :], ACT.Exp).then_inc(gate_x, 1)
            mixture(0, ACT.Gelu)
            evac96(10)
            queries(10, 1.0)
            for t in range(TT):
                act.wait_ge(sa_max, t + 1)
                ps = bank[lies_in[("s", t)]]
                act.activation(P1[:, t, :], ps[0:CP, 0:N], ACT.Exp, bias=nm1[:, t:t + 1],
                               accum_out=sum1[:, t:t + 1]).then_inc(act_evac, 1)
            for b in range(B):
                for c in range(NT):
                    ps = take(("pT", b, c))
                    act.activation(PT1[:, NT * b + c, :], ps[0:CP, 0:N], ACT.Copy).then_inc(act_evac, 1)
            evac96(11)
            act.wait_ge(gate_e, 2)
            act.activation(lg[:, :, :], lg[:, :, :], ACT.Exp).then_inc(gate_x, 1)
            mixture(1, ACT.Silu)

        @block.vector
        def _(dve):
            steps = [0]

            def take(key):
                dve.wait_ge(mm_dve, ready_at[key])
                return bank[lies_in[key]]

            def link(ins):
                steps[0] += 1
                ins.then_inc(dve_step, 1)
                dve.wait_ge(dve_step, steps[0])

            def ln_stats(src, tiles, rows):
                for t in tiles:
                    ins = dve.bn_stats(st[0:rows, t, :], src[:, t, :])
                link(ins)
                for t in tiles:
                    ins = dve.bn_aggr(mv[0:rows, t, :], st[0:rows, t, :])
                link(ins)
                t0, t1 = tiles[0], tiles[-1] + 1
                dve.tensor_scalar(ve[0:rows, t0:t1], mv[0:rows, t0:t1, 1], EPS, None, ALU.add).then_inc(ln_var, 1)

            def ln_apply(n, g, src, dst, tiles, rows):
                dve.wait_ge(ln_rstd, B * POWER[n] + g + 1)
                for t in tiles:
                    ins = dve.tensor_scalar(dst[:, t, :], src[:, t, :], mv[0:rows, t, 0:1], rstd[0:rows, t:t + 1],
                                            ALU.subtract, ALU.mult)
                ins.then_inc(ln_y, 1)

            def pair(b):
                return range(2 * b, 2 * b + 2)

            def add_to_x(key, b, r):
                ps = take(key)
                xs = x[:, 2 * b:2 * b + 2, :]
                dve.tensor_tensor(xs, xs, ps[:, 0:NI].rearrange("p (t d) -> p t d", t=2), ALU.add)\
                    .then_inc(dve_evac, 1)
                dve.wait_ge(dve_evac, free_at[key])
                for t in pair(b):
                    ins = dve.tensor_tensor(x[:, t, :], x[:, t, :], row[:, r:r + D], ALU.add)
                link(ins)
                ln_stats(x, pair(b), 128)

            for b in range(B):
                ps = take(("x", b))
                dve.tensor_copy(x[:, 2 * b:2 * b + 2, :], ps[:, 0:NI].rearrange("p (t d) -> p t d", t=2))\
                    .then_inc(dve_evac, 1)
                dve.wait_ge(dve_evac, free_at[("x", b)])
                ln_stats(x, pair(b), 128)
            for l in range(L):
                for b in range(B):
                    ln_apply(2 * l, b, x, y_v, pair(b), 128)
                for b in range(B):
                    for p in range(2):
                        ps = take(("k", l, b, p))
                        s = NC4 * b + 2 * p
                        dve.tensor_reduce(nkmax[:, s:s + 2], ps[:, :].rearrange("p (c t) -> p c t", c=2), AX.X,
                                          ALU.max, negate=True).then_inc(kmax_ready, 1)

                def finish_q(t):
                    dve.wait_ge(q_exp, VT * l + t + 1)
                    qh = q_v[:, t, :].rearrange("p (h d) -> p h d", h=NH)
                    link(dve.tensor_reduce(qsum[:, t, :], qh, AX.X, ALU.add))
                    link(dve.reciprocal(qrec[:, t, :], qsum[:, t, :]))
                    dve.tensor_tensor(qh, qh, qrec[:, t, :].unsqueeze(2).to_broadcast([128, NH, DH]),
                                      ALU.mult).then_inc(q_norm, 1)

                for t in range(VT):
                    ps = take(("q", l, t))
                    pq = ps[:, :].rearrange("p (h d) -> p h d", h=NH)
                    link(dve.tensor_reduce(qmax[:, t, :], pq, AX.X, ALU.max))
                    dve.tensor_tensor(q_v[:, t, :].rearrange("p (h d) -> p h d", h=NH), pq,
                                      qmax[:, t, :].unsqueeze(2).to_broadcast([128, NH, DH]),
                                      ALU.subtract).then_inc(dve_evac, 1)
                    if t >= 2:
                        finish_q(t - 2)
                finish_q(VT - 2)
                finish_q(VT - 1)
                dve.wait_ge(act_evac, free_at[("k", l, B - 1, 1)])
                link(dve.reciprocal(krec[:, :], ksum[:, :]))
                if l == 0:
                    dve.wait_ge(ctx_zeroed, 1)
                for b in range(B):
                    ps = take(("ctx", l, b))
                    pc = ps[:, :].rearrange("p (c d) -> p c d", c=NC4)
                    dve.tensor_copy(ctxT[0:64, b, :, 0:64], pc[0:64, :, 0:64])
                    dve.tensor_copy(ctxT[64:128, b, :, 64:128], pc[64:128, :, 64:128]).then_inc(dve_evac, 1)
                for b in range(B):
                    ps = take(("g", l, b))
                    dve.scalar_tensor_tensor(
                        out=gmat[:, b, :, :], in0=ps[:, :].rearrange("p (c d) -> p c d", c=NC4),
                        scalar=DH ** -0.5,
                        in1=krec[:, NC4 * b:NC4 * b + NC4].unsqueeze(2).to_broadcast([128, NC4, D]),
                        op0=ALU.mult, op1=ALU.mult).then_inc(dve_evac, 1)
                for b in range(B):
                    add_to_x(("o", l, b), b, R_OUT + D * l)
                for b in range(B):
                    ln_apply(2 * l + 1, b, x, y_v, pair(b), 128)
                for b in range(B):
                    add_to_x(("f2", l, b), b, R_FF2 + D * l)
            for b in range(B):
                ln_apply(2 * L, b, x, y_v, pair(b), 128)
            for b in range(B):
                for i in range(NT):
                    n = min(CP, NI - CP * i)
                    ps = take(("h", b, i))
                    dve.tensor_tensor(h[0:n, NT * b + i, :], ps[0:n, 0:C], row[0:n, R_HEAD:R_HEAD + C],
                                      ALU.add).then_inc(dve_evac, 1)
            
            def three(b):
                return range(NT * b, NT * b + NT)

            def normalise(n, src, dst):
                for b in range(B):
                    ln_stats(src, three(b), CP)
                for b in range(B):
                    ln_apply(n, b, src, dst, three(b), CP)

            def keys_values(n, vdst):
                for b in range(B):
                    for o in range(CK):
                        ps = take(("qk", n, b, 1, o))
                        dve.tensor_copy(kT[0:CP, o, N * b:N * b + N], ps[0:CP, 0:N]).then_inc(dve_evac, 1)
                    for t in three(b):
                        ps = take(("v", n, t))
                        dve.tensor_copy(vdst(t), ps[0:CP, 0:C].rearrange("p (h d) -> p h d", h=H))\
                            .then_inc(dve_evac, 1)

            def head_values(t):
                return vpad[0:CP, t, :, 0:HD]

            def add_projection(dst, b, r):
                for i in range(NT):
                    ps = take(("proj", r, b, i))
                    t = NT * b + i
                    dve.tensor_tensor(dst[:, t, :], dst[:, t, :], ps[0:CP, 0:C], ALU.add).then_inc(dve_evac, 1)

            dve.wait_ge(ld_head, 16 * (1 + B))
            dve.wait_ge(dve_evac, free_at[("h", B - 1, NT - 1)])
            normalise(5, h, y96)
            dve.wait_ge(ld_fused, LD_FUSED)
            dve.wait_ge(fused_consts, 1)
            dve.tensor_tensor(wmix[:, :], wmix[:, :], wdelta[:, :], ALU.mult).then_inc(wmix_ready, 1)
            dve.tensor_scalar(lam_a[:, :], lam[:, :], -2.0, 1.0, ALU.mult, ALU.add).then_inc(wmix_ready, 1)
            dve.tensor_scalar(lam_b[:, :], lam[:, :], 3.0, None, ALU.mult).then_inc(wmix_ready, 1)
            dve.wait_ge(wmix_ready, 3)
            keys_values(5, head_values)
            for b in range(B):
                with dve.Fori(0, JT // 4) as it:
                    def row_max(u):
                        dve.wait_ge(tk_s, it * 4 + (JT * b + u + 1))
                        dve.tensor_reduce(nm[u][0:MR, :], bank[u][0:MR, 0:N], AX.X, ALU.max, negate=True)\
                            .then_inc(tk_max, 1)

                    def divide(u):
                        dve.wait_ge(tk_exp, it * 4 + (JT * b + u + 1))
                        dve.reciprocal(rs[u][0:MR, :], sums[u][0:MR, :]).then_inc(tk_r, 1)
                        dve.wait_ge(tk_r, it * 4 + (JT * b + u + 1))
                        dve.tensor_scalar(wms[u][:, :], wmix[:, :], rs[u][:, 0:1], None, ALU.mult)\
                            .then_inc(tk_w, 1)

                    row_max(0)
                    row_max(1)
                    divide(0)
                    row_max(2)
                    divide(1)
                    row_max(3)
                    divide(2)
                    divide(3)
                dve.wait_ge(act_evac, free_at[("u", b, HG - 1)])
                for g in range(HG):
                    ins = dve.tensor_scalar(zT[:, g, :], uT[:, g, :], lam_b[:, g:g + 1], None, ALU.mult)
                ins.then_inc(z_ready, 1)
                for g in range(HG):
                    ps = take(("w", b, g))
                    dve.scalar_tensor_tensor(out=oT[:, g, :], in0=uT[:, g, :], scalar=lam_a[:, g:g + 1],
                                             in1=ps[:, 0:N], op0=ALU.mult, op1=ALU.add).then_inc(dve_evac, 1)
                add_projection(h, b, R_P0)
            dve.wait_ge(dve_evac, free_at[("proj", R_P0, B - 1, NT - 1)])
            normalise(6, h, z)
            dve.wait_ge(ln_y, B * 7)
            normalise(7, z, y96)
            keys_values(7, head_values)
            for G in range(HG):
                with dve.Fori(0, B) as b:
                    k = b + B * G

                    def divide_head(j):
                        dve.wait_ge(mh_exp, k * 12 + NT * (j + 1))
                        dve.reciprocal(rsh[:, j, :], sumh[:, j, :]).then_inc(mh_r, 1)
                        dve.wait_ge(mh_r, k * 4 + (j + 1))
                        for i in range(NT):
                            ins = dve.tensor_scalar(P4[j][:, i, :], P4[j][:, i, :], rsh[:, j, i:i + 1], None,
                                                    ALU.mult)
                        ins.then_inc(mh_p, 1)

                    for j in range(4):
                        for i in range(NT):
                            s = NT * j + i
                            dve.wait_ge(mh_s, k * 12 + (s + 1))
                            dve.tensor_reduce(nmh[:, j, i:i + 1], bank[s % 4][0:CP, 0:N], AX.X, ALU.max,
                                              negate=True).then_inc(mh_max, 1)
                        if j:
                            divide_head(j - 1)
                    divide_head(3)
                    dve.wait_ge(mh_o, k + 1)
                    dve.tensor_copy(oT4[:, bass.ds(b, 1), G, :], bank[6][:, 0:N].unsqueeze(1)).then_inc(mh_oT, 1)
            for b in range(B):
                add_projection(z, b, R_P1)
            dve.wait_ge(dve_evac, free_at[("proj", R_P1, B - 1, NT - 1)])
            normalise(8, z, y96)

            def bcast(v):
                return v.unsqueeze(2).to_broadcast([CP, TT, EX])

            def experts_of_tokens():
                for t in range(TT):
                    ins = dve.max(top[:, t, :], lg[:, t, :])
                link(ins)
                for t in range(TT):
                    ins = dve.max_index(topi[:, t, :], top[:, t, :], lg[:, t, :])
                link(ins)

            def one_hot(dst, i):
                link(dve.tensor_tensor(dst[:, :, :], iota8[:, :].unsqueeze(1).to_broadcast([CP, TT, EX]),
                                       bcast(topi[:, :, i]), ALU.is_equal))

            def add_experts(s):
                for t in range(TT):
                    dve.wait_ge(ex_y[s], t + 1)
                    dve.tensor_tensor(h[:, t, :], h[:, t, :], bank[4 + t % 4][0:CP, 0:C], ALU.add)\
                        .then_inc(ex_add[s], 1)
                with dve.Fori(0, EX // 2) as it:
                    for k in range(2 * NG):
                        p, g = divmod(k, NG)
                        for i in range(GT):
                            t = GT * g + i
                            dve.wait_ge(ex_y[s], it * (2 * TT) + (TT + GT * k + i + 1))
                            dve.scalar_tensor_tensor(out=h[:, t, :], in0=bank[4 + i][0:CP, 0:C],
                                                     scalar=cw[:, t, bass.ds(it * 2 + p, 1)], in1=h[:, t, :],
                                                     op0=ALU.mult, op1=ALU.add).then_inc(ex_add[s], 1)

            for b in range(B):
                ps = take(("gate", 0, b))
                dve.tensor_tensor(lg[:, NT * b:NT * b + NT, :],
                                  ps[0:CP, 0:NT * EX].rearrange("p (t e) -> p t e", t=NT),
                                  row[0:CP, R_GB:R_GB + EX].unsqueeze(1).to_broadcast([CP, NT, EX]),
                                  ALU.add).then_inc(dve_evac, 1)
            dve.wait_ge(dve_evac, free_at[("gate", 0, B - 1)])
            experts_of_tokens()
            dve.tensor_tensor(s12[:, :], top[:, :, 1], top[:, :, 0], ALU.subtract).then_inc(gate_e, 1)
            dve.tensor_tensor(h[:, :, :], h[:, :, :], z[:, :, :], ALU.add)
            one_hot(oh, 1)
            one_hot(cw, 0)
            dve.wait_ge(gate_x, 1)
            link(dve.tensor_scalar(s12b[:, :], s12[:, :], 1.0, None, ALU.add))
            link(dve.reciprocal(s12b[:, :], s12b[:, :]))
            link(dve.tensor_tensor(s12[:, :], s12[:, :], s12b[:, :], ALU.mult))
            link(dve.tensor_tensor(cw[:, :, :], cw[:, :, :], bcast(s12b[:, :]), ALU.mult))
            link(dve.tensor_tensor(oh[:, :, :], oh[:, :, :], bcast(s12[:, :]), ALU.mult))
            dve.tensor_tensor(cw[:, :, :], cw[:, :, :], oh[:, :, :], ALU.add).then_inc(cw_ready, 1)
            dve.wait_ge(cw_ready, 1)
            add_experts(0)
            dve.wait_ge(ex_add[0], TT * (EX + 1))
            normalise(9, h, z)
            dve.wait_ge(ln_y, B * 10)
            for t in range(TT):
                ins = dve.bn_stats(st[0:CP, t, :], z[:, t, :])
            link(ins)
            for b in range(B):
                ins = dve.bn_aggr(bstat[:, b, :], st[0:CP, NT * b:NT * b + NT, :])
            link(ins)
            dve.tensor_copy(ms[:, 0:B], bstat[:, :, 0])
            link(dve.tensor_tensor(ms[:, B:2 * B], bstat[:, :, 0], bstat[:, :, 0], ALU.mult))
            dve.tensor_tensor(ms[:, B:2 * B], ms[:, B:2 * B], bstat[:, :, 1], ALU.add).then_inc(bn_stat, 1)
            ps = take(("moments",))
            dve.tensor_scalar(msm[:, :], ps[0:CP, 0:2 * B], 1.0 / CP, None, ALU.mult).then_inc(dve_evac, 1)
            dve.wait_ge(dve_evac, free_at[("moments",)])
            link(dve.tensor_tensor(bve[:, :], msm[:, 0:B], msm[:, 0:B], ALU.mult))
            link(dve.tensor_tensor(bve[:, :], msm[:, B:2 * B], bve[:, :], ALU.subtract))
            dve.tensor_scalar(bve[:, :], bve[:, :], EPS, None, ALU.add).then_inc(bn_var, 1)
            dve.wait_ge(bn_rstd, 1)
            for b in range(B):
                dve.tensor_scalar(y96[:, NT * b:NT * b + NT, :], z[:, NT * b:NT * b + NT, :], msm[:, b:b + 1],
                                  brs[:, b:b + 1], ALU.subtract, ALU.mult).then_inc(ln_y, 1)
            keys_values(10, lambda t: v1[:, t, :].rearrange("p (h d) -> p h d", h=H))
            for t in range(TT):
                ps = take(("s", t))
                dve.tensor_reduce(nm1[:, t:t + 1], ps[0:CP, 0:N], AX.X, ALU.max, negate=True).then_inc(sa_max, 1)
            dve.wait_ge(act_evac, free_at[("s", TT - 1)])
            link(dve.reciprocal(rec1[:, :], sum1[:, :]))
            for t in range(TT):
                ps = take(("a", t))
                dve.scalar_tensor_tensor(out=h[:, t, :], in0=ps[0:CP, 0:C], scalar=rec1[:, t:t + 1],
                                         in1=h[:, t, :], op0=ALU.mult, op1=ALU.add).then_inc(dve_evac, 1)
            dve.wait_ge(dve_evac, free_at[("a", TT - 1)])
            normalise(11, h, y96)
            for b in range(B):
                ps = take(("gate", 1, b))
                dve.tensor_copy(lg[:, NT * b:NT * b + NT, :],
                                ps[0:CP, 0:NT * EX].rearrange("p (t e) -> p t e", t=NT)).then_inc(dve_evac, 1)
            dve.wait_ge(dve_evac, free_at[("gate", 1, B - 1)])
            experts_of_tokens()
            one_hot(cw, 0)
            dve.tensor_tensor(lg[:, :, :], lg[:, :, :], bcast(top[:, :, 0]), ALU.subtract).then_inc(gate_e, 1)
            dve.wait_ge(gate_x, 2)
            link(dve.tensor_reduce(s12[:, :], lg[:, :, :], AX.X, ALU.add))
            link(dve.reciprocal(s12b[:, :], s12[:, :]))
            dve.tensor_tensor(cw[:, :, :], cw[:, :, :], bcast(s12b[:, :]), ALU.mult).then_inc(cw_ready, 1)
            dve.wait_ge(cw_ready, 2)
            add_experts(1)

        @block.gpsimd
        def _(pool):
            pool.memset(ident[:, :], 0.0).then_inc(pool_step, 1)
            pool.memset(mhalf[:, :], -0.5)
            pool.wait_ge(pool_step, 1)
            pool.affine_select(out=ident[:, :], in_=ident[:, :], compare_op=ALU.not_equal, fill=1.0, base=0,
                               pattern=[[-1, 128]], channel_multiplier=1).then_inc(consts_ready, 1)
            pool.wait_ge(consts_ready, 1)

            def power(n, tiles, rows):
                pool.wait_ge(ln_var, n + 1)
                t0, t1 = tiles[0], tiles[-1] + 1
                pool.tensor_tensor(rstd[0:rows, t0:t1], ve[0:rows, t0:t1], mhalf[0:rows, t0:t1], ALU.pow)\
                    .then_inc(ln_rstd, 1)

            for n in range(2 * L + 1):
                if n == 1:
                    pool.memset(ctxT, 0.0).then_inc(ctx_zeroed, 1)
                for b in range(B):
                    power(B * n + b, range(2 * b, 2 * b + 2), 128)
            
            pool.wait_ge(act_evac, free_at[("yT", 2 * L, B - 1)])
            pool.memset(vpad[0:CP, :, :, HD:HP], 0.0).then_inc(pool_step, 1)
            pool.wait_ge(pool_step, 2)
            pool.memset(kT[CP:CP + 1, 1, :], 1.0).then_inc(pool_step, 1)
            pool.wait_ge(pool_step, 3)
            pool.memset(ones[:, :], 1.0)
            for i in range(4):
                pool.memset(pt[i][:, :], 1.0)
                pool.memset(rs[i][:, :], 1.0)
            pool.iota(iota8[:, :], [[1, EX]], base=0, channel_multiplier=0, allow_small_or_imprecise_dtypes=True)\
                .then_inc(fused_consts, 1)
            for b in range(B):
                power(B * 5 + b, range(NT * b, NT * b + NT), CP)

            pool.wait_ge(act_evac, free_at[("qk", 5, B - 1, 0, CK - 1)])
            pool.wait_ge(ld_fused, LD_FUSED)

            def mixed_queries(u, n0):
                pool.tensor_tensor(
                    qg[u][0:CP, :, :].rearrange("p k (h n) -> p k h n", h=H),
                    qT[0:CP, :, bass.ds(n0, RT)].unsqueeze(2).to_broadcast([CP, CK, H, RT]),
                    wlT[:, :, :].unsqueeze(3).to_broadcast([CP, CK, H, RT]), ALU.mult).then_inc(tk_q, 1)

            for u in range(4):
                mixed_queries(u, RT * u)
            with pool.Fori(1, B * JT // 4) as it:
                for u in range(4):
                    pool.wait_ge(tk_s, it * 4 + (u - 3))
                    mixed_queries(u, it * (4 * RT) + RT * u)
            for n in (6, 7):
                for b in range(B):
                    power(B * n + b, range(NT * b, NT * b + NT), CP)
            pool.wait_ge(act_evac, free_at[("qk", 7, B - 1, 0, CK - 1)])
            pool.wait_ge(dve_evac, free_at[("v", 7, TT - 1)])

            def four_heads(G, b, first):
                k = b + B * G
                for j in range(4):
                    o, r = divmod(4 * G + j, H // CK)
                    if not first:
                        pool.wait_ge(mh_s, k * 12 + (NT * (j + 1) - 12))
                        pool.nop(nofuse=True)
                    pool.tensor_tensor(qh4[j][:, :], qT[0:CP, o, bass.ds(b * N, N)],
                                       hmask[:, o, r:r + 1].to_broadcast([CP, N]), ALU.mult).then_inc(mh_q, 1)
                if not first:
                    pool.wait_ge(mh_o, k + 0)
                    pool.nop(nofuse=True)
                for j in range(4):
                    ins = pool.tensor_copy(vh4[j][:, :, :], vpad[0:CP, bass.ds(b * NT, NT), 4 * G + j, :])
                ins.then_inc(mh_v, 1)

            four_heads(0, 0, True)
            for G in range(HG):
                with pool.Fori(0 if G else 1, B) as b:
                    four_heads(G, b, False)
            for n in (8, 9):
                for b in range(B):
                    power(B * n + b, range(NT * b, NT * b + NT), CP)
            pool.wait_ge(bn_var, 1)
            pool.tensor_tensor(brs[:, :], bve[:, :], mhalf[0:CP, 0:B], ALU.pow).then_inc(bn_rstd, 1)
            for b in range(B):
                power(B * 10 + b, range(NT * b, NT * b + NT), CP)

        @block.sync
        def _(sp):
            sp.dma_start(convw, a["conv_w"]).then_inc(ld_conv, 16)
            sp.dma_start(vec[:, :], a["vec"]).then_inc(ld_row, 16)
            sp.dma_start(row[:, :], a["row"].to_broadcast([128, R_END])).then_inc(ld_row, 16)
            for i in range(8):
                sp.dma_start(patches[:, 2 * i:2 * i + 2, :], a["patches"][:, 2 * i:2 * i + 2, :])\
                    .then_inc(ld_patch[i], 16)
            for l in range(L):
                sp.dma_start(wqkv[l], a["qkv_w"][l]).then_inc(ld_layer[l], 16)
                sp.dma_start(wout[l], a["out_w"][l]).then_inc(ld_layer[l], 16)
                sp.dma_start(wff1[l], a["ff1_w"][l]).then_inc(ld_layer[l], 16)
                sp.dma_start(wff2[l], a["ff2_w"][l]).then_inc(ld_layer[l], 16)
            sp.dma_start(headw[:, :], a["head_w"]).then_inc(ld_head, 16)
            for b in range(B):
                sp.dma_start(h[64:CP, NT * b + 2, :], a["txt"][b]).then_inc(ld_head, 16)
            
            for i in range(3):
                sp.dma_start(wqkv96[i][:, :, :], a["qkv96"][i]).then_inc(ld_fused, 16)
            sp.dma_start(wlT[:, :, :], a["wlT"]).then_inc(ld_fused, 16)
            sp.dma_start(wmix[:, :], a["wmix"]).then_inc(ld_fused, 16)
            sp.dma_start(wdelta[:, :], a["wdelta"]).then_inc(ld_fused, 16)
            sp.dma_start(lam[:, :], a["lam"]).then_inc(ld_fused, 16)
            for i in range(4):
                sp.dma_start(qg[i][CP:CP + 1, 1, :], a["bl"]).then_inc(ld_fused, 16)
            sp.dma_start(hmask[:, :, :], a["hmask"]).then_inc(ld_fused, 16)
            sp.dma_start(vec96[:, :, :], a["vec96"]).then_inc(ld_fused, 16)
            for i in range(2):
                sp.dma_start(gate_w[i][:, :, :], a["gate_w"][i]).then_inc(ld_fused, 16)
                sp.dma_start(b2[i][:, :], a["b2"][i]).then_inc(ld_fused, 16)
                sp.dma_start(wproj[i][:, :, :], a["wproj"][i]).then_inc(ld_fused, 16)
            def load_expert(s, p, e):
                sp.dma_start(ew1[p], a["ew1"][s, bass.ds(e, 1)].rearrange("a p k f -> p (a k) f"))\
                    .then_inc(ld_exp[p], 16)
                sp.dma_start(experts[p][:, CK * F:], a["ew2"][s, bass.ds(e, 1)].rearrange("a p f -> p (a f)"))\
                    .then_inc(ld_exp[p], 16)

            sp.wait_ge(fused_consts, 1)
            for s in range(2):
                for p in range(2):
                    if s:
                        sp.wait_ge(ex_y[0], TT * (EX + p))
                    load_expert(s, p, p)
                with sp.Fori(1, EX // 2) as it:
                    for p in range(2):
                        sp.wait_ge(ex_y[s], it * (2 * TT) + TT * p)
                        load_expert(s, p, it * 2 + p)
            sp.wait_ge(ex_add[1], TT * (EX + 1))
            for b in range(B):
                sp.dma_start(out[b].rearrange("(i p) c -> p i c", p=CP), h[:, NT * b:NT * b + NT, :])\
                    .then_inc(stored, 16)
            sp.wait_ge(stored, 16 * B)



def lay_out(i):
    import numpy as np

    def g(name):
        return np.asarray(i[name])

    def cols(v):
        return v.reshape(-1, 128).T

    def cols96(v):
        return v.reshape(CK, CP).T

    def rows_to_tiles(w, p):
        return w.reshape(w.shape[0] // p, p, w.shape[1]).transpose(1, 0, 2)

    t = "L0_tok_"
    o = {}
    im = g("x").reshape(B, 32, 16, 8, 16, 8)
    o["patches"] = im.transpose(1, 3, 5, 0, 2, 4).reshape(KC, 128, TI).transpose(1, 0, 2)
    o["conv_w"] = rows_to_tiles(g(t + "conv_w").reshape(D, 2048).T, 128)
    o["qkv_w"] = g(t + "qkv_w")
    o["out_w"] = np.stack([rows_to_tiles(w, 128) for w in g(t + "out_w")])
    o["ff1_w"] = g(t + "ff1_w")
    o["ff2_w"] = np.stack([rows_to_tiles(w, 128) for w in g(t + "ff2_w")])
    o["head_w"] = g(t + "head_w")
    o["txt"] = g("txt")
    o["vec"] = np.concatenate([cols(g(t + n)) for n in ("conv_b", "ln1_g", "ln1_b", "ln2_g", "ln2_b",
                                                        "lnf_g", "lnf_b", "ff1_b")], axis=1)
    o["row"] = np.concatenate([g(n).reshape(-1) for n in (
        t + "out_b", t + "ff2_b", t + "head_b", "L0_attn_b_proj", "L0_ffn_proj_b", "L0_attn_lamb",
        "L0_ffn_gate_b")])[None]
    
    s = "L0_attn_"
    f = "L0_ffn_"
    o["qkv96"] = np.stack([rows_to_tiles(w, CP) for w in (
        g(s + "W_qkv"), g(f + "qkv_w").T,
        np.concatenate([g("L1_attn_W" + n).T for n in "qkv"], axis=1))])
    o["wlT"] = np.repeat(g(s + "W_l"), HD, axis=0).reshape(CK, CP, H).transpose(1, 0, 2)
    o["wmix"] = np.concatenate([np.repeat(np.repeat(g(s + "W_w"), RT, axis=0), RT, axis=1),
                                np.repeat(g(s + "b_w"), RT)[None]])
    o["wdelta"] = np.concatenate([np.tile(np.eye(RT, dtype=np.float32), (H, H)), np.ones((1, MR), np.float32)])
    o["lam"] = np.repeat(g(s + "lamb").reshape(HG, 4), HP, axis=1).T
    o["bl"] = np.repeat(g(s + "b_l"), RT)[None]
    o["hmask"] = np.repeat(np.eye(H // CK, dtype=np.float32), HD, axis=0)[:, None].repeat(CK, axis=1)
    o["vec96"] = np.stack([cols96(g(f + n)) for n in ("ln1_g", "ln1_b", "ln2_g", "ln2_b")], axis=1)

    def by_column_tile(w):
        p = np.zeros((4, HP, HG, C), np.float32)
        p[:, 0:HD] = w.reshape(HG, 4, HD, C).transpose(1, 2, 0, 3)
        return p.reshape(128, HG, C)

    o["wproj"] = np.stack([by_column_tile(w) for w in (g(s + "W_proj"), g(f + "proj_w").T)])
    o["gate_w"] = np.stack([rows_to_tiles(w, CP) for w in (g(f + "gate_w").T, g("L1_ffn_Wg"))])
    o["b2"] = np.stack([g(f + "b2"), g("L1_ffn_b2")])
    w1 = [g(f + "w1").transpose(0, 2, 1), g("L1_ffn_W1")]
    w2 = [g(f + "w2").transpose(0, 2, 1), g("L1_ffn_W2")]
    b1 = [g(f + "b1"), g("L1_ffn_b1")]
    o["ew1"] = np.stack([w.reshape(EX, CK, CP, F).transpose(0, 2, 1, 3) for w in w1])
    o["ew2"] = np.concatenate([
        np.stack([w.reshape(EX, FC, 128, C).transpose(0, 2, 1, 3).reshape(EX, 128, FC * C) for w in w2]),
        np.stack([v.reshape(EX, FC, 128).transpose(0, 2, 1) for v in b1])], axis=3)
    return {n: np.ascontiguousarray(v) for n, v in o.items()}


def kernel(**inputs):
    import concourse.bacc as bacc
    from concourse import mybir as mb
    from concourse.bass_utils import run_bass_kernel_spmd

    nc = bacc.Bacc("TRN2", target_bir_lowering=False, num_devices=1)
    arrays = lay_out(inputs)
    aps = {n: nc.dram_tensor("in_" + n, v.shape, mb.dt.from_np(v.dtype), kind="ExternalInput").ap()
           for n, v in arrays.items()}
    out = nc.dram_tensor("out_h", (B, N, C), F32, kind="ExternalOutput").ap()
    build(nc, aps, out)
    r = run_bass_kernel_spmd(nc, [{"in_" + n: v for n, v in arrays.items()}], core_ids=[0])
    return r.results[0]["out_h"]
```

```python
from contextlib import ExitStack

import concourse.bass as bass
from concourse import mybir

F32 = mybir.dt.float32
U32 = mybir.dt.uint32
ACT = mybir.ActivationFunctionType
ALU = mybir.AluOpType
AX = mybir.AxisListType

B = 4
D = 128
KC = 16
NI = 256
TI = B * NI
VT = TI // 128
L = 2
NH, DH = 8, 64
INNER = NH * DH
M = 512
NC4 = INNER // 128
C = 192
CP = 96
CK = C // CP
N = 288
NT = N // CP
T = B * N
TT = B * NT
H = 12
HD = 16
HP = 32
HG = H // 4
RT = 9
MR = H * RT
JT = N // RT
EX = 8
F = 768
FC = F // 128
HH = FC // 2
CHOICES = [2, 1]
SLOTS = [(T * r + EX * 127) // 128 for r in CHOICES]
SLOTS = [s + s % 2 for s in SLOTS]
GMAX = TT * 2
NB = (T + 127) // 128
K_TRI, K_CUM, K_128, K_S = 0, CP, CP + EX * EX, CP + EX * EX + NB
K_END = K_S + max(SLOTS) + 2
EPS = 1e-5
POWER = [0, 1, 2, 3, 4, 5, 6, 7, 8, 9, None, 10]

V_CONV, V_G1, V_B1, V_G2, V_B2, V_GF, V_BF, V_F1 = 0, 1, 3, 5, 7, 9, 10, 11
V_END = V_F1 + L * NC4
R_OUT = 0
R_FF2 = R_OUT + L * D
R_HEAD = R_FF2 + L * D
R_P0 = R_HEAD + C
R_P1 = R_P0 + C
R_LAM = R_P1 + C
R_GB = R_LAM + H
R_END = R_GB + EX

LD_FUSED = 16 * (1 + 3 + 4 + 4 + 2 + 6)


def build(nc, a, out):
    with ExitStack() as ctx:
        def sb(name, shape, dt=F32):
            return ctx.enter_context(nc.sbuf_tensor(name, shape, dt))

        def sem(name):
            return ctx.enter_context(nc.semaphore(name))

        bank = [ctx.enter_context(nc.psum_tensor(f"bank{i}", [128, 512], F32)) for i in range(8)]

        ident = sb("ident", [128, 128])
        ones = sb("ones", [128, 128])
        vec = sb("vec", [128, V_END])
        row = sb("row", [128, R_END])
        big = sb("big", [128, 16384])
        patches = big[:, :].rearrange("p (k t) -> p k t", k=KC)
        expkT = big[:, 0:4096].rearrange("p (c t) -> p c t", c=NC4)
        expk = big[:, 4096:8192].rearrange("p (t c) -> p t c", t=VT)
        v_v = big[:, 8192:12288].rearrange("p (t c) -> p t c", t=VT)
        qT_v = big[:, 12288:16384].rearrange("p (c t) -> p c t", c=NC4)
        gmat = big[:, 0:2048].rearrange("p (b c d) -> p b c d", b=B, c=NC4)
        low = sb("low", [128, 14848])
        at = [0]

        def low_part(n):
            at[0] += n
            assert at[0] <= 14848, at[0]
            return low[:, at[0] - n:at[0]]

        convw = low_part(KC * D).rearrange("p (k d) -> p k d", k=KC)
        ctxT = convw.rearrange("p (b c) d -> p b c d", b=B)
        wqkv = [low_part(3 * INNER) for _ in range(L)]
        wout = [low_part(NC4 * D).rearrange("p (c d) -> p c d", c=NC4) for _ in range(L)]
        wff1 = [low_part(M) for _ in range(L)]
        wff2 = [low_part(NC4 * D).rearrange("p (c d) -> p c d", c=NC4) for _ in range(L)]
        x = low_part(TI).rearrange("p (t d) -> p t d", t=VT)
        xT = low_part(TI)
        q_v = low_part(VT * INNER).rearrange("p (t c) -> p t c", t=VT)
        hid_v = q_v.rearrange("p t c -> p (t c)").rearrange("p (c t) -> p c t", c=NC4)
        at[0] = 0
        qT = low_part(CK * T).rearrange("p (c t) -> p c t", c=CK)
        kT = low_part(CK * T).rearrange("p (c t) -> p c t", c=CK)
        y = sb("y", [128, TT * C])
        yT = sb("yT", [128, CK * T])
        uT = y[:, 0:HG * N].rearrange("p (g n) -> p g n", g=HG)
        zT = y[:, HG * N:2 * HG * N].rearrange("p (g n) -> p g n", g=HG)
        oT = yT[:, 0:HG * N].rearrange("p (g n) -> p g n", g=HG)
        znat = yT[0:CP, HG * N:HG * N + NT * H * HP].rearrange("p (c h d) -> p c h d", c=NT, h=H)
        vpad = low_part(TT * H * HP).rearrange("p (t h d) -> p t h d", t=TT, h=H)
        WE = FC * C + FC
        w1all = big[0:CP, 0:EX * CK * F].rearrange("p (e f) -> p e f", e=EX)
        w2all = low[:, 5388:5388 + EX * WE].rearrange("p (e f) -> p e f", e=EX)
        w1s = [low[0:CP, CK * F * p:CK * F * (p + 1)] for p in range(2)]
        ew1 = [w.rearrange("p (k f) -> p k f", k=CK) for w in w1s]
        AT = big[0:CP, 0:NT * H * N].rearrange("p (c h n) -> p c h n", c=NT, h=H)
        P4 = [big[0:CP, NT * N * j:NT * N * (j + 1)].rearrange("p (i n) -> p i n", i=NT) for j in range(8)]
        qh4 = [big[0:CP, 8 * NT * N + N * j:8 * NT * N + N * (j + 1)] for j in range(4)]
        vh4 = [big[0:CP, 8 * NT * N + 4 * N + NT * HP * j:8 * NT * N + 4 * N + NT * HP * (j + 1)]
               .rearrange("p (c d) -> p c d", c=NT) for j in range(4)]
        oT4 = big[:, 8448:8448 + B * HG * N].rearrange("p (b g n) -> p b g n", b=B, g=HG)
        P1 = low[0:CP, 7936:7936 + TT * N].rearrange("p (t n) -> p t n", t=TT)
        PT1 = low[0:CP, 7936 + TT * N:7936 + 2 * TT * N].rearrange("p (t n) -> p t n", t=TT)
        v1 = vpad.rearrange("p t h d -> p (t h d)")[0:CP, 0:TT * C].rearrange("p (t c) -> p t c", t=TT)
        slot_part = big[:, EX * CK * F:]
        xin = [slot_part[:, 192 * p:192 * p + 192] for p in range(2)]
        xsT = [slot_part[0:CP, 384 + 256 * p:640 + 256 * p].rearrange("p (k t) -> p k t", k=CK) for p in range(2)]
        hidS = [slot_part[:, 896 + F * p:896 + F * (p + 1)].rearrange("p (f t) -> p f t", f=FC) for p in range(2)]
        yout = [slot_part[:, 896 + 2 * F + C * p:896 + 2 * F + C * (p + 1)] for p in range(2)]

        y_v = y[:, 0:TI].rearrange("p (t d) -> p t d", t=VT)
        y96 = y[0:CP, :].rearrange("p (t c) -> p t c", t=TT)
        yT_v = yT[:, 0:TI]
        yT96 = yT[0:CP, :].rearrange("p (c t) -> p c t", c=CK)
        h = sb("h", [CP, TT, C])
        z = sb("z", [CP, TT, C])
        back = [z, y96]
        headw = sb("headw", [128, C])
        wqkv96 = [sb(f"wqkv96_{i}", [CP, CK, 3 * C]) for i in range(3)]
        wproj = [sb(f"wproj{i}", [128, HG, C]) for i in range(2)]
        wlT = sb("wlT", [CP, CK, H])
        wmix = sb("wmix", [MR + 1, MR])
        wdelta = sb("wdelta", [MR + 1, MR])
        lam = sb("lam", [128, HG])
        lam_a = sb("lam_a", [128, HG])
        lam_b = sb("lam_b", [128, HG])
        qg = [sb(f"qg{i}", [CP + 1, CK, MR]) for i in range(4)]
        pt = [sb(f"pt{i}", [MR + 1, N]) for i in range(4)]
        wms = [sb(f"wms{i}", [MR + 1, MR]) for i in range(4)]
        rs = [sb(f"rs{i}", [MR + 1, 1]) for i in range(4)]
        sums = [sb(f"sums{i}", [128, 1]) for i in range(4)]
        nm = [sb(f"nm{i}", [128, 1]) for i in range(4)]
        hmask = sb("hmask", [CP, CK, H // CK])
        vec96 = sb("vec96", [CP, 4, CK])
        gate_w = [sb(f"gate_w{i}", [CP, CK, EX]) for i in range(2)]
        b2 = [sb(f"b2_{i}", [EX, C]) for i in range(2)]
        lg = sb("lg", [CP, TT, EX])
        oh = sb("oh", [CP, TT, EX])
        cw = sb("cw", [CP, TT, EX])
        top = sb("top", [CP, TT, EX])
        topi = sb("topi", [CP, TT, EX], U32)
        iota8 = sb("iota8", [CP, EX])
        s12 = sb("s12", [CP, TT])
        s12b = sb("s12b", [CP, TT])
        cwT = sb("cwT", [EX, T])
        zeros = sb("zeros", [128, C])
        consts = sb("consts", [CP, K_END])
        tri = consts[:, K_TRI:K_TRI + CP]
        cum = consts[:, K_CUM:K_CUM + EX * EX].rearrange("p (e f) -> p e f", e=EX)
        route_part = [big[0:CP, 15104 + GMAX * EX * i:15104 + GMAX * EX * (i + 1)]
                      .rearrange("p (g e) -> p g e", e=EX) for i in range(5)]
        ohr = route_part[0]
        cnt = big[0:CP, 15104 + GMAX * EX:15104 + 3 * GMAX * EX].rearrange("p (a g e) -> p a g e", a=2, e=EX)
        scan = route_part[3:5]
        cmp = big[0:CP, 15104 + 5 * GMAX * EX:15104 + 5 * GMAX * EX + (max(SLOTS) + 2) * EX]
        tiles_of = sb("tiles_of", [CP, EX])
        end_of = sb("end_of", [CP, EX])
        start_of = sb("start_of", [CP, EX])
        posf = sb("posf", [CP, GMAX])
        pos = [sb(f"pos{i}", [CP, GMAX], U32) for i in range(2)]
        eidf = sb("eidf", [1, max(SLOTS) + 2])
        eid = [sb(f"eid{i}", [1, max(SLOTS) + 2], U32) for i in range(2)]
        nmh = sb("nmh", [CP, 4, NT])
        sumh = sb("sumh", [CP, 4, NT])
        rsh = sb("rsh", [CP, 4, NT])
        ms = sb("ms", [CP, 2 * B])
        msm = sb("msm", [CP, 2 * B])
        bstat = sb("bstat", [CP, B, 2])
        bve = sb("bve", [CP, B])
        brs = sb("brs", [CP, B])
        nm1 = sb("smax1", [CP, TT])
        sum1 = sb("sum1", [CP, TT])
        rec1 = sb("rec1", [CP, TT])
        st = sb("st", [128, TT, 6])
        mv = sb("mv", [128, TT, 2])
        ve = sb("ve", [128, TT])
        rstd = sb("rstd", [128, TT])
        mhalf = sb("mhalf", [128, TT])
        nkmax = sb("nkmax", [128, 16])
        ksum = sb("ksum", [128, 16])
        krec = sb("krec", [128, 16])
        qmax = sb("qmax", [128, 8, NH])
        qsum = sb("qsum", [128, 8, NH])
        qrec = sb("qrec", [128, 8, NH])

        slots_in = [nc.dram_tensor(f"slots_in{s}", (SLOTS[s] * 128, C), F32).ap() for s in range(2)]
        slots_out = [nc.dram_tensor(f"slots_out{s}", (SLOTS[s] * 128, C), F32).ap() for s in range(2)]

        ld_row = sem("ld_row")
        ld_conv = sem("ld_conv")
        ld_patch = [sem(f"ld_patch{i}") for i in range(8)]
        ld_layer = [sem(f"ld_layer{i}") for i in range(L)]
        ld_head = sem("ld_head")
        consts_ready = sem("consts_ready")
        mm_act = sem("mm_act")
        mm_dve = sem("mm_dve")
        act_evac = sem("act_evac")
        dve_evac = sem("dve_evac")
        ln_var = sem("ln_var")
        ln_rstd = sem("ln_rstd")
        ln_y = sem("ln_y")
        dve_step = sem("dve_step")
        kmax_ready = sem("kmax_ready")
        q_exp = sem("q_exp")
        q_norm = sem("q_norm")
        ctx_zeroed = sem("ctx_zeroed")
        pool_step = sem("pool_step")
        ld_fused = sem("ld_fused")
        fused_consts = sem("fused_consts")
        wmix_ready = sem("wmix_ready")
        tk_q = sem("tk_q")
        tk_s = sem("tk_s")
        tk_max = sem("tk_max")
        tk_exp = sem("tk_exp")
        tk_r = sem("tk_r")
        tk_w = sem("tk_w")
        tk_mix = sem("tk_mix")
        tk_at = sem("tk_at")
        z_ready = sem("z_ready")
        o_ready = sem("o_ready")
        mh_q = sem("mh_q")
        mh_s = sem("mh_s")
        mh_v = sem("mh_v")
        mh_max = sem("mh_max")
        mh_exp = sem("mh_exp")
        mh_r = sem("mh_r")
        mh_p = sem("mh_p")
        mh_t = sem("mh_t")
        mh_pt = sem("mh_pt")
        mh_o = sem("mh_o")
        mh_oT = sem("mh_oT")
        sa_max = sem("sa_max")
        sa_exp = sem("sa_exp")
        bn_stat = sem("bn_stat")
        bn_var = sem("bn_var")
        bn_rstd = sem("bn_rstd")
        gate_e = sem("gate_e")
        gate_x = sem("gate_x")
        cw_ready = sem("cw_ready")
        zeros_ready = sem("zeros_ready")
        routed = [sem(f"routed{i}") for i in range(2)]
        ld_w1 = [sem(f"ld_w1{i}") for i in range(2)]
        ld_w2 = [sem(f"ld_w2{i}") for i in range(2)]
        ex_w = [sem(f"ex_w{i}") for i in range(2)]
        ld_x = [sem(f"ld_x{i}") for i in range(2)]
        ex_tp = [sem(f"ex_tp{i}") for i in range(2)]
        ex_xT = [sem(f"ex_xT{i}") for i in range(2)]
        ex_hid = [sem(f"ex_hid{i}") for i in range(2)]
        ex_act = [sem(f"ex_act{i}") for i in range(2)]
        ex_y = [sem(f"ex_y{i}") for i in range(2)]
        ex_out = [sem(f"ex_out{i}") for i in range(2)]
        st_y = [[sem(f"st_y{i}{p}") for p in range(2)] for i in range(2)]
        gathered = [[sem(f"gathered{i}{b}") for b in range(B)] for i in range(2)]
        h_part = sem("h_part")
        oh_ready = sem("oh_ready")
        stored = sem("stored")

        block = ctx.enter_context(nc.Block())

        made = {"act": 0, "dve": 0}
        read = {"act": 0, "dve": 0}
        ready_at, free_at, lies_in = {}, {}, {}
        holder = [None] * 8
        evac = {"act": act_evac, "dve": dve_evac}
        mm_ready = {"act": mm_act, "dve": mm_dve}

        @block.tensor
        def _(pe):
            turn = [0]

            def claim(key, reader, last=None):
                i = turn[0] % 8
                turn[0] += 1
                if holder[i]:
                    pe.wait_ge(evac[holder[i][0]], holder[i][1])
                last = last or reader
                made[reader] += 1
                read[last] += 1
                ready_at[key], free_at[key], lies_in[key] = made[reader], read[last], i
                holder[i] = (last, read[last])
                return bank[i]

            def done(mm, reader):
                mm.then_inc(mm_ready[reader], 1)

            pe.wait_ge(ld_conv, 16)
            halves = [claim(("conv", i), "act") for i in range(2)]
            for k in range(KC):
                if k % 2 == 0:
                    pe.wait_ge(ld_patch[k // 2], 16)
                for i in range(2):
                    mm = pe.matmul(halves[i][:, :], convw[:, k, :], patches[:, k, 512 * i:512 * i + 512],
                                   start=(k == 0), stop=(k == KC - 1))
                    if k == KC - 1:
                        done(mm, "act")
            pe.wait_ge(consts_ready, 1)
            for b in range(B):
                pe.wait_ge(act_evac, free_at[("conv", b // 2)])
                ps = claim(("x", b), "dve")
                for i in range(2):
                    t = 2 * b + i
                    mm = pe.transpose(ps[:, 128 * i:128 * i + 128], xT[:, 128 * t:128 * t + 128], ident[:, :])
                done(mm, "dve")

            def turn_tokens(n):
                for b in range(B):
                    pe.wait_ge(ln_y, B * n + b + 1)
                    ps = claim(("yT", n, b), "act")
                    for i in range(2):
                        mm = pe.transpose(ps[:, 128 * i:128 * i + 128], y_v[:, 2 * b + i, :], ident[:, :])
                    done(mm, "act")

            for l in range(L):
                turn_tokens(2 * l)
                pe.wait_ge(ld_layer[l], 64)
                w = wqkv[l]
                for b in range(B):
                    pe.wait_ge(act_evac, free_at[("yT", 2 * l, b)])
                    for p in range(2):
                        ps = claim(("k", l, b, p), "dve", "act")
                        for i in range(2):
                            c = 2 * p + i
                            mm = pe.matmul(ps[:, NI * i:NI * i + NI], w[:, INNER + 128 * c:INNER + 128 * c + 128],
                                           yT_v[:, NI * b:NI * b + NI], start=True, stop=True)
                        done(mm, "dve")
                for t in range(VT):
                    ps = claim(("q", l, t), "dve")
                    done(pe.matmul(ps[:, :], yT_v[:, 128 * t:128 * t + 128], w[:, 0:INNER],
                                   start=True, stop=True), "dve")
                    ps = claim(("v", l, t), "act")
                    done(pe.matmul(ps[:, :], yT_v[:, 128 * t:128 * t + 128], w[:, 2 * INNER:3 * INNER],
                                   start=True, stop=True), "act")
                for t in range(VT):
                    pe.wait_ge(act_evac, free_at[("k", l, t // 2, 1)])
                    ps = claim(("kt", l, t), "act")
                    for c in range(NC4):
                        mm = pe.transpose(ps[:, 128 * c:128 * c + 128], expkT[:, c, 128 * t:128 * t + 128],
                                          ident[:, :])
                    done(mm, "act")
                for b in range(B):
                    pe.wait_ge(act_evac, free_at[("kt", l, 2 * b + 1)])
                    ps = claim(("ctx", l, b), "dve")
                    for c in range(NC4):
                        for i in range(2):
                            t = 2 * b + i
                            mm = pe.matmul(ps[:, 128 * c:128 * c + 128], v_v[:, t, 128 * c:128 * c + 128],
                                           expk[:, t, 128 * c:128 * c + 128], start=(i == 0), stop=(i == 1))
                    done(mm, "dve")
                for t in range(VT):
                    pe.wait_ge(q_norm, VT * l + t + 1)
                    ps = claim(("qT", l, t), "act")
                    for c in range(NC4):
                        mm = pe.transpose(ps[:, 128 * c:128 * c + 128], q_v[:, t, 128 * c:128 * c + 128],
                                          ident[:, :])
                    done(mm, "act")
                for b in range(B):
                    pe.wait_ge(dve_evac, free_at[("ctx", l, b)])
                    ps = claim(("g", l, b), "dve")
                    for c in range(NC4):
                        mm = pe.matmul(ps[:, 128 * c:128 * c + 128], ctxT[:, b, c, :], wout[l][:, c, :],
                                       start=True, stop=True)
                    done(mm, "dve")
                for b in range(B):
                    pe.wait_ge(dve_evac, free_at[("g", l, b)])
                    ps = claim(("o", l, b), "dve")
                    for i in range(2):
                        t = 2 * b + i
                        pe.wait_ge(act_evac, free_at[("qT", l, t)])
                        for c in range(NC4):
                            mm = pe.matmul(ps[:, 128 * i:128 * i + 128], qT_v[:, c, 128 * t:128 * t + 128],
                                           gmat[:, b, c, :], start=(c == 0), stop=(c == NC4 - 1))
                    done(mm, "dve")
                turn_tokens(2 * l + 1)
                for b in range(B):
                    pe.wait_ge(act_evac, free_at[("yT", 2 * l + 1, b)])
                    for p in range(2):
                        ps = claim(("f1", l, b, p), "act")
                        for i in range(2):
                            c = 2 * p + i
                            mm = pe.matmul(ps[:, NI * i:NI * i + NI], wff1[l][:, 128 * c:128 * c + 128],
                                           yT_v[:, NI * b:NI * b + NI], start=True, stop=True)
                        done(mm, "act")
                for b in range(B):
                    pe.wait_ge(act_evac, free_at[("f1", l, b, 1)])
                    ps = claim(("f2", l, b), "dve")
                    for i in range(2):
                        t = 2 * b + i
                        for c in range(NC4):
                            mm = pe.matmul(ps[:, 128 * i:128 * i + 128], hid_v[:, c, 128 * t:128 * t + 128],
                                           wff2[l][:, c, :], start=(c == 0), stop=(c == NC4 - 1))
                    done(mm, "dve")
            turn_tokens(2 * L)
            pe.wait_ge(ld_head, 16 * (1 + B))
            for b in range(B):
                pe.wait_ge(act_evac, free_at[("yT", 2 * L, b)])
                for i in range(NT):
                    n = min(CP, NI - CP * i)
                    ps = claim(("h", b, i), "dve")
                    done(pe.matmul(ps[0:n, 0:C], yT_v[:, NI * b + CP * i:NI * b + CP * i + n], headw[:, :],
                                   start=True, stop=True), "dve")
            
            def turn96(n):
                for b in range(B):
                    pe.wait_ge(ln_y, B * n + b + 1)
                    for c in range(CK):
                        ps = claim(("yT", n, b, c), "act")
                        for i in range(NT):
                            mm = pe.transpose(ps[0:CP, CP * i:CP * i + CP],
                                              y96[:, NT * b + i, CP * c:CP * c + CP], ident[0:CP, 0:CP])
                        done(mm, "act")

            def qkv96(n, w):
                for b in range(B):
                    pe.wait_ge(act_evac, free_at[("yT", n, b, CK - 1)])
                    for j, reader in ((0, "act"), (1, "dve")):
                        for o in range(CK):
                            ps = claim(("qk", n, b, j, o), reader)
                            for k in range(CK):
                                mm = pe.matmul(ps[0:CP, 0:N], w[:, k, C * j + CP * o:C * j + CP * o + CP],
                                               yT96[:, k, N * b:N * b + N], start=(k == 0), stop=(k == CK - 1))
                            done(mm, reader)
                    for i in range(NT):
                        t = NT * b + i
                        ps = claim(("v", n, t), "dve")
                        for k in range(CK):
                            mm = pe.matmul(ps[0:CP, 0:C], yT96[:, k, CP * t:CP * t + CP],
                                           w[:, k, 2 * C:3 * C], start=(k == 0), stop=(k == CK - 1))
                        done(mm, "dve")

            def project(b, oT, w, r):
                for i in range(NT):
                    ps = claim(("proj", r, b, i), "dve")
                    pe.matmul(ps[0:CP, 0:C], ones[0:1, 0:CP], row[0:1, r:r + C], start=True, stop=False)
                    for g in range(HG):
                        mm = pe.matmul(ps[0:CP, 0:C], oT[:, g, CP * i:CP * i + CP], w[:, g, :],
                                       start=False, stop=(g == HG - 1))
                    done(mm, "dve")

            def free_banks():
                for i in range(8):
                    if holder[i]:
                        pe.wait_ge(evac[holder[i][0]], holder[i][1])
                        holder[i] = None

            pe.wait_ge(fused_consts, 1)
            turn96(5)
            pe.wait_ge(ld_fused, LD_FUSED)
            qkv96(5, wqkv96[0])
            free_banks()
            for b in range(B):
                def scores(it, u):
                    pe.wait_ge(tk_q, it * 4 + (JT * b + u + 1))
                    for k in range(CK):
                        r = CP + k
                        mm = pe.matmul(bank[u % 4][0:MR, 0:N], qg[u % 4][0:r, k, :], kT[0:r, k, N * b:N * b + N],
                                       start=(k == 0), stop=(k == CK - 1))
                    mm.then_inc(tk_s, 1)

                def mix(it, u):
                    pe.wait_ge(tk_w, it * 4 + (JT * b + u + 1))
                    for c in range(NT):
                        mm = pe.matmul(bank[4 + u][0:CP, MR * c:MR * c + MR], pt[u][:, CP * c:CP * c + CP],
                                       wms[u][:, :], start=True, stop=True)
                    mm.then_inc(tk_mix, 1)

                scores(0, 0)
                scores(0, 1)
                with pe.Fori(0, JT // 4 - 1) as it:
                    for u in range(4):
                        scores(it, u + 2)
                        mix(it, u)
                last = JT // 4 - 1
                scores(last, 2)
                mix(last, 0)
                scores(last, 3)
                for u in range(1, 4):
                    mix(last, u)
                pe.wait_ge(tk_at, JT * (b + 1))
                for g in range(HG):
                    ps = claim(("u", b, g), "act")
                    for c in range(NT):
                        for j in range(4):
                            mm = pe.matmul(ps[HP * j:HP * j + HP, 0:N], vpad[0:CP, NT * b + c, 4 * g + j, :],
                                           AT[:, c, 4 * g + j, :], start=(c == 0), stop=(c == NT - 1))
                    done(mm, "act")
                for i in range(NT):
                    pe.wait_ge(z_ready, b + 1)
                    ps = claim(("z", b, i), "act")
                    for g in range(HG):
                        mm = pe.transpose(ps[0:CP, 128 * g:128 * g + 128], zT[:, g, CP * i:CP * i + CP],
                                          ident[:, :])
                    done(mm, "act")
                for g in range(HG):
                    pe.wait_ge(act_evac, free_at[("z", b, NT - 1)])
                    ps = claim(("w", b, g), "dve")
                    for c in range(NT):
                        for j in range(4):
                            mm = pe.matmul(ps[HP * j:HP * j + HP, 0:N], znat[:, c, 4 * g + j, :],
                                           AT[:, c, 4 * g + j, :], start=(c == 0), stop=(c == NT - 1))
                    done(mm, "dve")
                pe.wait_ge(dve_evac, free_at[("w", b, HG - 1)])
                project(b, oT, wproj[0], R_P0)
                free_banks()

            turn96(7)
            qkv96(7, wqkv96[1])
            free_banks()

            def flip(k, j):
                pe.wait_ge(mh_p, k * 4 + (j + 1))
                for c in range(NT):
                    if j:
                        pe.wait_ge(mh_pt, k * 12 + (NT * j + c - 2))
                    for i in range(NT):
                        mm = pe.transpose(bank[(4, 5, 7)[c]][0:CP, CP * i:CP * i + CP],
                                          P4[j][:, i, CP * c:CP * c + CP], ident[0:CP, 0:CP])
                    mm.then_inc(mh_t, 1)

            def head_scores(G, b, j):
                k = b + B * G
                o = (4 * G + j) // (H // CK)
                pe.wait_ge(mh_q, k * 4 + (j + 1))
                for i in range(NT):
                    s = NT * j + i
                    if s >= 4:
                        pe.wait_ge(mh_exp, k * 12 + (s - 3))
                    pe.matmul(bank[s % 4][0:CP, 0:N], qh4[j][:, CP * i:CP * i + CP],
                              kT[0:CP, o, bass.ds(b * N, N)], start=True, stop=True).then_inc(mh_s, 1)

            def next_scores(k, G, b):
                pe.wait_ge(mh_q, k * 4 + 5)
                for i in range(NT):
                    pe.wait_ge(mh_exp, k * 12 + (9 + i))
                    pe.matmul(bank[i][0:CP, 0:N], qh4[0][:, CP * i:CP * i + CP],
                              kT[0:CP, 4 * G // (H // CK), bass.ds(b * N, N)], start=True, stop=True)\
                        .then_inc(mh_s, 1)

            def four_heads(G, b, following):
                k = b + B * G
                for j in range(1, 4):
                    head_scores(G, b, j)
                    flip(k, j - 1)
                if following:
                    next_scores(k, *following)
                flip(k, 3)
                pe.wait_ge(mh_v, k + 1)
                pe.wait_ge(mh_pt, k * 12 + 12)
                for c in range(NT):
                    for j in range(4):
                        mm = pe.matmul(bank[6][HP * j:HP * j + HP, 0:N], vh4[j][:, c, :], P4[4 + j][:, c, :],
                                       start=(c == 0), stop=(c == NT - 1))
                mm.then_inc(mh_o, 1)

            head_scores(0, 0, 0)
            for G in range(HG):
                with pe.Fori(0, B - 1) as b:
                    four_heads(G, b, (G, b + 1))
                four_heads(G, B - 1, (G + 1, 0) if G < HG - 1 else None)
            pe.wait_ge(mh_oT, B * HG)
            for b in range(B):
                project(b, oT4[:, b, :, :], wproj[1], R_P1)

            def mixture(s, n):
                for b in range(B):
                    pe.wait_ge(act_evac, free_at[("yT", n, b, CK - 1)])
                    ps = claim(("gate", s, b), "dve")
                    for i in range(NT):
                        t = NT * b + i
                        for k in range(CK):
                            mm = pe.matmul(ps[0:CP, EX * i:EX * i + EX], yT96[:, k, CP * t:CP * t + CP],
                                           gate_w[s][:, k, :], start=(k == 0), stop=(k == CK - 1))
                    done(mm, "dve")
                r = TT * CHOICES[s]
                pe.wait_ge(oh_ready, s + 1)
                ps = claim(("count", s), "dve")
                pe.matmul(ps[0:CP, 0:r * EX], tri, ohr[:, 0:r, :], start=True, stop=True)
                done(pe.matmul(ps[0:CP, r * EX:2 * r * EX], ones[0:CP, 0:CP], ohr[:, 0:r, :],
                               start=True, stop=True), "dve")
                pe.wait_ge(cw_ready, s + 1)
                for b in range(B):
                    ps = claim(("cwT", s, b), "act")
                    for i in range(NT):
                        mm = pe.transpose(ps[0:EX, CP * i:CP * i + CP], cw[:, NT * b + i, :], ident[0:CP, 0:CP])
                    done(mm, "act")
                for t in range(TT):
                    pe.wait_ge(act_evac, free_at[("cwT", s, t // NT)])
                    ps = claim(("b2", s, t), "dve")
                    done(pe.matmul(ps[0:CP, 0:C], cwT[:, CP * t:CP * t + CP], b2[s][:, :],
                                   start=True, stop=True), "dve")
                free_banks()
                n0 = SLOTS[0] // 2 * s
                pe.wait_ge(ld_w2[s], 16 * EX)
                pe.wait_ge(ex_out[s], 2)
                with pe.Fori(0, SLOTS[s] // 2) as it:
                    for p in range(2):
                        pe.wait_ge(ld_x[p], it * 16 + 16 * (n0 + 1))
                        for c in range(CK):
                            mm = pe.transpose(bank[p][0:CP, 128 * c:128 * c + 128],
                                              xin[p][:, CP * c:CP * c + CP], ident[:, :])
                        mm.then_inc(ex_tp[s], 1)
                    for p in range(2):
                        pe.wait_ge(ex_xT[s], it * 2 + (p + 1))
                        pe.wait_ge(ex_w[s], it * 2 + (p + 1))
                        for f in range(FC):
                            for c in range(CK):
                                mm = pe.matmul(bank[2 + 2 * p + f // HH][:, 128 * (f % HH):128 * (f % HH) + 128],
                                               ew1[p][:, c, 128 * f:128 * f + 128], xsT[p][:, c, :],
                                               start=(c == 0), stop=(c == CK - 1))
                            if f % HH == HH - 1:
                                mm.then_inc(ex_hid[s], 1)
                    for p in range(2):
                        e = pe.value_load(eid[s][0:1, bass.ds(it * 2 + p, 1)], min_val=0, max_val=EX - 1)
                        pe.wait_ge(ex_act[s], it * 4 + (2 * p + 2))
                        pe.wait_ge(ex_out[s], it * 2 + (p + 1))
                        for f in range(FC):
                            mm = pe.matmul(bank[6 + p][:, 0:C], hidS[p][:, f, :],
                                           w2all[:, bass.ds(e, 1), C * f:C * f + C],
                                           start=(f == 0), stop=(f == FC - 1))
                        mm.then_inc(ex_y[s], 1)

            turn96(8)
            mixture(0, 8)
            pe.wait_ge(bn_stat, 1)
            ps = claim(("moments",), "dve")
            done(pe.matmul(ps[0:CP, 0:2 * B], ones[0:CP, 0:CP], ms[:, :], start=True, stop=True), "dve")
            turn96(10)
            qkv96(10, wqkv96[2])
            for b in range(B):
                pe.wait_ge(act_evac, free_at[("qk", 10, b, 0, CK - 1)])
                pe.wait_ge(dve_evac, free_at[("v", 10, NT * b + NT - 1)])
                for i in range(NT):
                    t = NT * b + i
                    ps = claim(("s", t), "dve", "act")
                    for k in range(CK):
                        mm = pe.matmul(ps[0:CP, 0:N], qT[0:CP, k, CP * t:CP * t + CP],
                                       kT[0:CP, k, N * b:N * b + N], start=(k == 0), stop=(k == CK - 1))
                    done(mm, "dve")
            for b in range(B):
                pe.wait_ge(act_evac, free_at[("s", NT * b + NT - 1)])
                for c in range(NT):
                    ps = claim(("pT", b, c), "act")
                    for i in range(NT):
                        mm = pe.transpose(ps[0:CP, CP * i:CP * i + CP], P1[:, NT * b + i, CP * c:CP * c + CP],
                                          ident[0:CP, 0:CP])
                    done(mm, "act")
            for b in range(B):
                pe.wait_ge(act_evac, free_at[("pT", b, NT - 1)])
                for i in range(NT):
                    ps = claim(("a", NT * b + i), "dve")
                    for c in range(NT):
                        mm = pe.matmul(ps[0:CP, 0:C], PT1[:, NT * b + c, CP * i:CP * i + CP], v1[:, NT * b + c, :],
                                       start=(c == 0), stop=(c == NT - 1))
                    done(mm, "dve")
            turn96(11)
            mixture(1, 11)

        @block.scalar
        def _(act):
            def take(key):
                act.wait_ge(mm_act, ready_at[key])
                return bank[lies_in[key]]

            act.wait_ge(ld_row, 32)
            for i in range(2):
                ps = take(("conv", i))
                act.activation(xT[:, 512 * i:512 * i + 512], ps[:, :], ACT.Identity,
                               bias=vec[:, V_CONV:V_CONV + 1]).then_inc(act_evac, 1)

            def gain_shift(n, g, s):
                for b in range(B):
                    ps = take(("yT", n, b))
                    act.activation(yT_v[:, NI * b:NI * b + NI], ps[:, 0:NI], ACT.Identity,
                                   scale=vec[:, g:g + 1], bias=vec[:, s:s + 1]).then_inc(act_evac, 1)

            for l in range(L):
                gain_shift(2 * l, V_G1 + l, V_B1 + l)
                for b in range(B):
                    for p in range(2):
                        act.wait_ge(kmax_ready, 2 * (B * l + b) + p + 1)
                        ps = bank[lies_in[("k", l, b, p)]]
                        for i in range(2):
                            c = 2 * p + i
                            s = NC4 * b + c
                            ins = act.activation(expkT[:, c, NI * b:NI * b + NI], ps[:, NI * i:NI * i + NI],
                                                 ACT.Exp, bias=nkmax[:, s:s + 1], accum_out=ksum[:, s:s + 1])
                        ins.then_inc(act_evac, 1)
                for t in range(VT):
                    act.wait_ge(dve_evac, free_at[("q", l, t)])
                    act.activation(q_v[:, t, :], q_v[:, t, :], ACT.Exp).then_inc(q_exp, 1)
                    ps = take(("v", l, t))
                    act.activation(v_v[:, t, :], ps[:, :], ACT.Copy).then_inc(act_evac, 1)
                for t in range(VT):
                    ps = take(("kt", l, t))
                    act.activation(expk[:, t, :], ps[:, :], ACT.Copy).then_inc(act_evac, 1)
                for t in range(VT):
                    ps = take(("qT", l, t))
                    act.activation(qT_v[:, :, 128 * t:128 * t + 128],
                                   ps[:, :].rearrange("p (c t) -> p c t", c=NC4), ACT.Copy).then_inc(act_evac, 1)
                gain_shift(2 * l + 1, V_G2 + l, V_B2 + l)
                for b in range(B):
                    for p in range(2):
                        ps = take(("f1", l, b, p))
                        for i in range(2):
                            c = 2 * p + i
                            ins = act.activation(hid_v[:, c, NI * b:NI * b + NI], ps[:, NI * i:NI * i + NI],
                                                 ACT.Gelu, bias=vec[:, V_F1 + NC4 * l + c:V_F1 + NC4 * l + c + 1])
                        ins.then_inc(act_evac, 1)
            gain_shift(2 * L, V_GF, V_BF)
            
            def evac96(n, g=None, s=None):
                for b in range(B):
                    for c in range(CK):
                        ps = take(("yT", n, b, c))
                        if g is None:
                            ins = act.activation(yT96[:, c, N * b:N * b + N], ps[0:CP, 0:N], ACT.Copy)
                        else:
                            ins = act.activation(yT96[:, c, N * b:N * b + N], ps[0:CP, 0:N], ACT.Identity,
                                                 scale=vec96[:, g, c:c + 1], bias=vec96[:, s, c:c + 1])
                        ins.then_inc(act_evac, 1)

            def queries(n, scale):
                for b in range(B):
                    for o in range(CK):
                        ps = take(("qk", n, b, 0, o))
                        act.activation(qT[0:CP, o, N * b:N * b + N], ps[0:CP, 0:N], ACT.Copy, scale=scale)\
                            .then_inc(act_evac, 1)

            evac96(5)
            queries(5, HD ** -0.5)
            for b in range(B):
                with act.Fori(0, JT // 4) as it:
                    def softmax(u):
                        act.wait_ge(tk_max, it * 4 + (JT * b + u + 1))
                        act.activation(pt[u][0:MR, :], bank[u][0:MR, 0:N], ACT.Exp, bias=nm[u][0:MR, :],
                                       accum_out=sums[u][0:MR, :]).then_inc(tk_exp, 1)

                    def keep(u):
                        act.wait_ge(tk_mix, it * 4 + (JT * b + u + 1))
                        act.activation(AT[:, :, :, bass.ds(it * (4 * RT) + RT * u, RT)],
                                       bank[4 + u][0:CP, 0:NT * MR]
                                       .rearrange("p (c h n) -> p c h n", c=NT, h=H), ACT.Copy).then_inc(tk_at, 1)

                    softmax(0)
                    softmax(1)
                    softmax(2)
                    keep(0)
                    softmax(3)
                    keep(1)
                    keep(2)
                    keep(3)
                for g in range(HG):
                    ps = take(("u", b, g))
                    act.activation(uT[:, g, :], ps[:, 0:N], ACT.Copy).then_inc(act_evac, 1)
                for i in range(NT):
                    ps = take(("z", b, i))
                    act.activation(znat[:, i, :, :], ps[0:CP, 0:H * HP].rearrange("p (h d) -> p h d", h=H),
                                   ACT.Copy).then_inc(act_evac, 1)
            evac96(7, 0, 1)
            queries(7, HD ** -0.5)
            for G in range(HG):
                with act.Fori(0, B) as b:
                    k = b + B * G

                    def keep_flipped(j):
                        for c in range(NT):
                            act.wait_ge(mh_t, k * 12 + (NT * j + c + 1))
                            act.activation(P4[4 + j][:, c, :], bank[(4, 5, 7)[c]][0:CP, 0:N], ACT.Copy)\
                                .then_inc(mh_pt, 1)

                    for j in range(4):
                        for i in range(NT):
                            s = NT * j + i
                            act.wait_ge(mh_max, k * 12 + (s + 1))
                            act.activation(P4[j][:, i, :], bank[s % 4][0:CP, 0:N], ACT.Exp,
                                           bias=nmh[:, j, i:i + 1], accum_out=sumh[:, j, i:i + 1])\
                                .then_inc(mh_exp, 1)
                        if j:
                            keep_flipped(j - 1)
                    keep_flipped(3)

            def mixture(s, func):
                for b in range(B):
                    ps = take(("cwT", s, b))
                    act.activation(cwT[:, N * b:N * b + N], ps[0:EX, 0:N], ACT.Copy).then_inc(act_evac, 1)
                act.wait_ge(ld_w2[s], 16 * EX)
                act.wait_ge(ex_out[s], 2)
                with act.Fori(0, SLOTS[s] // 2) as it:
                    for p in range(2):
                        e = act.value_load(eid[s][0:1, bass.ds(it * 2 + p, 1)], min_val=0, max_val=EX - 1)
                        for q in range(2):
                            act.wait_ge(ex_hid[s], it * 4 + (2 * p + q + 1))
                            for f in range(HH * q, HH * q + HH):
                                ins = act.activation(hidS[p][:, f, :],
                                                     bank[2 + 2 * p + q][:, 128 * (f % HH):128 * (f % HH) + 128],
                                                     func, bias=w2all[:, bass.ds(e, 1), FC * C + f:FC * C + f + 1])
                            ins.then_inc(ex_act[s], 1)

            evac96(8, 2, 3)
            act.wait_ge(gate_e, 1)
            act.activation(s12[:, :], s12[:, :], ACT.Exp).then_inc(gate_x, 1)
            mixture(0, ACT.Gelu)
            evac96(10)
            queries(10, 1.0)
            for t in range(TT):
                act.wait_ge(sa_max, t + 1)
                ps = bank[lies_in[("s", t)]]
                act.activation(P1[:, t, :], ps[0:CP, 0:N], ACT.Exp, bias=nm1[:, t:t + 1],
                               accum_out=sum1[:, t:t + 1]).then_inc(act_evac, 1)
            for b in range(B):
                for c in range(NT):
                    ps = take(("pT", b, c))
                    act.activation(PT1[:, NT * b + c, :], ps[0:CP, 0:N], ACT.Copy).then_inc(act_evac, 1)
            evac96(11)
            act.wait_ge(gate_e, 2)
            act.activation(lg[:, :, :], lg[:, :, :], ACT.Exp).then_inc(gate_x, 1)
            mixture(1, ACT.Silu)

        @block.vector
        def _(dve):
            steps = [0]

            def take(key):
                dve.wait_ge(mm_dve, ready_at[key])
                return bank[lies_in[key]]

            def link(ins):
                steps[0] += 1
                ins.then_inc(dve_step, 1)
                dve.wait_ge(dve_step, steps[0])

            def ln_stats(src, tiles, rows):
                for t in tiles:
                    ins = dve.bn_stats(st[0:rows, t, :], src[:, t, :])
                link(ins)
                for t in tiles:
                    ins = dve.bn_aggr(mv[0:rows, t, :], st[0:rows, t, :])
                link(ins)
                t0, t1 = tiles[0], tiles[-1] + 1
                dve.tensor_scalar(ve[0:rows, t0:t1], mv[0:rows, t0:t1, 1], EPS, None, ALU.add).then_inc(ln_var, 1)

            def ln_apply(n, g, src, dst, tiles, rows):
                dve.wait_ge(ln_rstd, B * POWER[n] + g + 1)
                for t in tiles:
                    ins = dve.tensor_scalar(dst[:, t, :], src[:, t, :], mv[0:rows, t, 0:1], rstd[0:rows, t:t + 1],
                                            ALU.subtract, ALU.mult)
                ins.then_inc(ln_y, 1)

            def pair(b):
                return range(2 * b, 2 * b + 2)

            def add_to_x(key, b, r):
                ps = take(key)
                xs = x[:, 2 * b:2 * b + 2, :]
                dve.tensor_tensor(xs, xs, ps[:, 0:NI].rearrange("p (t d) -> p t d", t=2), ALU.add)\
                    .then_inc(dve_evac, 1)
                dve.wait_ge(dve_evac, free_at[key])
                for t in pair(b):
                    ins = dve.tensor_tensor(x[:, t, :], x[:, t, :], row[:, r:r + D], ALU.add)
                link(ins)
                ln_stats(x, pair(b), 128)

            for b in range(B):
                ps = take(("x", b))
                dve.tensor_copy(x[:, 2 * b:2 * b + 2, :], ps[:, 0:NI].rearrange("p (t d) -> p t d", t=2))\
                    .then_inc(dve_evac, 1)
                dve.wait_ge(dve_evac, free_at[("x", b)])
                ln_stats(x, pair(b), 128)
            for l in range(L):
                for b in range(B):
                    ln_apply(2 * l, b, x, y_v, pair(b), 128)
                for b in range(B):
                    for p in range(2):
                        ps = take(("k", l, b, p))
                        s = NC4 * b + 2 * p
                        dve.tensor_reduce(nkmax[:, s:s + 2], ps[:, :].rearrange("p (c t) -> p c t", c=2), AX.X,
                                          ALU.max, negate=True).then_inc(kmax_ready, 1)

                def finish_q(t):
                    dve.wait_ge(q_exp, VT * l + t + 1)
                    qh = q_v[:, t, :].rearrange("p (h d) -> p h d", h=NH)
                    link(dve.tensor_reduce(qsum[:, t, :], qh, AX.X, ALU.add))
                    link(dve.reciprocal(qrec[:, t, :], qsum[:, t, :]))
                    dve.tensor_tensor(qh, qh, qrec[:, t, :].unsqueeze(2).to_broadcast([128, NH, DH]),
                                      ALU.mult).then_inc(q_norm, 1)

                for t in range(VT):
                    ps = take(("q", l, t))
                    pq = ps[:, :].rearrange("p (h d) -> p h d", h=NH)
                    link(dve.tensor_reduce(qmax[:, t, :], pq, AX.X, ALU.max))
                    dve.tensor_tensor(q_v[:, t, :].rearrange("p (h d) -> p h d", h=NH), pq,
                                      qmax[:, t, :].unsqueeze(2).to_broadcast([128, NH, DH]),
                                      ALU.subtract).then_inc(dve_evac, 1)
                    if t >= 2:
                        finish_q(t - 2)
                finish_q(VT - 2)
                finish_q(VT - 1)
                dve.wait_ge(act_evac, free_at[("k", l, B - 1, 1)])
                link(dve.reciprocal(krec[:, :], ksum[:, :]))
                if l == 0:
                    dve.wait_ge(ctx_zeroed, 1)
                for b in range(B):
                    ps = take(("ctx", l, b))
                    pc = ps[:, :].rearrange("p (c d) -> p c d", c=NC4)
                    dve.tensor_copy(ctxT[0:64, b, :, 0:64], pc[0:64, :, 0:64])
                    dve.tensor_copy(ctxT[64:128, b, :, 64:128], pc[64:128, :, 64:128]).then_inc(dve_evac, 1)
                for b in range(B):
                    ps = take(("g", l, b))
                    dve.scalar_tensor_tensor(
                        out=gmat[:, b, :, :], in0=ps[:, :].rearrange("p (c d) -> p c d", c=NC4),
                        scalar=DH ** -0.5,
                        in1=krec[:, NC4 * b:NC4 * b + NC4].unsqueeze(2).to_broadcast([128, NC4, D]),
                        op0=ALU.mult, op1=ALU.mult).then_inc(dve_evac, 1)
                for b in range(B):
                    add_to_x(("o", l, b), b, R_OUT + D * l)
                for b in range(B):
                    ln_apply(2 * l + 1, b, x, y_v, pair(b), 128)
                for b in range(B):
                    add_to_x(("f2", l, b), b, R_FF2 + D * l)
            for b in range(B):
                ln_apply(2 * L, b, x, y_v, pair(b), 128)
            for b in range(B):
                for i in range(NT):
                    n = min(CP, NI - CP * i)
                    ps = take(("h", b, i))
                    dve.tensor_tensor(h[0:n, NT * b + i, :], ps[0:n, 0:C], row[0:n, R_HEAD:R_HEAD + C],
                                      ALU.add).then_inc(dve_evac, 1)
            
            def three(b):
                return range(NT * b, NT * b + NT)

            def normalise(n, src, dst):
                for b in range(B):
                    ln_stats(src, three(b), CP)
                for b in range(B):
                    ln_apply(n, b, src, dst, three(b), CP)

            def keys_values(n, vdst):
                for b in range(B):
                    for o in range(CK):
                        ps = take(("qk", n, b, 1, o))
                        dve.tensor_copy(kT[0:CP, o, N * b:N * b + N], ps[0:CP, 0:N]).then_inc(dve_evac, 1)
                    for t in three(b):
                        ps = take(("v", n, t))
                        dve.tensor_copy(vdst(t), ps[0:CP, 0:C].rearrange("p (h d) -> p h d", h=H))\
                            .then_inc(dve_evac, 1)

            def head_values(t):
                return vpad[0:CP, t, :, 0:HD]

            def add_projection(dst, b, r):
                for i in range(NT):
                    ps = take(("proj", r, b, i))
                    t = NT * b + i
                    dve.tensor_tensor(dst[:, t, :], dst[:, t, :], ps[0:CP, 0:C], ALU.add).then_inc(dve_evac, 1)

            dve.wait_ge(ld_head, 16 * (1 + B))
            dve.wait_ge(dve_evac, free_at[("h", B - 1, NT - 1)])
            normalise(5, h, y96)
            dve.wait_ge(ld_fused, LD_FUSED)
            dve.wait_ge(fused_consts, 1)
            dve.tensor_tensor(wmix[:, :], wmix[:, :], wdelta[:, :], ALU.mult).then_inc(wmix_ready, 1)
            dve.tensor_scalar(lam_a[:, :], lam[:, :], -2.0, 1.0, ALU.mult, ALU.add).then_inc(wmix_ready, 1)
            dve.tensor_scalar(lam_b[:, :], lam[:, :], 3.0, None, ALU.mult).then_inc(wmix_ready, 1)
            dve.wait_ge(wmix_ready, 3)
            keys_values(5, head_values)
            for b in range(B):
                with dve.Fori(0, JT // 4) as it:
                    def row_max(u):
                        dve.wait_ge(tk_s, it * 4 + (JT * b + u + 1))
                        dve.tensor_reduce(nm[u][0:MR, :], bank[u][0:MR, 0:N], AX.X, ALU.max, negate=True)\
                            .then_inc(tk_max, 1)

                    def divide(u):
                        dve.wait_ge(tk_exp, it * 4 + (JT * b + u + 1))
                        dve.reciprocal(rs[u][0:MR, :], sums[u][0:MR, :]).then_inc(tk_r, 1)
                        dve.wait_ge(tk_r, it * 4 + (JT * b + u + 1))
                        dve.tensor_scalar(wms[u][:, :], wmix[:, :], rs[u][:, 0:1], None, ALU.mult)\
                            .then_inc(tk_w, 1)

                    row_max(0)
                    row_max(1)
                    divide(0)
                    row_max(2)
                    divide(1)
                    row_max(3)
                    divide(2)
                    divide(3)
                dve.wait_ge(act_evac, free_at[("u", b, HG - 1)])
                for g in range(HG):
                    ins = dve.tensor_scalar(zT[:, g, :], uT[:, g, :], lam_b[:, g:g + 1], None, ALU.mult)
                ins.then_inc(z_ready, 1)
                for g in range(HG):
                    ps = take(("w", b, g))
                    dve.scalar_tensor_tensor(out=oT[:, g, :], in0=uT[:, g, :], scalar=lam_a[:, g:g + 1],
                                             in1=ps[:, 0:N], op0=ALU.mult, op1=ALU.add).then_inc(dve_evac, 1)
                add_projection(h, b, R_P0)
            dve.wait_ge(dve_evac, free_at[("proj", R_P0, B - 1, NT - 1)])
            normalise(6, h, z)
            dve.wait_ge(ln_y, B * 7)
            normalise(7, z, y96)
            keys_values(7, head_values)
            def keep_outputs(G, b):
                dve.wait_ge(mh_o, b + (B * G + 1))
                dve.tensor_copy(oT4[:, bass.ds(b, 1), G, :], bank[6][:, 0:N].unsqueeze(1)).then_inc(mh_oT, 1)

            def four_heads(G, b, before):
                k = b + B * G

                def divide_head(j):
                    dve.wait_ge(mh_exp, k * 12 + NT * (j + 1))
                    dve.reciprocal(rsh[:, j, :], sumh[:, j, :]).then_inc(mh_r, 1)
                    dve.wait_ge(mh_r, k * 4 + (j + 1))
                    for i in range(NT):
                        ins = dve.tensor_scalar(P4[j][:, i, :], P4[j][:, i, :], rsh[:, j, i:i + 1], None,
                                                ALU.mult)
                    ins.then_inc(mh_p, 1)

                for j in range(4):
                    for i in range(NT):
                        s = NT * j + i
                        dve.wait_ge(mh_s, k * 12 + (s + 1))
                        dve.tensor_reduce(nmh[:, j, i:i + 1], bank[s % 4][0:CP, 0:N], AX.X, ALU.max,
                                          negate=True).then_inc(mh_max, 1)
                        if i == 0 and j:
                            divide_head(j - 1)
                    if j == 0 and before:
                        keep_outputs(*before)
                divide_head(3)

            for G in range(HG):
                four_heads(G, 0, (G - 1, B - 1) if G else None)
                with dve.Fori(1, B) as b:
                    four_heads(G, b, (G, b - 1))
            keep_outputs(HG - 1, B - 1)
            for b in range(B):
                add_projection(z, b, R_P1)
            dve.wait_ge(dve_evac, free_at[("proj", R_P1, B - 1, NT - 1)])
            normalise(8, z, y96)

            def bcast(v):
                return v.unsqueeze(2).to_broadcast([CP, TT, EX])

            def experts_of_tokens():
                for t in range(TT):
                    ins = dve.max(top[:, t, :], lg[:, t, :])
                link(ins)
                for t in range(TT):
                    ins = dve.max_index(topi[:, t, :], top[:, t, :], lg[:, t, :])
                link(ins)

            def one_hot(dst, i):
                link(dve.tensor_tensor(dst[:, :, :], iota8[:, :].unsqueeze(1).to_broadcast([CP, TT, EX]),
                                       bcast(topi[:, :, i]), ALU.is_equal))

            def route(s):
                r = TT * CHOICES[s]
                for c in range(CHOICES[s]):
                    ins = dve.tensor_tensor(ohr[:, TT * c:TT * c + TT, :],
                                            iota8[:, :].unsqueeze(1).to_broadcast([CP, TT, EX]),
                                            bcast(topi[:, :, c]), ALU.is_equal)
                ins.then_inc(oh_ready, 1)
                ps = take(("count", s))
                dve.tensor_copy(cnt[:, :, 0:r, :], ps[0:CP, 0:2 * r * EX]
                                .rearrange("p (a g e) -> p a g e", a=2, g=r)).then_inc(dve_evac, 1)
                dve.wait_ge(dve_evac, free_at[("count", s)])
                old, new = cnt[:, 1, :, :], scan[0]
                d, n = 1, 0
                while d < r:
                    dve.tensor_copy(new[:, 0:d, :], old[:, 0:d, :])
                    link(dve.tensor_tensor(new[:, d:r, :], old[:, d:r, :], old[:, 0:r - d, :], ALU.add))
                    n += 1
                    old, new, d = new, scan[n % 2], 2 * d
                c3 = cmp[:, 0:EX * NB].rearrange("p (e k) -> p e k", e=EX)
                link(dve.tensor_tensor(c3, old[:, r - 1, :].unsqueeze(2).to_broadcast([CP, EX, NB]),
                                       consts[:, K_128:K_128 + NB].unsqueeze(1).to_broadcast([CP, EX, NB]),
                                       ALU.is_gt))
                link(dve.tensor_reduce(tiles_of[:, :], c3, AX.X, ALU.add))
                c3 = cmp[:, 0:EX * EX].rearrange("p (e f) -> p e f", e=EX)
                link(dve.tensor_tensor(c3, tiles_of[:, :].unsqueeze(1).to_broadcast([CP, EX, EX]), cum, ALU.mult))
                link(dve.tensor_reduce(end_of[:, :], c3, AX.X, ALU.add))
                n = SLOTS[s] + 2
                c3 = cmp[0:1, 0:n * EX].rearrange("p (s e) -> p s e", e=EX)
                link(dve.tensor_tensor(c3, end_of[0:1, :].unsqueeze(1).to_broadcast([1, n, EX]),
                                       consts[0:1, K_S:K_S + n].unsqueeze(2).to_broadcast([1, n, EX]), ALU.is_le))
                link(dve.tensor_reduce(eidf[0:1, 0:n], c3, AX.X, ALU.add))
                dve.tensor_scalar(eid[s][0:1, 0:n], eidf[0:1, 0:n], float(EX - 1), None, ALU.min)\
                    .then_inc(ex_out[s], 1)
                link(dve.tensor_tensor(start_of[:, :], end_of[:, :], tiles_of[:, :], ALU.subtract))
                link(dve.tensor_scalar(start_of[:, :], start_of[:, :], 128.0, None, ALU.mult))
                link(dve.tensor_tensor(new[:, 0:r, :], old[:, 0:r, :], cnt[:, 1, 0:r, :], ALU.subtract))
                link(dve.tensor_tensor(new[:, 0:r, :], new[:, 0:r, :], cnt[:, 0, 0:r, :], ALU.add))
                link(dve.tensor_tensor(new[:, 0:r, :], new[:, 0:r, :],
                                       start_of[:, :].unsqueeze(1).to_broadcast([CP, r, EX]), ALU.add))
                link(dve.tensor_tensor(new[:, 0:r, :], new[:, 0:r, :], ohr[:, 0:r, :], ALU.mult))
                link(dve.tensor_reduce(posf[:, 0:r], new[:, 0:r, :], AX.X, ALU.add))
                dve.tensor_copy(pos[s][:, 0:r], posf[:, 0:r]).then_inc(ex_out[s], 1)

            def add_experts(s, weights):
                for t in range(TT):
                    ps = take(("b2", s, t))
                    dve.tensor_tensor(h[:, t, :], h[:, t, :], ps[0:CP, 0:C], ALU.add).then_inc(dve_evac, 1)

                def place(p, n):
                    e = dve.value_load(eid[s][0:1, bass.ds(n, 1)], min_val=0, max_val=EX - 1)
                    dve.tensor_copy(w1s[p], w1all[:, bass.ds(e, 1), :].rearrange("p a f -> p (a f)"))\
                        .then_inc(ex_w[s], 1)

                dve.wait_ge(ld_w1[s], 16 * EX)
                dve.wait_ge(ex_out[s], 2)
                for p in range(2):
                    place(p, p)
                with dve.Fori(0, SLOTS[s] // 2) as it:
                    for p in range(2):
                        dve.wait_ge(ex_tp[s], it * 2 + (p + 1))
                        for c in range(CK):
                            part = bank[p][0:CP, 128 * c:128 * c + 128]
                            if s == 0:
                                ins = dve.tensor_scalar(xsT[p][:, c, :], part, vec96[:, 2, c:c + 1],
                                                        vec96[:, 3, c:c + 1], ALU.mult, ALU.add)
                            else:
                                ins = dve.tensor_copy(xsT[p][:, c, :], part)
                        ins.then_inc(ex_xT[s], 1)
                    for p in range(2):
                        dve.wait_ge(ex_hid[s], it * 4 + (2 * p + 2))
                        place(p, it * 2 + (p + 2))
                    for p in range(2):
                        dve.wait_ge(ex_y[s], it * 2 + (p + 1))
                        dve.wait_ge(st_y[s][p], it * 16 + 16)
                        dve.tensor_copy(yout[p], bank[6 + p][:, 0:C]).then_inc(ex_out[s], 1)
                dve.wait_ge(dve_evac, free_at[("b2", s, TT - 1)])
                for b in range(B):
                    dve.wait_ge(gathered[s][b], 16 * NT * CHOICES[s])
                    for c in range(CHOICES[s]):
                        for t in three(b):
                            ins = dve.scalar_tensor_tensor(out=h[:, t, :], in0=back[c][:, t, :],
                                                           scalar=weights[c][:, t:t + 1], in1=h[:, t, :],
                                                           op0=ALU.mult, op1=ALU.add)
                        if c < CHOICES[s] - 1:
                            link(ins)
                    ins.then_inc(h_part, 1)
                    dve.wait_ge(h_part, B * s + b + 1)
                    if s == 0:
                        ln_stats(h, three(b), CP)

            for b in range(B):
                ps = take(("gate", 0, b))
                dve.tensor_tensor(lg[:, NT * b:NT * b + NT, :],
                                  ps[0:CP, 0:NT * EX].rearrange("p (t e) -> p t e", t=NT),
                                  row[0:CP, R_GB:R_GB + EX].unsqueeze(1).to_broadcast([CP, NT, EX]),
                                  ALU.add).then_inc(dve_evac, 1)
            dve.wait_ge(dve_evac, free_at[("gate", 0, B - 1)])
            experts_of_tokens()
            dve.tensor_tensor(s12[:, :], top[:, :, 1], top[:, :, 0], ALU.subtract).then_inc(gate_e, 1)
            dve.tensor_tensor(h[:, :, :], h[:, :, :], z[:, :, :], ALU.add)
            route(0)
            one_hot(oh, 1)
            one_hot(cw, 0)
            dve.wait_ge(gate_x, 1)
            link(dve.tensor_scalar(s12b[:, :], s12[:, :], 1.0, None, ALU.add))
            link(dve.reciprocal(s12b[:, :], s12b[:, :]))
            link(dve.tensor_tensor(s12[:, :], s12[:, :], s12b[:, :], ALU.mult))
            link(dve.tensor_tensor(cw[:, :, :], cw[:, :, :], bcast(s12b[:, :]), ALU.mult))
            link(dve.tensor_tensor(oh[:, :, :], oh[:, :, :], bcast(s12[:, :]), ALU.mult))
            dve.tensor_tensor(cw[:, :, :], cw[:, :, :], oh[:, :, :], ALU.add).then_inc(cw_ready, 1)
            dve.wait_ge(cw_ready, 1)
            add_experts(0, [s12b, s12])
            for b in range(B):
                ln_apply(9, b, h, z, three(b), CP)
            dve.wait_ge(ln_y, B * 10)
            for t in range(TT):
                ins = dve.bn_stats(st[0:CP, t, :], z[:, t, :])
            link(ins)
            for b in range(B):
                ins = dve.bn_aggr(bstat[:, b, :], st[0:CP, NT * b:NT * b + NT, :])
            link(ins)
            dve.tensor_copy(ms[:, 0:B], bstat[:, :, 0])
            link(dve.tensor_tensor(ms[:, B:2 * B], bstat[:, :, 0], bstat[:, :, 0], ALU.mult))
            dve.tensor_tensor(ms[:, B:2 * B], ms[:, B:2 * B], bstat[:, :, 1], ALU.add).then_inc(bn_stat, 1)
            ps = take(("moments",))
            dve.tensor_scalar(msm[:, :], ps[0:CP, 0:2 * B], 1.0 / CP, None, ALU.mult).then_inc(dve_evac, 1)
            dve.wait_ge(dve_evac, free_at[("moments",)])
            link(dve.tensor_tensor(bve[:, :], msm[:, 0:B], msm[:, 0:B], ALU.mult))
            link(dve.tensor_tensor(bve[:, :], msm[:, B:2 * B], bve[:, :], ALU.subtract))
            dve.tensor_scalar(bve[:, :], bve[:, :], EPS, None, ALU.add).then_inc(bn_var, 1)
            dve.wait_ge(bn_rstd, 1)
            for b in range(B):
                dve.tensor_scalar(y96[:, NT * b:NT * b + NT, :], z[:, NT * b:NT * b + NT, :], msm[:, b:b + 1],
                                  brs[:, b:b + 1], ALU.subtract, ALU.mult).then_inc(ln_y, 1)
            keys_values(10, lambda t: v1[:, t, :].rearrange("p (h d) -> p h d", h=H))
            for t in range(TT):
                ps = take(("s", t))
                dve.tensor_reduce(nm1[:, t:t + 1], ps[0:CP, 0:N], AX.X, ALU.max, negate=True).then_inc(sa_max, 1)
            dve.wait_ge(act_evac, free_at[("s", TT - 1)])
            link(dve.reciprocal(rec1[:, :], sum1[:, :]))
            for t in range(TT):
                ps = take(("a", t))
                dve.scalar_tensor_tensor(out=h[:, t, :], in0=ps[0:CP, 0:C], scalar=rec1[:, t:t + 1],
                                         in1=h[:, t, :], op0=ALU.mult, op1=ALU.add).then_inc(dve_evac, 1)
            dve.wait_ge(dve_evac, free_at[("a", TT - 1)])
            normalise(11, h, y96)
            for b in range(B):
                ps = take(("gate", 1, b))
                dve.tensor_copy(lg[:, NT * b:NT * b + NT, :],
                                ps[0:CP, 0:NT * EX].rearrange("p (t e) -> p t e", t=NT)).then_inc(dve_evac, 1)
            dve.wait_ge(dve_evac, free_at[("gate", 1, B - 1)])
            experts_of_tokens()
            route(1)
            one_hot(cw, 0)
            dve.tensor_tensor(lg[:, :, :], lg[:, :, :], bcast(top[:, :, 0]), ALU.subtract).then_inc(gate_e, 1)
            dve.wait_ge(gate_x, 2)
            link(dve.tensor_reduce(s12[:, :], lg[:, :, :], AX.X, ALU.add))
            link(dve.reciprocal(s12b[:, :], s12[:, :]))
            dve.tensor_tensor(cw[:, :, :], cw[:, :, :], bcast(s12b[:, :]), ALU.mult).then_inc(cw_ready, 1)
            dve.wait_ge(cw_ready, 2)
            add_experts(1, [s12b])

        @block.gpsimd
        def _(pool):
            pool.memset(ident[:, :], 0.0).then_inc(pool_step, 1)
            pool.memset(mhalf[:, :], -0.5)
            pool.wait_ge(pool_step, 1)
            pool.affine_select(out=ident[:, :], in_=ident[:, :], compare_op=ALU.not_equal, fill=1.0, base=0,
                               pattern=[[-1, 128]], channel_multiplier=1).then_inc(consts_ready, 1)
            pool.wait_ge(consts_ready, 1)
            pool.memset(zeros[:, :], 0.0).then_inc(zeros_ready, 1)
            pool.wait_ge(zeros_ready, 1)
            for s in range(2):
                n = SLOTS[s] // 2
                for p in range(2):
                    pool.dma_start(slots_in[s][128 * n * p:128 * n * (p + 1), :].rearrange("(s p) c -> p s c", p=128),
                                 zeros[:, :].unsqueeze(1).to_broadcast([128, n, C])).then_inc(st_y[s][p], 16)

            def power(n, tiles, rows):
                pool.wait_ge(ln_var, n + 1)
                t0, t1 = tiles[0], tiles[-1] + 1
                pool.tensor_tensor(rstd[0:rows, t0:t1], ve[0:rows, t0:t1], mhalf[0:rows, t0:t1], ALU.pow)\
                    .then_inc(ln_rstd, 1)

            for n in range(2 * L + 1):
                if n == 1:
                    pool.memset(ctxT, 0.0).then_inc(ctx_zeroed, 1)
                for b in range(B):
                    power(B * n + b, range(2 * b, 2 * b + 2), 128)
            
            pool.wait_ge(act_evac, free_at[("yT", 2 * L, B - 1)])
            pool.memset(vpad[0:CP, :, :, HD:HP], 0.0).then_inc(pool_step, 1)
            pool.wait_ge(pool_step, 2)
            pool.memset(kT[CP:CP + 1, 1, :], 1.0).then_inc(pool_step, 1)
            pool.wait_ge(pool_step, 3)
            pool.memset(ones[:, :], 1.0)
            for i in range(4):
                pool.memset(pt[i][:, :], 1.0)
                pool.memset(rs[i][:, :], 1.0)
            pool.iota(iota8[:, :], [[1, EX]], base=0, channel_multiplier=0, allow_small_or_imprecise_dtypes=True)\
                .then_inc(fused_consts, 1)
            for b in range(B):
                power(B * 5 + b, range(NT * b, NT * b + NT), CP)

            pool.wait_ge(act_evac, free_at[("qk", 5, B - 1, 0, CK - 1)])
            pool.wait_ge(ld_fused, LD_FUSED)

            def mixed_queries(u, n0):
                pool.tensor_tensor(
                    qg[u][0:CP, :, :].rearrange("p k (h n) -> p k h n", h=H),
                    qT[0:CP, :, bass.ds(n0, RT)].unsqueeze(2).to_broadcast([CP, CK, H, RT]),
                    wlT[:, :, :].unsqueeze(3).to_broadcast([CP, CK, H, RT]), ALU.mult).then_inc(tk_q, 1)

            for u in range(4):
                mixed_queries(u, RT * u)
            with pool.Fori(1, B * JT // 4) as it:
                for u in range(4):
                    pool.wait_ge(tk_s, it * 4 + (u - 3))
                    mixed_queries(u, it * (4 * RT) + RT * u)
            for n in (6, 7):
                for b in range(B):
                    power(B * n + b, range(NT * b, NT * b + NT), CP)
            pool.wait_ge(act_evac, free_at[("qk", 7, B - 1, 0, CK - 1)])
            pool.wait_ge(dve_evac, free_at[("v", 7, TT - 1)])

            def four_heads(G, b, first):
                k = b + B * G
                for j in range(4):
                    o, r = divmod(4 * G + j, H // CK)
                    if not first:
                        pool.wait_ge(mh_s, k * 12 + (NT * (j + 1) - 12))
                        pool.nop(nofuse=True)
                    pool.tensor_tensor(qh4[j][:, :], qT[0:CP, o, bass.ds(b * N, N)],
                                       hmask[:, o, r:r + 1].to_broadcast([CP, N]), ALU.mult).then_inc(mh_q, 1)
                if not first:
                    pool.wait_ge(mh_o, k + 0)
                    pool.nop(nofuse=True)
                for j in range(4):
                    ins = pool.tensor_copy(vh4[j][:, :, :], vpad[0:CP, bass.ds(b * NT, NT), 4 * G + j, :])
                ins.then_inc(mh_v, 1)

            four_heads(0, 0, True)
            for G in range(HG):
                with pool.Fori(0 if G else 1, B) as b:
                    four_heads(G, b, False)
            def mixture(s):
                for p in range(2):
                    pool.wait_ge(st_y[s][p], 16)
                pool.wait_ge(ex_out[s], 2)
                for g in range(TT * CHOICES[s]):
                    pool.indirect_dma_start(slots_in[s], bass.IndirectOffsetOnAxis(ap=pos[s][:, g:g + 1], axis=0),
                                            y96[:, g % TT, :], None).then_inc(routed[s], 16)
                with pool.Fori(0, SLOTS[s] // 2) as it:
                    for p in range(2):
                        pool.wait_ge(ex_out[s], it * 2 + (p + 3))
                        pool.dma_start(slots_out[s][bass.ds(it * 256 + 128 * p, 128), :], yout[p])\
                            .then_inc(st_y[s][p], 16)
                for p in range(2):
                    pool.wait_ge(st_y[s][p], 16 + 16 * (SLOTS[s] // 2))
                for b in range(B):
                    for c in range(CHOICES[s]):
                        for g in range(TT * c + NT * b, TT * c + NT * b + NT):
                            pool.indirect_dma_start(back[g // TT][:, g % TT, :], None, slots_out[s],
                                                    bass.IndirectOffsetOnAxis(ap=pos[s][:, g:g + 1], axis=0))\
                                .then_inc(gathered[s][b], 16)

            for b in range(B):
                power(B * 8 + b, range(NT * b, NT * b + NT), CP)
            mixture(0)
            for b in range(B):
                power(B * 9 + b, range(NT * b, NT * b + NT), CP)
            pool.wait_ge(bn_var, 1)
            pool.tensor_tensor(brs[:, :], bve[:, :], mhalf[0:CP, 0:B], ALU.pow).then_inc(bn_rstd, 1)
            for b in range(B):
                power(B * 10 + b, range(NT * b, NT * b + NT), CP)
            mixture(1)

        @block.sync
        def _(sp):
            sp.dma_start(convw, a["conv_w"]).then_inc(ld_conv, 16)
            sp.dma_start(vec[:, :], a["vec"]).then_inc(ld_row, 16)
            sp.dma_start(row[:, :], a["row"].to_broadcast([128, R_END])).then_inc(ld_row, 16)
            for i in range(8):
                sp.dma_start(patches[:, 2 * i:2 * i + 2, :], a["patches"][:, 2 * i:2 * i + 2, :])\
                    .then_inc(ld_patch[i], 16)
            for l in range(L):
                sp.dma_start(wqkv[l], a["qkv_w"][l]).then_inc(ld_layer[l], 16)
                sp.dma_start(wout[l], a["out_w"][l]).then_inc(ld_layer[l], 16)
                sp.dma_start(wff1[l], a["ff1_w"][l]).then_inc(ld_layer[l], 16)
                sp.dma_start(wff2[l], a["ff2_w"][l]).then_inc(ld_layer[l], 16)
            sp.dma_start(headw[:, :], a["head_w"]).then_inc(ld_head, 16)
            for b in range(B):
                sp.dma_start(h[64:CP, NT * b + 2, :], a["txt"][b]).then_inc(ld_head, 16)
            
            sp.dma_start(consts[:, :], a["consts"]).then_inc(ld_fused, 16)
            for i in range(3):
                sp.dma_start(wqkv96[i][:, :, :], a["qkv96"][i]).then_inc(ld_fused, 16)
            sp.dma_start(wlT[:, :, :], a["wlT"]).then_inc(ld_fused, 16)
            sp.dma_start(wmix[:, :], a["wmix"]).then_inc(ld_fused, 16)
            sp.dma_start(wdelta[:, :], a["wdelta"]).then_inc(ld_fused, 16)
            sp.dma_start(lam[:, :], a["lam"]).then_inc(ld_fused, 16)
            for i in range(4):
                sp.dma_start(qg[i][CP:CP + 1, 1, :], a["bl"]).then_inc(ld_fused, 16)
            sp.dma_start(hmask[:, :, :], a["hmask"]).then_inc(ld_fused, 16)
            sp.dma_start(vec96[:, :, :], a["vec96"]).then_inc(ld_fused, 16)
            for i in range(2):
                sp.dma_start(gate_w[i][:, :, :], a["gate_w"][i]).then_inc(ld_fused, 16)
                sp.dma_start(b2[i][:, :], a["b2"][i]).then_inc(ld_fused, 16)
                sp.dma_start(wproj[i][:, :, :], a["wproj"][i]).then_inc(ld_fused, 16)
            def load_w1(s):
                for e in range(EX):
                    sp.dma_start(w1all[:, e, :], a["ew1"][s, e].rearrange("p k f -> p (k f)")).then_inc(ld_w1[s], 16)

            def load_w2(s):
                for e in range(EX):
                    sp.dma_start(w2all[:, e, :], a["ew2"][s, e]).then_inc(ld_w2[s], 16)

            def load_x(s, p, n):
                sp.dma_start(xin[p], slots_in[s][bass.ds(n * 128, 128), :]).then_inc(ld_x[p], 16)

            for s in range(2):
                if s == 0:
                    sp.wait_ge(dve_evac, free_at[("proj", R_P1, B - 1, NT - 1)])
                    load_w1(0)
                else:
                    sp.wait_ge(ex_w[0], SLOTS[0] + 2)
                    load_w1(1)
                    sp.wait_ge(dve_evac, free_at[("a", TT - 1)])
                load_w2(s)
                sp.wait_ge(routed[s], 16 * TT * CHOICES[s])
                for p in range(2):
                    load_x(s, p, p)
                with sp.Fori(1, SLOTS[s] // 2) as it:
                    for p in range(2):
                        sp.wait_ge(ex_tp[s], it * 2 + (p - 1))
                        load_x(s, p, it * 2 + p)
            for b in range(B):
                sp.wait_ge(h_part, B + b + 1)
                sp.dma_start(out[b].rearrange("(i p) c -> p i c", p=CP), h[:, NT * b:NT * b + NT, :])\
                    .then_inc(stored, 16)
            sp.wait_ge(stored, 16 * B)



def lay_out(i):
    import numpy as np

    def g(name):
        return np.asarray(i[name])

    def cols(v):
        return v.reshape(-1, 128).T

    def cols96(v):
        return v.reshape(CK, CP).T

    def rows_to_tiles(w, p):
        return w.reshape(w.shape[0] // p, p, w.shape[1]).transpose(1, 0, 2)

    t = "L0_tok_"
    o = {}
    im = g("x").reshape(B, 32, 16, 8, 16, 8)
    o["patches"] = im.transpose(1, 3, 5, 0, 2, 4).reshape(KC, 128, TI).transpose(1, 0, 2)
    o["conv_w"] = rows_to_tiles(g(t + "conv_w").reshape(D, 2048).T, 128)
    o["qkv_w"] = g(t + "qkv_w")
    o["out_w"] = np.stack([rows_to_tiles(w, 128) for w in g(t + "out_w")])
    o["ff1_w"] = g(t + "ff1_w")
    o["ff2_w"] = np.stack([rows_to_tiles(w, 128) for w in g(t + "ff2_w")])
    o["head_w"] = g(t + "head_w")
    o["txt"] = g("txt")
    o["vec"] = np.concatenate([cols(g(t + n)) for n in ("conv_b", "ln1_g", "ln1_b", "ln2_g", "ln2_b",
                                                        "lnf_g", "lnf_b", "ff1_b")], axis=1)
    o["row"] = np.concatenate([g(n).reshape(-1) for n in (
        t + "out_b", t + "ff2_b", t + "head_b", "L0_attn_b_proj", "L0_ffn_proj_b", "L0_attn_lamb",
        "L0_ffn_gate_b")])[None]
    
    o["consts"] = np.concatenate([
        np.triu(np.ones((CP, CP), np.float32), 1),
        np.tile(np.tril(np.ones((EX, EX), np.float32)).reshape(1, -1), (CP, 1)),
        np.tile(np.arange(NB, dtype=np.float32)[None] * 128, (CP, 1)),
        np.tile(np.arange(max(SLOTS) + 2, dtype=np.float32)[None], (CP, 1))], axis=1)
    s = "L0_attn_"
    f = "L0_ffn_"
    o["qkv96"] = np.stack([rows_to_tiles(w, CP) for w in (
        g(s + "W_qkv"), g(f + "qkv_w").T,
        np.concatenate([g("L1_attn_W" + n).T for n in "qkv"], axis=1))])
    o["wlT"] = np.repeat(g(s + "W_l"), HD, axis=0).reshape(CK, CP, H).transpose(1, 0, 2)
    o["wmix"] = np.concatenate([np.repeat(np.repeat(g(s + "W_w"), RT, axis=0), RT, axis=1),
                                np.repeat(g(s + "b_w"), RT)[None]])
    o["wdelta"] = np.concatenate([np.tile(np.eye(RT, dtype=np.float32), (H, H)), np.ones((1, MR), np.float32)])
    o["lam"] = np.repeat(g(s + "lamb").reshape(HG, 4), HP, axis=1).T
    o["bl"] = np.repeat(g(s + "b_l"), RT)[None]
    o["hmask"] = np.repeat(np.eye(H // CK, dtype=np.float32), HD, axis=0)[:, None].repeat(CK, axis=1)
    o["vec96"] = np.stack([cols96(g(f + n)) for n in ("ln1_g", "ln1_b", "ln2_g", "ln2_b")], axis=1)

    def by_column_tile(w):
        p = np.zeros((4, HP, HG, C), np.float32)
        p[:, 0:HD] = w.reshape(HG, 4, HD, C).transpose(1, 2, 0, 3)
        return p.reshape(128, HG, C)

    o["wproj"] = np.stack([by_column_tile(w) for w in (g(s + "W_proj"), g(f + "proj_w").T)])
    o["gate_w"] = np.stack([rows_to_tiles(w, CP) for w in (g(f + "gate_w").T, g("L1_ffn_Wg"))])
    o["b2"] = np.stack([g(f + "b2"), g("L1_ffn_b2")])
    w1 = [g(f + "w1").transpose(0, 2, 1), g("L1_ffn_W1")]
    w2 = [g(f + "w2").transpose(0, 2, 1), g("L1_ffn_W2")]
    b1 = [g(f + "b1"), g("L1_ffn_b1")]
    o["ew1"] = np.stack([w.reshape(EX, CK, CP, F).transpose(0, 2, 1, 3) for w in w1])
    o["ew2"] = np.concatenate([
        np.stack([w.reshape(EX, FC, 128, C).transpose(0, 2, 1, 3).reshape(EX, 128, FC * C) for w in w2]),
        np.stack([v.reshape(EX, FC, 128).transpose(0, 2, 1) for v in b1])], axis=3)
    return {n: np.ascontiguousarray(v) for n, v in o.items()}


def kernel(**inputs):
    import concourse.bacc as bacc
    from concourse import mybir as mb
    from concourse.bass_utils import run_bass_kernel_spmd

    nc = bacc.Bacc("TRN2", target_bir_lowering=False, num_devices=1)
    arrays = lay_out(inputs)
    aps = {n: nc.dram_tensor("in_" + n, v.shape, mb.dt.from_np(v.dtype), kind="ExternalInput").ap()
           for n, v in arrays.items()}
    out = nc.dram_tensor("out_h", (B, N, C), F32, kind="ExternalOutput").ap()
    build(nc, aps, out)
    r = run_bass_kernel_spmd(nc, [{"in_" + n: v for n, v in arrays.items()}], core_ids=[0])
    return r.results[0]["out_h"]
```

```python
from contextlib import ExitStack

import concourse.bass as bass
from concourse import mybir

F32 = mybir.dt.float32
BF16 = mybir.dt.bfloat16
U32 = mybir.dt.uint32
ACT = mybir.ActivationFunctionType
ALU = mybir.AluOpType
AX = mybir.AxisListType

B = 4
D = 128
KC = 16
NI = 256
TI = B * NI
VT = TI // 128
L = 2
NH, DH = 8, 64
INNER = NH * DH
M = 512
NC4 = INNER // 128
C = 192
CP = 96
CK = C // CP
N = 288
NT = N // CP
T = B * N
TT = B * NT
H = 12
HD = 16
HP = 32
HG = H // 4
RT = 9
MR = H * RT
JT = N // RT
EX = 8
F = 768
FC = F // 128
HH = FC // 2
CHOICES = [2, 1]
SLOTS = [(T * r + EX * 127) // 128 for r in CHOICES]
SLOTS = [s + s % 2 for s in SLOTS]
GMAX = TT * 2
NB = (T + 127) // 128
K_TRI, K_CUM, K_128, K_S = 0, CP, CP + EX * EX, CP + EX * EX + NB
K_ROW = K_S + max(SLOTS) + 2
K_P1 = K_ROW + GMAX
K_LO = K_P1 + 1
K_END = K_LO + 128
ROUTE_AT, SMALL_AT, W2_AT, P1_AT = 15104, 16288, 5388, 7936
EPS = 1e-5
POWER = [0, 1, 2, 3, 4, 5, 6, 7, 8, 9, None, 10]

V_CONV, V_G1, V_B1, V_G2, V_B2, V_GF, V_BF, V_F1 = 0, 1, 3, 5, 7, 9, 10, 11
V_SPARE = V_F1 + L * NC4
V_END = V_SPARE + 2
R_OUT = 0
R_FF2 = R_OUT + L * D
R_HEAD = R_FF2 + L * D
R_P0 = R_HEAD + C
R_P1 = R_P0 + C
R_LAM = R_P1 + C
R_GB = R_LAM + H
R_END = R_GB + EX

LD_FUSED = 16 * (1 + 3 + 4 + 4 + 2 + 6)


def build(nc, a, out):
    with ExitStack() as ctx:
        def sb(name, shape, dt=F32):
            return ctx.enter_context(nc.sbuf_tensor(name, shape, dt))

        def sem(name):
            return ctx.enter_context(nc.semaphore(name))

        bank = [ctx.enter_context(nc.psum_tensor(f"bank{i}", [128, 512], F32)) for i in range(8)]

        ident = sb("ident", [128, 128])
        ones = sb("ones", [128, 128])
        vec = sb("vec", [128, V_END])
        row = sb("row", [128, R_END])
        big = sb("big", [128, 16384])
        patches = big[:, :].rearrange("p (k t) -> p k t", k=KC)
        expkT = big[:, 0:4096].rearrange("p (c t) -> p c t", c=NC4)
        expk = big[:, 4096:8192].rearrange("p (t c) -> p t c", t=VT)
        v_v = big[:, 8192:12288].rearrange("p (t c) -> p t c", t=VT)
        qT_v = big[:, 12288:16384].rearrange("p (c t) -> p c t", c=NC4)
        gmat = big[:, 0:2048].rearrange("p (b c d) -> p b c d", b=B, c=NC4)
        low = sb("low", [128, 14848])
        at = [0]

        def low_part(n):
            at[0] += n
            assert at[0] <= 14848, at[0]
            return low[:, at[0] - n:at[0]]

        convw = low_part(KC * D).rearrange("p (k d) -> p k d", k=KC)
        ctxT = convw.rearrange("p (b c) d -> p b c d", b=B)
        wqkv = [low_part(3 * INNER) for _ in range(L)]
        wout = [low_part(NC4 * D).rearrange("p (c d) -> p c d", c=NC4) for _ in range(L)]
        wff1 = [low_part(M) for _ in range(L)]
        wff2 = [low_part(NC4 * D).rearrange("p (c d) -> p c d", c=NC4) for _ in range(L)]
        x = low_part(TI).rearrange("p (t d) -> p t d", t=VT)
        xT = low_part(TI)
        q_v = low_part(VT * INNER).rearrange("p (t c) -> p t c", t=VT)
        hid_v = q_v.rearrange("p t c -> p (t c)").rearrange("p (c t) -> p c t", c=NC4)
        at[0] = 0
        qT = low_part(CK * T).rearrange("p (c t) -> p c t", c=CK)
        kT = low_part(CK * T).rearrange("p (c t) -> p c t", c=CK)
        y = sb("y", [128, TT * C])
        yT = sb("yT", [128, CK * T])
        uT = y[:, 0:HG * N].rearrange("p (g n) -> p g n", g=HG)
        zT = y[:, HG * N:2 * HG * N].rearrange("p (g n) -> p g n", g=HG)
        oT = yT[:, 0:HG * N].rearrange("p (g n) -> p g n", g=HG)
        znat = yT[0:CP, HG * N:HG * N + NT * H * HP].rearrange("p (c h d) -> p c h d", c=NT, h=H)
        vpad = low_part(TT * H * HP).rearrange("p (t h d) -> p t h d", t=TT, h=H)
        WE = FC * C + FC
        w1all = big[0:CP, 0:EX * CK * F].rearrange("p (e f) -> p e f", e=EX)
        w2all = low[:, W2_AT:W2_AT + EX * WE].rearrange("p (e f) -> p e f", e=EX)
        w1s = [low[0:CP, CK * F * p:CK * F * (p + 1)] for p in range(2)]
        ew1 = [w.rearrange("p (k f) -> p k f", k=CK) for w in w1s]
        AT = big[0:CP, 0:NT * H * N].rearrange("p (c h n) -> p c h n", c=NT, h=H)
        P4 = [big[0:CP, NT * N * j:NT * N * (j + 1)].rearrange("p (i n) -> p i n", i=NT) for j in range(8)]
        qh4 = [big[0:CP, 8 * NT * N + N * j:8 * NT * N + N * (j + 1)] for j in range(4)]
        vh4 = [big[0:CP, 8 * NT * N + 4 * N + NT * HP * j:8 * NT * N + 4 * N + NT * HP * (j + 1)]
               .rearrange("p (c d) -> p c d", c=NT) for j in range(4)]
        oT4 = big[:, 8448:8448 + B * HG * N].rearrange("p (b g n) -> p b g n", b=B, g=HG)
        P1 = low[0:CP, P1_AT:P1_AT + TT * N].rearrange("p (t n) -> p t n", t=TT)
        PT1 = low[0:CP, P1_AT + TT * N:P1_AT + 2 * TT * N].rearrange("p (t n) -> p t n", t=TT)
        v1 = vpad.rearrange("p t h d -> p (t h d)")[0:CP, 0:TT * C].rearrange("p (t c) -> p t c", t=TT)
        slot_part = big[:, EX * CK * F:]
        xin = [slot_part[:, 192 * p:192 * p + 192] for p in range(2)]
        xsT = [slot_part[0:CP, 384 + 256 * p:640 + 256 * p].rearrange("p (k t) -> p k t", k=CK) for p in range(2)]
        hidS = [slot_part[:, 896 + F * p:896 + F * (p + 1)].rearrange("p (f t) -> p f t", f=FC) for p in range(2)]
        yout = [slot_part[:, 896 + 2 * F + C * p:896 + 2 * F + C * (p + 1)] for p in range(2)]

        y_v = y[:, 0:TI].rearrange("p (t d) -> p t d", t=VT)
        y96 = y[0:CP, :].rearrange("p (t c) -> p t c", t=TT)
        yT_v = yT[:, 0:TI]
        yT96 = yT[0:CP, :].rearrange("p (c t) -> p c t", c=CK)
        h = sb("h", [CP, TT, C])
        z = sb("z", [CP, TT, C])
        back = [z, y96]
        headw = sb("headw", [128, C])
        wqkv96 = [sb(f"wqkv96_{i}", [CP, CK, 3 * C]) for i in range(3)]
        wproj = [sb(f"wproj{i}", [128, HG, C]) for i in range(2)]
        wlT = sb("wlT", [CP, CK, H])
        wmix = sb("wmix", [MR + 1, MR])
        wdelta = sb("wdelta", [MR + 1, MR])
        lam = sb("lam", [128, HG])
        lam_a = sb("lam_a", [128, HG])
        lam_b = sb("lam_b", [128, HG])
        qg = [sb(f"qg{i}", [CP + 1, CK, MR]) for i in range(4)]
        pt = [sb(f"pt{i}", [MR + 1, N]) for i in range(4)]
        wms = [sb(f"wms{i}", [MR + 1, MR]) for i in range(4)]
        rs = [sb(f"rs{i}", [MR + 1, 1]) for i in range(4)]
        sums = [sb(f"sums{i}", [128, 1]) for i in range(4)]
        nm = [sb(f"nm{i}", [128, 1]) for i in range(4)]
        hmask = sb("hmask", [CP, CK, H // CK])
        vec96 = sb("vec96", [CP, 4, CK])
        gate_w = [sb(f"gate_w{i}", [CP, CK, EX]) for i in range(2)]
        b2 = [sb(f"b2_{i}", [EX, C]) for i in range(2)]
        lg = sb("lg", [CP, TT, EX])
        oh = sb("oh", [CP, TT, EX])
        cw = sb("cw", [CP, TT, EX])
        top = sb("top", [CP, TT, EX])
        topi = sb("topi", [CP, TT, EX], U32)
        iota8 = sb("iota8", [CP, EX])
        s12 = sb("s12", [CP, TT])
        s12b = sb("s12b", [CP, TT])
        cwT = sb("cwT", [EX, T])
        consts = sb("consts", [CP, K_END])
        tri = consts[:, K_TRI:K_TRI + CP]
        cum = consts[:, K_CUM:K_CUM + EX * EX].rearrange("p (e f) -> p e f", e=EX)
        route_part = [big[0:CP, ROUTE_AT + GMAX * EX * i:ROUTE_AT + GMAX * EX * (i + 1)]
                      .rearrange("p (g e) -> p g e", e=EX) for i in range(5)]
        ohr = route_part[0]
        cnt = big[0:CP, ROUTE_AT + GMAX * EX:ROUTE_AT + 3 * GMAX * EX].rearrange("p (a g e) -> p a g e", a=2, e=EX)
        scan = route_part[3:5]
        cmp = big[0:CP, ROUTE_AT + 5 * GMAX * EX:ROUTE_AT + 5 * GMAX * EX + (max(SLOTS) + 2) * EX]
        small = big[0:CP, SMALL_AT:16384].rearrange("p (a g) -> p a g", g=GMAX)
        past = slot_part[0:CP, 0:GMAX * (max(SLOTS) + 1)]
        in_tile = slot_part[0:CP, GMAX * (max(SLOTS) + 1):2 * GMAX * (max(SLOTS) + 1)].bitcast(BF16)
        place_of = low[0:CP, 0:GMAX * 64].bitcast(BF16).rearrange("p (g n) -> p g n", g=GMAX)
        one_tile = slot_part[0:CP, 2 * GMAX * (max(SLOTS) + 1):3 * GMAX * (max(SLOTS) + 1)]
        slot_f = slot_part[:, 3 * GMAX * (max(SLOTS) + 1):3 * GMAX * (max(SLOTS) + 1) + 3 * max(SLOTS)]\
            .rearrange("p (a n) -> p a n", a=3)
        tiles_of = sb("tiles_of", [CP, EX])
        end_of = sb("end_of", [CP, EX])
        start_of = sb("start_of", [CP, EX])
        posf = sb("posf", [CP, GMAX])
        slot_row = [sb(f"slot_row{i}", [128, SLOTS[i]], U32) for i in range(2)]
        eidf = sb("eidf", [1, max(SLOTS) + 2])
        eid = [sb(f"eid{i}", [1, max(SLOTS) + 2], U32) for i in range(2)]
        nmh = sb("nmh", [CP, 4, NT])
        sumh = sb("sumh", [CP, 4, NT])
        rsh = sb("rsh", [CP, 4, NT])
        ms = sb("ms", [CP, 2 * B])
        msm = sb("msm", [CP, 2 * B])
        bstat = sb("bstat", [CP, B, 2])
        bve = sb("bve", [CP, B])
        brs = sb("brs", [CP, B])
        nm1 = sb("smax1", [CP, TT])
        sum1 = sb("sum1", [CP, TT])
        rec1 = sb("rec1", [CP, TT])
        st = sb("st", [128, TT, 6])
        mv = sb("mv", [128, TT, 2])
        ve = sb("ve", [128, TT])
        rstd = sb("rstd", [128, TT])
        mhalf = sb("mhalf", [128, TT])
        nkmax = sb("nkmax", [128, 16])
        ksum = sb("ksum", [128, 16])
        krec = sb("krec", [128, 16])
        qmax = sb("qmax", [128, 8, NH])
        qsum = sb("qsum", [128, 8, NH])
        qrec = sb("qrec", [128, 8, NH])

        ROWS = [T * r + 128 for r in CHOICES]
        tokens = [nc.dram_tensor(f"tokens{s}", (ROWS[s], C), F32).ap() for s in range(2)]
        results = [nc.dram_tensor(f"results{s}", (ROWS[s], C), F32).ap() for s in range(2)]

        ld_row = sem("ld_row")
        ld_conv = sem("ld_conv")
        ld_patch = [sem(f"ld_patch{i}") for i in range(8)]
        ld_layer = [sem(f"ld_layer{i}") for i in range(L)]
        ld_head = sem("ld_head")
        consts_ready = sem("consts_ready")
        mm_act = sem("mm_act")
        mm_dve = sem("mm_dve")
        act_evac = sem("act_evac")
        dve_evac = sem("dve_evac")
        ln_var = sem("ln_var")
        ln_rstd = sem("ln_rstd")
        ln_y = sem("ln_y")
        dve_step = sem("dve_step")
        kmax_ready = sem("kmax_ready")
        q_exp = sem("q_exp")
        q_norm = sem("q_norm")
        ctx_zeroed = sem("ctx_zeroed")
        pool_step = sem("pool_step")
        ld_fused = sem("ld_fused")
        fused_consts = sem("fused_consts")
        wmix_ready = sem("wmix_ready")
        tk_q = sem("tk_q")
        tk_s = sem("tk_s")
        tk_max = sem("tk_max")
        tk_exp = sem("tk_exp")
        tk_r = sem("tk_r")
        tk_w = sem("tk_w")
        tk_mix = sem("tk_mix")
        tk_at = sem("tk_at")
        z_ready = sem("z_ready")
        o_ready = sem("o_ready")
        mh_q = sem("mh_q")
        mh_s = sem("mh_s")
        mh_v = sem("mh_v")
        mh_max = sem("mh_max")
        mh_exp = sem("mh_exp")
        mh_r = sem("mh_r")
        mh_p = sem("mh_p")
        mh_t = sem("mh_t")
        mh_pt = sem("mh_pt")
        mh_o = sem("mh_o")
        mh_oT = sem("mh_oT")
        sa_max = sem("sa_max")
        sa_exp = sem("sa_exp")
        bn_stat = sem("bn_stat")
        bn_var = sem("bn_var")
        bn_rstd = sem("bn_rstd")
        bn_y = sem("bn_y")
        gate_e = sem("gate_e")
        gate_x = sem("gate_x")
        cw_ready = sem("cw_ready")
        zeros_ready = sem("zeros_ready")
        tokens_out = [sem(f"tokens_out{i}") for i in range(2)]
        in_slots = sem("in_slots")
        ld_w1 = [sem(f"ld_w1{i}") for i in range(2)]
        ld_w2 = [sem(f"ld_w2{i}") for i in range(2)]
        ex_w = [sem(f"ex_w{i}") for i in range(2)]
        ld_x = [sem(f"ld_x{i}") for i in range(2)]
        ex_tp = [sem(f"ex_tp{i}") for i in range(2)]
        ex_xT = [sem(f"ex_xT{i}") for i in range(2)]
        ex_hid = [sem(f"ex_hid{i}") for i in range(2)]
        ex_act = [sem(f"ex_act{i}") for i in range(2)]
        ex_y = [sem(f"ex_y{i}") for i in range(2)]
        ex_out = [sem(f"ex_out{i}") for i in range(2)]
        st_y = [[sem(f"st_y{i}{p}") for p in range(2)] for i in range(2)]
        gathered = [[sem(f"gathered{i}{b}") for b in range(B)] for i in range(2)]
        h_part = sem("h_part")
        oh_ready = sem("oh_ready")
        stored = sem("stored")

        block = ctx.enter_context(nc.Block())

        made = {"act": 0, "dve": 0}
        read = {"act": 0, "dve": 0}
        ready_at, free_at, lies_in = {}, {}, {}
        holder = [None] * 8
        evac = {"act": act_evac, "dve": dve_evac}
        mm_ready = {"act": mm_act, "dve": mm_dve}

        @block.tensor
        def _(pe):
            turn = [0]

            def claim(key, reader, last=None):
                i = turn[0] % 8
                turn[0] += 1
                if holder[i]:
                    pe.wait_ge(evac[holder[i][0]], holder[i][1])
                last = last or reader
                made[reader] += 1
                read[last] += 1
                ready_at[key], free_at[key], lies_in[key] = made[reader], read[last], i
                holder[i] = (last, read[last])
                return bank[i]

            def done(mm, reader):
                mm.then_inc(mm_ready[reader], 1)

            pe.wait_ge(ld_conv, 16)
            halves = [claim(("conv", i), "act") for i in range(2)]
            for k in range(KC):
                if k % 2 == 0:
                    pe.wait_ge(ld_patch[k // 2], 16)
                for i in range(2):
                    mm = pe.matmul(halves[i][:, :], convw[:, k, :], patches[:, k, 512 * i:512 * i + 512],
                                   start=(k == 0), stop=(k == KC - 1))
                    if k == KC - 1:
                        done(mm, "act")
            pe.wait_ge(consts_ready, 1)
            for b in range(B):
                pe.wait_ge(act_evac, free_at[("conv", b // 2)])
                ps = claim(("x", b), "dve")
                for i in range(2):
                    t = 2 * b + i
                    mm = pe.transpose(ps[:, 128 * i:128 * i + 128], xT[:, 128 * t:128 * t + 128], ident[:, :])
                done(mm, "dve")

            def turn_tokens(n):
                for b in range(B):
                    pe.wait_ge(ln_y, B * n + b + 1)
                    ps = claim(("yT", n, b), "act")
                    for i in range(2):
                        mm = pe.transpose(ps[:, 128 * i:128 * i + 128], y_v[:, 2 * b + i, :], ident[:, :])
                    done(mm, "act")

            for l in range(L):
                turn_tokens(2 * l)
                pe.wait_ge(ld_layer[l], 64)
                w = wqkv[l]
                for b in range(B):
                    pe.wait_ge(act_evac, free_at[("yT", 2 * l, b)])
                    for p in range(2):
                        ps = claim(("k", l, b, p), "dve", "act")
                        for i in range(2):
                            c = 2 * p + i
                            mm = pe.matmul(ps[:, NI * i:NI * i + NI], w[:, INNER + 128 * c:INNER + 128 * c + 128],
                                           yT_v[:, NI * b:NI * b + NI], start=True, stop=True)
                        done(mm, "dve")
                for t in range(VT):
                    ps = claim(("q", l, t), "dve")
                    done(pe.matmul(ps[:, :], yT_v[:, 128 * t:128 * t + 128], w[:, 0:INNER],
                                   start=True, stop=True), "dve")
                    ps = claim(("v", l, t), "act")
                    done(pe.matmul(ps[:, :], yT_v[:, 128 * t:128 * t + 128], w[:, 2 * INNER:3 * INNER],
                                   start=True, stop=True), "act")
                for t in range(VT):
                    pe.wait_ge(act_evac, free_at[("k", l, t // 2, 1)])
                    ps = claim(("kt", l, t), "act")
                    for c in range(NC4):
                        mm = pe.transpose(ps[:, 128 * c:128 * c + 128], expkT[:, c, 128 * t:128 * t + 128],
                                          ident[:, :])
                    done(mm, "act")
                for b in range(B):
                    pe.wait_ge(act_evac, free_at[("kt", l, 2 * b + 1)])
                    ps = claim(("ctx", l, b), "dve")
                    for c in range(NC4):
                        for i in range(2):
                            t = 2 * b + i
                            mm = pe.matmul(ps[:, 128 * c:128 * c + 128], v_v[:, t, 128 * c:128 * c + 128],
                                           expk[:, t, 128 * c:128 * c + 128], start=(i == 0), stop=(i == 1))
                    done(mm, "dve")
                for t in range(VT):
                    pe.wait_ge(q_norm, VT * l + t + 1)
                    ps = claim(("qT", l, t), "act")
                    for c in range(NC4):
                        mm = pe.transpose(ps[:, 128 * c:128 * c + 128], q_v[:, t, 128 * c:128 * c + 128],
                                          ident[:, :])
                    done(mm, "act")
                for b in range(B):
                    pe.wait_ge(dve_evac, free_at[("ctx", l, b)])
                    ps = claim(("g", l, b), "dve")
                    for c in range(NC4):
                        mm = pe.matmul(ps[:, 128 * c:128 * c + 128], ctxT[:, b, c, :], wout[l][:, c, :],
                                       start=True, stop=True)
                    done(mm, "dve")
                for b in range(B):
                    pe.wait_ge(dve_evac, free_at[("g", l, b)])
                    ps = claim(("o", l, b), "dve")
                    for i in range(2):
                        t = 2 * b + i
                        pe.wait_ge(act_evac, free_at[("qT", l, t)])
                        for c in range(NC4):
                            mm = pe.matmul(ps[:, 128 * i:128 * i + 128], qT_v[:, c, 128 * t:128 * t + 128],
                                           gmat[:, b, c, :], start=(c == 0), stop=(c == NC4 - 1))
                    done(mm, "dve")
                turn_tokens(2 * l + 1)
                for b in range(B):
                    pe.wait_ge(act_evac, free_at[("yT", 2 * l + 1, b)])
                    for p in range(2):
                        ps = claim(("f1", l, b, p), "act")
                        for i in range(2):
                            c = 2 * p + i
                            mm = pe.matmul(ps[:, NI * i:NI * i + NI], wff1[l][:, 128 * c:128 * c + 128],
                                           yT_v[:, NI * b:NI * b + NI], start=True, stop=True)
                        done(mm, "act")
                for b in range(B):
                    pe.wait_ge(act_evac, free_at[("f1", l, b, 1)])
                    ps = claim(("f2", l, b), "dve")
                    for i in range(2):
                        t = 2 * b + i
                        for c in range(NC4):
                            mm = pe.matmul(ps[:, 128 * i:128 * i + 128], hid_v[:, c, 128 * t:128 * t + 128],
                                           wff2[l][:, c, :], start=(c == 0), stop=(c == NC4 - 1))
                    done(mm, "dve")
            turn_tokens(2 * L)
            pe.wait_ge(ld_head, 16 * (1 + B))
            for b in range(B):
                pe.wait_ge(act_evac, free_at[("yT", 2 * L, b)])
                for i in range(NT):
                    n = min(CP, NI - CP * i)
                    ps = claim(("h", b, i), "dve")
                    done(pe.matmul(ps[0:n, 0:C], yT_v[:, NI * b + CP * i:NI * b + CP * i + n], headw[:, :],
                                   start=True, stop=True), "dve")
            
            def turn96_of(n, b):
                for c in range(CK):
                    ps = claim(("yT", n, b, c), "act")
                    for i in range(NT):
                        mm = pe.transpose(ps[0:CP, CP * i:CP * i + CP],
                                          y96[:, NT * b + i, CP * c:CP * c + CP], ident[0:CP, 0:CP])
                    done(mm, "act")

            def turn96(n):
                for b in range(B):
                    pe.wait_ge(ln_y, B * POWER[n] + b + 1)
                    turn96_of(n, b)

            def qkv96(n, w):
                for b in range(B):
                    pe.wait_ge(act_evac, free_at[("yT", n, b, CK - 1)])
                    for j, reader in ((0, "act"), (1, "dve")):
                        for o in range(CK):
                            ps = claim(("qk", n, b, j, o), reader)
                            for k in range(CK):
                                mm = pe.matmul(ps[0:CP, 0:N], w[:, k, C * j + CP * o:C * j + CP * o + CP],
                                               yT96[:, k, N * b:N * b + N], start=(k == 0), stop=(k == CK - 1))
                            done(mm, reader)
                    for i in range(NT):
                        t = NT * b + i
                        ps = claim(("v", n, t), "dve")
                        for k in range(CK):
                            mm = pe.matmul(ps[0:CP, 0:C], yT96[:, k, CP * t:CP * t + CP],
                                           w[:, k, 2 * C:3 * C], start=(k == 0), stop=(k == CK - 1))
                        done(mm, "dve")

            def project(b, oT, w, r):
                for i in range(NT):
                    ps = claim(("proj", r, b, i), "dve")
                    pe.matmul(ps[0:CP, 0:C], ones[0:1, 0:CP], row[0:1, r:r + C], start=True, stop=False)
                    for g in range(HG):
                        mm = pe.matmul(ps[0:CP, 0:C], oT[:, g, CP * i:CP * i + CP], w[:, g, :],
                                       start=False, stop=(g == HG - 1))
                    done(mm, "dve")

            def free_banks():
                for i in range(8):
                    if holder[i]:
                        pe.wait_ge(evac[holder[i][0]], holder[i][1])
                        holder[i] = None

            pe.wait_ge(fused_consts, 1)
            turn96(5)
            pe.wait_ge(ld_fused, LD_FUSED)
            qkv96(5, wqkv96[0])
            free_banks()
            for b in range(B):
                def scores(it, u):
                    pe.wait_ge(tk_q, it * 4 + (JT * b + u + 1))
                    for k in range(CK):
                        r = CP + k
                        mm = pe.matmul(bank[u % 4][0:MR, 0:N], qg[u % 4][0:r, k, :], kT[0:r, k, N * b:N * b + N],
                                       start=(k == 0), stop=(k == CK - 1))
                    mm.then_inc(tk_s, 1)

                def mix(it, u):
                    pe.wait_ge(tk_w, it * 4 + (JT * b + u + 1))
                    for c in range(NT):
                        mm = pe.matmul(bank[4 + u][0:CP, MR * c:MR * c + MR], pt[u][:, CP * c:CP * c + CP],
                                       wms[u][:, :], start=True, stop=True)
                    mm.then_inc(tk_mix, 1)

                scores(0, 0)
                scores(0, 1)
                with pe.Fori(0, JT // 4 - 1) as it:
                    for u in range(4):
                        scores(it, u + 2)
                        mix(it, u)
                last = JT // 4 - 1
                scores(last, 2)
                mix(last, 0)
                scores(last, 3)
                for u in range(1, 4):
                    mix(last, u)
                pe.wait_ge(tk_at, JT * (b + 1))
                for g in range(HG):
                    ps = claim(("u", b, g), "act")
                    for c in range(NT):
                        for j in range(4):
                            mm = pe.matmul(ps[HP * j:HP * j + HP, 0:N], vpad[0:CP, NT * b + c, 4 * g + j, :],
                                           AT[:, c, 4 * g + j, :], start=(c == 0), stop=(c == NT - 1))
                    done(mm, "act")
                for i in range(NT):
                    pe.wait_ge(z_ready, b + 1)
                    ps = claim(("z", b, i), "act")
                    for g in range(HG):
                        mm = pe.transpose(ps[0:CP, 128 * g:128 * g + 128], zT[:, g, CP * i:CP * i + CP],
                                          ident[:, :])
                    done(mm, "act")
                for g in range(HG):
                    pe.wait_ge(act_evac, free_at[("z", b, NT - 1)])
                    ps = claim(("w", b, g), "dve")
                    for c in range(NT):
                        for j in range(4):
                            mm = pe.matmul(ps[HP * j:HP * j + HP, 0:N], znat[:, c, 4 * g + j, :],
                                           AT[:, c, 4 * g + j, :], start=(c == 0), stop=(c == NT - 1))
                    done(mm, "dve")
                pe.wait_ge(dve_evac, free_at[("w", b, HG - 1)])
                project(b, oT, wproj[0], R_P0)
                free_banks()

            turn96(7)
            qkv96(7, wqkv96[1])
            free_banks()

            def flip(k, j):
                pe.wait_ge(mh_p, k * 4 + (j + 1))
                for c in range(NT):
                    if j:
                        pe.wait_ge(mh_pt, k * 12 + (NT * j + c - 2))
                    for i in range(NT):
                        mm = pe.transpose(bank[(4, 5, 7)[c]][0:CP, CP * i:CP * i + CP],
                                          P4[j][:, i, CP * c:CP * c + CP], ident[0:CP, 0:CP])
                    mm.then_inc(mh_t, 1)

            def head_scores(G, b, j):
                k = b + B * G
                o = (4 * G + j) // (H // CK)
                pe.wait_ge(mh_q, k * 4 + (j + 1))
                for i in range(NT):
                    s = NT * j + i
                    if s >= 4:
                        pe.wait_ge(mh_exp, k * 12 + (s - 3))
                    pe.matmul(bank[s % 4][0:CP, 0:N], qh4[j][:, CP * i:CP * i + CP],
                              kT[0:CP, o, bass.ds(b * N, N)], start=True, stop=True).then_inc(mh_s, 1)

            def next_scores(k, G, b):
                pe.wait_ge(mh_q, k * 4 + 5)
                for i in range(NT):
                    pe.wait_ge(mh_exp, k * 12 + (9 + i))
                    pe.matmul(bank[i][0:CP, 0:N], qh4[0][:, CP * i:CP * i + CP],
                              kT[0:CP, 4 * G // (H // CK), bass.ds(b * N, N)], start=True, stop=True)\
                        .then_inc(mh_s, 1)

            def outputs(k):
                pe.wait_ge(mh_v, k + 1)
                pe.wait_ge(mh_pt, k * 12 + 12)
                for c in range(NT):
                    for j in range(4):
                        mm = pe.matmul(bank[6][HP * j:HP * j + HP, 0:N], vh4[j][:, c, :], P4[4 + j][:, c, :],
                                       start=(c == 0), stop=(c == NT - 1))
                mm.then_inc(mh_o, 1)

            def four_heads(G, b, first, following):
                k = b + B * G
                for j in range(1, 4):
                    head_scores(G, b, j)
                    if j == 1 and not first:
                        outputs(k - 1)
                    flip(k, j - 1)
                if following:
                    next_scores(k, *following)
                flip(k, 3)

            head_scores(0, 0, 0)
            for G in range(HG):
                four_heads(G, 0, G == 0, (G, 1))
                with pe.Fori(1, B - 1) as b:
                    four_heads(G, b, False, (G, b + 1))
                four_heads(G, B - 1, False, (G + 1, 0) if G < HG - 1 else None)
            outputs(B * HG - 1)
            pe.wait_ge(mh_oT, B * HG)
            for b in range(B):
                project(b, oT4[:, b, :, :], wproj[1], R_P1)

            def mixture(s, n):
                for b in range(B):
                    pe.wait_ge(act_evac, free_at[("yT", n, b, CK - 1)])
                    ps = claim(("gate", s, b), "dve")
                    for i in range(NT):
                        t = NT * b + i
                        for k in range(CK):
                            mm = pe.matmul(ps[0:CP, EX * i:EX * i + EX], yT96[:, k, CP * t:CP * t + CP],
                                           gate_w[s][:, k, :], start=(k == 0), stop=(k == CK - 1))
                    done(mm, "dve")
                r = TT * CHOICES[s]
                pe.wait_ge(oh_ready, s + 1)
                ps = claim(("count", s), "dve")
                pe.matmul(ps[0:CP, 0:r * EX], tri, ohr[:, 0:r, :], start=True, stop=True)
                done(pe.matmul(ps[0:CP, r * EX:2 * r * EX], ones[0:CP, 0:CP], ohr[:, 0:r, :],
                               start=True, stop=True), "dve")
                pe.wait_ge(in_slots, s + 1)
                ps = claim(("slots", s), "dve")
                n = SLOTS[s]
                for g in range(r):
                    mm = pe.matmul(ps[:, 0:2 * n], place_of[:, g, :], in_tile[:, 2 * n * g:2 * n * g + 2 * n],
                                   start=(g == 0), stop=(g == r - 1))
                done(mm, "dve")
                free_banks()
                n0 = SLOTS[0] // 2 * s
                pe.wait_ge(ld_w2[s], 16 * EX)
                pe.wait_ge(ex_out[s], 2)

                def turn_slots(p, turn):
                    pe.wait_ge(ld_x[p], turn)
                    for c in range(CK):
                        mm = pe.transpose(bank[p][0:CP, 128 * c:128 * c + 128],
                                          xin[p][:, CP * c:CP * c + CP], ident[:, :])
                    mm.then_inc(ex_tp[s], 1)

                def two_tiles(it, next_turn):
                    for p in range(2):
                        pe.wait_ge(ex_xT[s], it * 2 + (p + 1))
                        pe.wait_ge(ex_w[s], it * 2 + (p + 1))
                        for f in range(FC):
                            for c in range(CK):
                                mm = pe.matmul(bank[2 + 2 * p + f // HH][:, 128 * (f % HH):128 * (f % HH) + 128],
                                               ew1[p][:, c, 128 * f:128 * f + 128], xsT[p][:, c, :],
                                               start=(c == 0), stop=(c == CK - 1))
                            if f % HH == HH - 1:
                                mm.then_inc(ex_hid[s], 1)
                    if next_turn is not None:
                        for p in range(2):
                            turn_slots(p, next_turn)
                    for p in range(2):
                        e = pe.value_load(eid[s][0:1, bass.ds(it * 2 + p, 1)], min_val=0, max_val=EX - 1)
                        pe.wait_ge(ex_act[s], it * 4 + (2 * p + 2))
                        pe.wait_ge(ex_out[s], it * 2 + (p + 1))
                        for f in range(FC):
                            mm = pe.matmul(bank[6 + p][:, 0:C], hidS[p][:, f, :],
                                           w2all[:, bass.ds(e, 1), C * f:C * f + C],
                                           start=(f == 0), stop=(f == FC - 1))
                        mm.then_inc(ex_y[s], 1)

                for p in range(2):
                    turn_slots(p, 16 * (n0 + 1))
                with pe.Fori(0, SLOTS[s] // 2 - 1) as it:
                    two_tiles(it, it * 16 + 16 * (n0 + 2))
                two_tiles(SLOTS[s] // 2 - 1, None)
                pe.wait_ge(ex_out[s], SLOTS[s] + 2)
                pe.wait_ge(cw_ready, s + 1)
                for b in range(B):
                    ps = claim(("cwT", s, b), "act")
                    for i in range(NT):
                        mm = pe.transpose(ps[0:EX, CP * i:CP * i + CP], cw[:, NT * b + i, :], ident[0:CP, 0:CP])
                    done(mm, "act")
                for t in range(TT):
                    pe.wait_ge(act_evac, free_at[("cwT", s, t // NT)])
                    ps = claim(("b2", s, t), "dve")
                    done(pe.matmul(ps[0:CP, 0:C], cwT[:, CP * t:CP * t + CP], b2[s][:, :],
                                   start=True, stop=True), "dve")

            turn96(8)
            mixture(0, 8)
            def moments(b):
                pe.wait_ge(bn_stat, b + 1)
                ps = claim(("moments", b), "dve")
                done(pe.matmul(ps[0:CP, 0:2], ones[0:CP, 0:CP], ms[:, 2 * b:2 * b + 2], start=True, stop=True), "dve")

            def turn_joint(b):
                pe.wait_ge(bn_y, b + 1)
                turn96_of(10, b)

            for b in range(B - 1):
                moments(b)
            for b in range(B - 2):
                turn_joint(b)
            moments(B - 1)
            for b in range(B - 2, B):
                turn_joint(b)
            qkv96(10, wqkv96[2])
            for b in range(B):
                pe.wait_ge(act_evac, free_at[("qk", 10, b, 0, CK - 1)])
                pe.wait_ge(dve_evac, free_at[("v", 10, NT * b + NT - 1)])
                for i in range(NT):
                    t = NT * b + i
                    ps = claim(("s", t), "dve", "act")
                    for k in range(CK):
                        mm = pe.matmul(ps[0:CP, 0:N], qT[0:CP, k, CP * t:CP * t + CP],
                                       kT[0:CP, k, N * b:N * b + N], start=(k == 0), stop=(k == CK - 1))
                    done(mm, "dve")
            for b in range(B):
                pe.wait_ge(act_evac, free_at[("s", NT * b + NT - 1)])
                for c in range(NT):
                    ps = claim(("pT", b, c), "act")
                    for i in range(NT):
                        mm = pe.transpose(ps[0:CP, CP * i:CP * i + CP], P1[:, NT * b + i, CP * c:CP * c + CP],
                                          ident[0:CP, 0:CP])
                    done(mm, "act")
            for b in range(B):
                pe.wait_ge(act_evac, free_at[("pT", b, NT - 1)])
                for i in range(NT):
                    ps = claim(("a", NT * b + i), "dve")
                    for c in range(NT):
                        mm = pe.matmul(ps[0:CP, 0:C], PT1[:, NT * b + c, CP * i:CP * i + CP], v1[:, NT * b + c, :],
                                       start=(c == 0), stop=(c == NT - 1))
                    done(mm, "dve")
            turn96(11)
            mixture(1, 11)

        @block.scalar
        def _(act):
            def take(key):
                act.wait_ge(mm_act, ready_at[key])
                return bank[lies_in[key]]

            act.wait_ge(ld_row, 32)
            for i in range(2):
                ps = take(("conv", i))
                act.activation(xT[:, 512 * i:512 * i + 512], ps[:, :], ACT.Identity,
                               bias=vec[:, V_CONV:V_CONV + 1]).then_inc(act_evac, 1)

            def gain_shift(n, g, s):
                for b in range(B):
                    ps = take(("yT", n, b))
                    act.activation(yT_v[:, NI * b:NI * b + NI], ps[:, 0:NI], ACT.Identity,
                                   scale=vec[:, g:g + 1], bias=vec[:, s:s + 1]).then_inc(act_evac, 1)

            for l in range(L):
                gain_shift(2 * l, V_G1 + l, V_B1 + l)
                for b in range(B):
                    for p in range(2):
                        act.wait_ge(kmax_ready, 2 * (B * l + b) + p + 1)
                        ps = bank[lies_in[("k", l, b, p)]]
                        for i in range(2):
                            c = 2 * p + i
                            s = NC4 * b + c
                            ins = act.activation(expkT[:, c, NI * b:NI * b + NI], ps[:, NI * i:NI * i + NI],
                                                 ACT.Exp, bias=nkmax[:, s:s + 1], accum_out=ksum[:, s:s + 1])
                        ins.then_inc(act_evac, 1)
                for t in range(VT):
                    act.wait_ge(dve_evac, free_at[("q", l, t)])
                    act.activation(q_v[:, t, :], q_v[:, t, :], ACT.Exp).then_inc(q_exp, 1)
                    ps = take(("v", l, t))
                    act.activation(v_v[:, t, :], ps[:, :], ACT.Copy).then_inc(act_evac, 1)
                for t in range(VT):
                    ps = take(("kt", l, t))
                    act.activation(expk[:, t, :], ps[:, :], ACT.Copy).then_inc(act_evac, 1)
                for t in range(VT):
                    ps = take(("qT", l, t))
                    act.activation(qT_v[:, :, 128 * t:128 * t + 128],
                                   ps[:, :].rearrange("p (c t) -> p c t", c=NC4), ACT.Copy).then_inc(act_evac, 1)
                gain_shift(2 * l + 1, V_G2 + l, V_B2 + l)
                for b in range(B):
                    for p in range(2):
                        ps = take(("f1", l, b, p))
                        for i in range(2):
                            c = 2 * p + i
                            ins = act.activation(hid_v[:, c, NI * b:NI * b + NI], ps[:, NI * i:NI * i + NI],
                                                 ACT.Gelu, bias=vec[:, V_F1 + NC4 * l + c:V_F1 + NC4 * l + c + 1])
                        ins.then_inc(act_evac, 1)
            gain_shift(2 * L, V_GF, V_BF)
            
            def evac96(n, g=None, s=None):
                for b in range(B):
                    for c in range(CK):
                        ps = take(("yT", n, b, c))
                        if g is None:
                            ins = act.activation(yT96[:, c, N * b:N * b + N], ps[0:CP, 0:N], ACT.Copy)
                        else:
                            ins = act.activation(yT96[:, c, N * b:N * b + N], ps[0:CP, 0:N], ACT.Identity,
                                                 scale=vec96[:, g, c:c + 1], bias=vec96[:, s, c:c + 1])
                        ins.then_inc(act_evac, 1)

            def queries(n, scale):
                for b in range(B):
                    for o in range(CK):
                        ps = take(("qk", n, b, 0, o))
                        act.activation(qT[0:CP, o, N * b:N * b + N], ps[0:CP, 0:N], ACT.Copy, scale=scale)\
                            .then_inc(act_evac, 1)

            evac96(5)
            queries(5, HD ** -0.5)
            for b in range(B):
                with act.Fori(0, JT // 4) as it:
                    def softmax(u):
                        act.wait_ge(tk_max, it * 4 + (JT * b + u + 1))
                        act.activation(pt[u][0:MR, :], bank[u][0:MR, 0:N], ACT.Exp, bias=nm[u][0:MR, :],
                                       accum_out=sums[u][0:MR, :]).then_inc(tk_exp, 1)

                    def keep(u):
                        act.wait_ge(tk_mix, it * 4 + (JT * b + u + 1))
                        act.activation(AT[:, :, :, bass.ds(it * (4 * RT) + RT * u, RT)],
                                       bank[4 + u][0:CP, 0:NT * MR]
                                       .rearrange("p (c h n) -> p c h n", c=NT, h=H), ACT.Copy).then_inc(tk_at, 1)

                    softmax(0)
                    softmax(1)
                    softmax(2)
                    keep(0)
                    softmax(3)
                    keep(1)
                    keep(2)
                    keep(3)
                for g in range(HG):
                    ps = take(("u", b, g))
                    act.activation(uT[:, g, :], ps[:, 0:N], ACT.Copy).then_inc(act_evac, 1)
                for i in range(NT):
                    ps = take(("z", b, i))
                    act.activation(znat[:, i, :, :], ps[0:CP, 0:H * HP].rearrange("p (h d) -> p h d", h=H),
                                   ACT.Copy).then_inc(act_evac, 1)
            evac96(7, 0, 1)
            queries(7, HD ** -0.5)
            def keep_flipped(k, j):
                for c in range(NT):
                    act.wait_ge(mh_t, k * 12 + (NT * j + c + 1))
                    act.activation(P4[4 + j][:, c, :], bank[(4, 5, 7)[c]][0:CP, 0:N], ACT.Copy).then_inc(mh_pt, 1)

            def four_heads(G, b, first):
                k = b + B * G
                for j in range(4):
                    for i in range(NT):
                        s = NT * j + i
                        act.wait_ge(mh_max, k * 12 + (s + 1))
                        act.activation(P4[j][:, i, :], bank[s % 4][0:CP, 0:N], ACT.Exp,
                                       bias=nmh[:, j, i:i + 1], accum_out=sumh[:, j, i:i + 1]).then_inc(mh_exp, 1)
                    if j:
                        keep_flipped(k, j - 1)
                    elif not first:
                        keep_flipped(k - 1, 3)

            for G in range(HG):
                four_heads(G, 0, G == 0)
                with act.Fori(1, B) as b:
                    four_heads(G, b, False)
            keep_flipped(B * HG - 1, 3)

            def mixture(s, func):
                act.wait_ge(ld_w2[s], 16 * EX)
                act.wait_ge(ex_out[s], 2)
                with act.Fori(0, SLOTS[s] // 2) as it:
                    for p in range(2):
                        e = act.value_load(eid[s][0:1, bass.ds(it * 2 + p, 1)], min_val=0, max_val=EX - 1)
                        for q in range(2):
                            act.wait_ge(ex_hid[s], it * 4 + (2 * p + q + 1))
                            for f in range(HH * q, HH * q + HH):
                                ins = act.activation(hidS[p][:, f, :],
                                                     bank[2 + 2 * p + q][:, 128 * (f % HH):128 * (f % HH) + 128],
                                                     func, bias=w2all[:, bass.ds(e, 1), FC * C + f:FC * C + f + 1])
                            ins.then_inc(ex_act[s], 1)

                for b in range(B):
                    ps = take(("cwT", s, b))
                    act.activation(cwT[:, N * b:N * b + N], ps[0:EX, 0:N], ACT.Copy).then_inc(act_evac, 1)

            evac96(8, 2, 3)
            act.wait_ge(gate_e, 1)
            act.activation(s12[:, :], s12[:, :], ACT.Exp).then_inc(gate_x, 1)
            mixture(0, ACT.Gelu)
            evac96(10)
            queries(10, 1.0)
            for t in range(TT):
                act.wait_ge(sa_max, t + 1)
                ps = bank[lies_in[("s", t)]]
                act.activation(P1[:, t, :], ps[0:CP, 0:N], ACT.Exp, bias=nm1[:, t:t + 1],
                               accum_out=sum1[:, t:t + 1]).then_inc(act_evac, 1)
            for b in range(B):
                for c in range(NT):
                    ps = take(("pT", b, c))
                    act.activation(PT1[:, NT * b + c, :], ps[0:CP, 0:N], ACT.Copy).then_inc(act_evac, 1)
            evac96(11)
            act.wait_ge(gate_e, 2)
            act.activation(lg[:, :, :], lg[:, :, :], ACT.Exp).then_inc(gate_x, 1)
            mixture(1, ACT.Silu)

        @block.vector
        def _(dve):
            steps = [0]

            def take(key):
                dve.wait_ge(mm_dve, ready_at[key])
                return bank[lies_in[key]]

            def link(ins):
                steps[0] += 1
                ins.then_inc(dve_step, 1)
                dve.wait_ge(dve_step, steps[0])

            def ln_stats(src, tiles, rows):
                for t in tiles:
                    ins = dve.bn_stats(st[0:rows, t, :], src[:, t, :])
                link(ins)
                for t in tiles:
                    ins = dve.bn_aggr(mv[0:rows, t, :], st[0:rows, t, :])
                link(ins)
                t0, t1 = tiles[0], tiles[-1] + 1
                dve.tensor_scalar(ve[0:rows, t0:t1], mv[0:rows, t0:t1, 1], EPS, None, ALU.add).then_inc(ln_var, 1)

            def ln_apply(n, g, src, dst, tiles, rows):
                ln_apply_at(B * POWER[n] + g + 1, src, dst, tiles, rows)

            def ln_apply_at(turn, src, dst, tiles, rows):
                dve.wait_ge(ln_rstd, turn)
                for t in tiles:
                    ins = dve.tensor_scalar(dst[:, t, :], src[:, t, :], mv[0:rows, t, 0:1], rstd[0:rows, t:t + 1],
                                            ALU.subtract, ALU.mult)
                ins.then_inc(ln_y, 1)

            def pair(b):
                return range(2 * b, 2 * b + 2)

            def add_to_x(key, b, r):
                ps = take(key)
                xs = x[:, 2 * b:2 * b + 2, :]
                dve.tensor_tensor(xs, xs, ps[:, 0:NI].rearrange("p (t d) -> p t d", t=2), ALU.add)\
                    .then_inc(dve_evac, 1)
                dve.wait_ge(dve_evac, free_at[key])
                for t in pair(b):
                    ins = dve.tensor_tensor(x[:, t, :], x[:, t, :], row[:, r:r + D], ALU.add)
                link(ins)
                ln_stats(x, pair(b), 128)

            for b in range(B):
                ps = take(("x", b))
                dve.tensor_copy(x[:, 2 * b:2 * b + 2, :], ps[:, 0:NI].rearrange("p (t d) -> p t d", t=2))\
                    .then_inc(dve_evac, 1)
                dve.wait_ge(dve_evac, free_at[("x", b)])
                ln_stats(x, pair(b), 128)
            for l in range(L):
                for b in range(B):
                    ln_apply(2 * l, b, x, y_v, pair(b), 128)
                for b in range(B):
                    for p in range(2):
                        ps = take(("k", l, b, p))
                        s = NC4 * b + 2 * p
                        dve.tensor_reduce(nkmax[:, s:s + 2], ps[:, :].rearrange("p (c t) -> p c t", c=2), AX.X,
                                          ALU.max, negate=True).then_inc(kmax_ready, 1)

                def finish_q(t):
                    dve.wait_ge(q_exp, VT * l + t + 1)
                    qh = q_v[:, t, :].rearrange("p (h d) -> p h d", h=NH)
                    link(dve.tensor_reduce(qsum[:, t, :], qh, AX.X, ALU.add))
                    link(dve.reciprocal(qrec[:, t, :], qsum[:, t, :]))
                    dve.tensor_tensor(qh, qh, qrec[:, t, :].unsqueeze(2).to_broadcast([128, NH, DH]),
                                      ALU.mult).then_inc(q_norm, 1)

                for t in range(VT):
                    ps = take(("q", l, t))
                    pq = ps[:, :].rearrange("p (h d) -> p h d", h=NH)
                    link(dve.tensor_reduce(qmax[:, t, :], pq, AX.X, ALU.max))
                    dve.tensor_tensor(q_v[:, t, :].rearrange("p (h d) -> p h d", h=NH), pq,
                                      qmax[:, t, :].unsqueeze(2).to_broadcast([128, NH, DH]),
                                      ALU.subtract).then_inc(dve_evac, 1)
                    if t >= 2:
                        finish_q(t - 2)
                finish_q(VT - 2)
                finish_q(VT - 1)
                dve.wait_ge(act_evac, free_at[("k", l, B - 1, 1)])
                link(dve.reciprocal(krec[:, :], ksum[:, :]))
                if l == 0:
                    dve.wait_ge(ctx_zeroed, 1)
                for b in range(B):
                    ps = take(("ctx", l, b))
                    pc = ps[:, :].rearrange("p (c d) -> p c d", c=NC4)
                    dve.tensor_copy(ctxT[0:64, b, :, 0:64], pc[0:64, :, 0:64])
                    dve.tensor_copy(ctxT[64:128, b, :, 64:128], pc[64:128, :, 64:128]).then_inc(dve_evac, 1)
                for b in range(B):
                    ps = take(("g", l, b))
                    dve.scalar_tensor_tensor(
                        out=gmat[:, b, :, :], in0=ps[:, :].rearrange("p (c d) -> p c d", c=NC4),
                        scalar=DH ** -0.5,
                        in1=krec[:, NC4 * b:NC4 * b + NC4].unsqueeze(2).to_broadcast([128, NC4, D]),
                        op0=ALU.mult, op1=ALU.mult).then_inc(dve_evac, 1)
                for b in range(B):
                    add_to_x(("o", l, b), b, R_OUT + D * l)
                for b in range(B):
                    ln_apply(2 * l + 1, b, x, y_v, pair(b), 128)
                for b in range(B):
                    add_to_x(("f2", l, b), b, R_FF2 + D * l)
            for b in range(B):
                ln_apply(2 * L, b, x, y_v, pair(b), 128)
            for b in range(B):
                for i in range(NT):
                    n = min(CP, NI - CP * i)
                    ps = take(("h", b, i))
                    dve.tensor_tensor(h[0:n, NT * b + i, :], ps[0:n, 0:C], row[0:n, R_HEAD:R_HEAD + C],
                                      ALU.add).then_inc(dve_evac, 1)
            
            def three(b):
                return range(NT * b, NT * b + NT)

            def normalise(n, src, dst):
                for b in range(B):
                    ln_stats(src, three(b), CP)
                for b in range(B):
                    ln_apply(n, b, src, dst, three(b), CP)

            def keys_values(n, vdst):
                for b in range(B):
                    for o in range(CK):
                        ps = take(("qk", n, b, 1, o))
                        dve.tensor_copy(kT[0:CP, o, N * b:N * b + N], ps[0:CP, 0:N]).then_inc(dve_evac, 1)
                    for t in three(b):
                        ps = take(("v", n, t))
                        dve.tensor_copy(vdst(t), ps[0:CP, 0:C].rearrange("p (h d) -> p h d", h=H))\
                            .then_inc(dve_evac, 1)

            def head_values(t):
                return vpad[0:CP, t, :, 0:HD]

            def add_projection(dst, b, r):
                for i in range(NT):
                    ps = take(("proj", r, b, i))
                    t = NT * b + i
                    dve.tensor_tensor(dst[:, t, :], dst[:, t, :], ps[0:CP, 0:C], ALU.add).then_inc(dve_evac, 1)

            dve.wait_ge(ld_head, 16 * (1 + B))
            dve.wait_ge(dve_evac, free_at[("h", B - 1, NT - 1)])
            normalise(5, h, y96)
            dve.wait_ge(ld_fused, LD_FUSED)
            dve.wait_ge(fused_consts, 1)
            dve.tensor_tensor(wmix[:, :], wmix[:, :], wdelta[:, :], ALU.mult).then_inc(wmix_ready, 1)
            dve.tensor_scalar(lam_a[:, :], lam[:, :], -2.0, 1.0, ALU.mult, ALU.add).then_inc(wmix_ready, 1)
            dve.tensor_scalar(lam_b[:, :], lam[:, :], 3.0, None, ALU.mult).then_inc(wmix_ready, 1)
            dve.wait_ge(wmix_ready, 3)
            keys_values(5, head_values)
            for s in range(2):
                for p in range(2):
                    dve.wait_ge(st_y[s][p], 16)

            def first_normalised(b):
                ln_apply_at(B * 6 + 2 * b + 1, h, z, three(b), CP)
                dve.wait_ge(ln_y, B * 6 + b + 1)
                ln_stats(z, three(b), CP)

            for b in range(B):
                with dve.Fori(0, JT // 4) as it:
                    def row_max(u):
                        dve.wait_ge(tk_s, it * 4 + (JT * b + u + 1))
                        dve.tensor_reduce(nm[u][0:MR, :], bank[u][0:MR, 0:N], AX.X, ALU.max, negate=True)\
                            .then_inc(tk_max, 1)

                    def divide(u):
                        dve.wait_ge(tk_exp, it * 4 + (JT * b + u + 1))
                        dve.reciprocal(rs[u][0:MR, :], sums[u][0:MR, :]).then_inc(tk_r, 1)
                        dve.wait_ge(tk_r, it * 4 + (JT * b + u + 1))
                        dve.tensor_scalar(wms[u][:, :], wmix[:, :], rs[u][:, 0:1], None, ALU.mult)\
                            .then_inc(tk_w, 1)

                    row_max(0)
                    row_max(1)
                    divide(0)
                    row_max(2)
                    divide(1)
                    row_max(3)
                    divide(2)
                    divide(3)
                if b:
                    dve.wait_ge(dve_evac, free_at[("proj", R_P0, b - 1, NT - 1)])
                    ln_stats(h, three(b - 1), CP)
                dve.wait_ge(act_evac, free_at[("u", b, HG - 1)])
                for g in range(HG):
                    ins = dve.tensor_scalar(zT[:, g, :], uT[:, g, :], lam_b[:, g:g + 1], None, ALU.mult)
                ins.then_inc(z_ready, 1)
                if b:
                    first_normalised(b - 1)
                for g in range(HG):
                    ps = take(("w", b, g))
                    dve.scalar_tensor_tensor(out=oT[:, g, :], in0=uT[:, g, :], scalar=lam_a[:, g:g + 1],
                                             in1=ps[:, 0:N], op0=ALU.mult, op1=ALU.add).then_inc(dve_evac, 1)
                add_projection(h, b, R_P0)
            dve.wait_ge(dve_evac, free_at[("proj", R_P0, B - 1, NT - 1)])
            ln_stats(h, three(B - 1), CP)
            first_normalised(B - 1)
            for b in range(B):
                ln_apply_at(B * 6 + 2 * b + 2, z, y96, three(b), CP)
            keys_values(7, head_values)
            def keep_outputs(G, b):
                dve.wait_ge(mh_o, b + (B * G + 1))
                dve.tensor_copy(oT4[:, bass.ds(b, 1), G, :], bank[6][:, 0:N].unsqueeze(1)).then_inc(mh_oT, 1)

            def divide_head(k, j):
                dve.wait_ge(mh_exp, k * 12 + NT * (j + 1))
                dve.reciprocal(rsh[:, j, :], sumh[:, j, :]).then_inc(mh_r, 1)
                dve.wait_ge(mh_r, k * 4 + (j + 1))
                for i in range(NT):
                    ins = dve.tensor_scalar(P4[j][:, i, :], P4[j][:, i, :], rsh[:, j, i:i + 1], None, ALU.mult)
                ins.then_inc(mh_p, 1)

            def four_heads(G, b, before):
                k = b + B * G
                for j in range(4):
                    for i in range(NT):
                        s = NT * j + i
                        dve.wait_ge(mh_s, k * 12 + (s + 1))
                        dve.tensor_reduce(nmh[:, j, i:i + 1], bank[s % 4][0:CP, 0:N], AX.X, ALU.max,
                                          negate=True).then_inc(mh_max, 1)
                        if i == 0 and j:
                            divide_head(k, j - 1)
                        elif i == 0 and before:
                            divide_head(k - 1, 3)
                    if j == 1 and before:
                        keep_outputs(*before)

            for G in range(HG):
                four_heads(G, 0, (G - 1, B - 1) if G else None)
                with dve.Fori(1, B) as b:
                    four_heads(G, b, (G, b - 1))
            divide_head(B * HG - 1, 3)
            keep_outputs(HG - 1, B - 1)
            for b in range(B):
                add_projection(z, b, R_P1)
                dve.wait_ge(dve_evac, free_at[("proj", R_P1, b, NT - 1)])
                ln_stats(z, three(b), CP)
                if b:
                    ln_apply(8, b - 1, z, y96, three(b - 1), CP)
            ln_apply(8, B - 1, z, y96, three(B - 1), CP)

            def bcast(v):
                return v.unsqueeze(2).to_broadcast([CP, TT, EX])

            def experts_of_tokens():
                for t in range(TT):
                    ins = dve.max(top[:, t, :], lg[:, t, :])
                link(ins)
                for t in range(TT):
                    ins = dve.max_index(topi[:, t, :], top[:, t, :], lg[:, t, :])
                link(ins)

            def one_hot(dst, i):
                link(dve.tensor_tensor(dst[:, :, :], iota8[:, :].unsqueeze(1).to_broadcast([CP, TT, EX]),
                                       bcast(topi[:, :, i]), ALU.is_equal))

            def route(s):
                r = TT * CHOICES[s]
                for c in range(CHOICES[s]):
                    ins = dve.tensor_tensor(ohr[:, TT * c:TT * c + TT, :],
                                            iota8[:, :].unsqueeze(1).to_broadcast([CP, TT, EX]),
                                            bcast(topi[:, :, c]), ALU.is_equal)
                ins.then_inc(oh_ready, 1)
                ps = take(("count", s))
                dve.tensor_copy(cnt[:, :, 0:r, :], ps[0:CP, 0:2 * r * EX]
                                .rearrange("p (a g e) -> p a g e", a=2, g=r)).then_inc(dve_evac, 1)
                dve.wait_ge(dve_evac, free_at[("count", s)])
                old, new = cnt[:, 1, :, :], scan[0]
                d, n = 1, 0
                while d < r:
                    dve.tensor_copy(new[:, 0:d, :], old[:, 0:d, :])
                    link(dve.tensor_tensor(new[:, d:r, :], old[:, d:r, :], old[:, 0:r - d, :], ALU.add))
                    n += 1
                    old, new, d = new, scan[n % 2], 2 * d
                c3 = cmp[:, 0:EX * NB].rearrange("p (e k) -> p e k", e=EX)
                link(dve.tensor_tensor(c3, old[:, r - 1, :].unsqueeze(2).to_broadcast([CP, EX, NB]),
                                       consts[:, K_128:K_128 + NB].unsqueeze(1).to_broadcast([CP, EX, NB]),
                                       ALU.is_gt))
                link(dve.tensor_reduce(tiles_of[:, :], c3, AX.X, ALU.add))
                c3 = cmp[:, 0:EX * EX].rearrange("p (e f) -> p e f", e=EX)
                link(dve.tensor_tensor(c3, tiles_of[:, :].unsqueeze(1).to_broadcast([CP, EX, EX]), cum, ALU.mult))
                link(dve.tensor_reduce(end_of[:, :], c3, AX.X, ALU.add))
                n = SLOTS[s]
                c3 = cmp[0:1, 0:n * EX].rearrange("p (s e) -> p s e", e=EX)
                link(dve.tensor_tensor(c3, end_of[0:1, :].unsqueeze(1).to_broadcast([1, n, EX]),
                                       consts[0:1, K_S:K_S + n].unsqueeze(2).to_broadcast([1, n, EX]), ALU.is_le))
                link(dve.tensor_reduce(eidf[0:1, 0:n], c3, AX.X, ALU.add))
                dve.tensor_scalar(eid[s][0:1, 0:n], eidf[0:1, 0:n], float(EX - 1), None, ALU.min)\
                    .then_inc(ex_out[s], 1)
                link(dve.tensor_tensor(start_of[:, :], end_of[:, :], tiles_of[:, :], ALU.subtract))
                link(dve.tensor_scalar(start_of[:, :], start_of[:, :], 128.0, None, ALU.mult))
                link(dve.tensor_tensor(new[:, 0:r, :], old[:, 0:r, :], cnt[:, 1, 0:r, :], ALU.subtract))
                link(dve.tensor_tensor(new[:, 0:r, :], new[:, 0:r, :], cnt[:, 0, 0:r, :], ALU.add))
                link(dve.tensor_tensor(new[:, 0:r, :], new[:, 0:r, :],
                                       start_of[:, :].unsqueeze(1).to_broadcast([CP, r, EX]), ALU.add))
                link(dve.tensor_tensor(new[:, 0:r, :], new[:, 0:r, :], ohr[:, 0:r, :], ALU.mult))
                link(dve.tensor_reduce(posf[:, 0:r], new[:, 0:r, :], AX.X, ALU.add))
                n = SLOTS[s]
                by_128, count, place = small[:, 0, 0:r], small[:, 1, 0:r], small[:, 2, 0:r]
                ge = past[:, 0:r * (n + 1)].rearrange("p (g n) -> p g n", g=r)
                one = one_tile[:, 0:r * n].rearrange("p (g n) -> p g n", g=r)
                of_token = in_tile[:, 0:2 * r * n].rearrange("p (g a n) -> p g a n", g=r, a=2)
                link(dve.tensor_scalar(by_128, posf[:, 0:r], 1.0 / 128, None, ALU.mult))
                link(dve.tensor_tensor(ge, consts[:, K_S:K_S + n + 1].unsqueeze(1).to_broadcast([CP, r, n + 1]),
                                       by_128.unsqueeze(2).to_broadcast([CP, r, n + 1]), ALU.is_le))
                dve.tensor_tensor(one, ge[:, :, 0:n], ge[:, :, 1:n + 1], ALU.subtract)
                link(dve.tensor_reduce(count, ge, AX.X, ALU.add))
                link(dve.scalar_tensor_tensor(out=place, in0=count, scalar=-128.0, in1=posf[:, 0:r],
                                              op0=ALU.mult, op1=ALU.add))
                dve.tensor_scalar(of_token[:, :, 0, :], one, consts[:, K_P1:K_P1 + 1], None, ALU.mult)
                dve.tensor_tensor(of_token[:, :, 1, :], one,
                                  consts[:, K_ROW:K_ROW + r].unsqueeze(2).to_broadcast([CP, r, n]), ALU.mult)
                dve.tensor_tensor(place_of[:, 0:r, :],
                                  consts[:, K_LO:K_LO + 128].unsqueeze(1).to_broadcast([CP, r, 128]),
                                  place.unsqueeze(2).to_broadcast([CP, r, 128]), ALU.is_equal)\
                    .then_inc(in_slots, 1)
                ps = take(("slots", s))
                dve.tensor_copy(slot_f[:, 0:2, 0:n], ps[:, 0:2 * n].rearrange("p (a n) -> p a n", a=2))\
                    .then_inc(dve_evac, 1)
                dve.wait_ge(dve_evac, free_at[("slots", s)])
                dve.scalar_tensor_tensor(out=slot_f[:, 1, 0:n], in0=slot_f[:, 1, 0:n], scalar=float(CP),
                                         in1=slot_f[:, 0, 0:n], op0=ALU.mult, op1=ALU.add)
                link(dve.tensor_scalar(slot_f[:, 2, 0:n], slot_f[:, 0, 0:n], 0.0, vec[:, V_SPARE + s:V_SPARE + s + 1],
                                       ALU.is_equal, ALU.mult))
                dve.scalar_tensor_tensor(out=slot_row[s][:, :], in0=slot_f[:, 1, 0:n], scalar=-1.0,
                                         in1=slot_f[:, 2, 0:n], op0=ALU.add, op1=ALU.add).then_inc(ex_out[s], 1)

            def add_experts(s, weights_of_tokens):

                def place(p, n):
                    e = dve.value_load(eid[s][0:1, bass.ds(n, 1)], min_val=0, max_val=EX - 1)
                    dve.tensor_copy(w1s[p], w1all[:, bass.ds(e, 1), :].rearrange("p a f -> p (a f)"))\
                        .then_inc(ex_w[s], 1)

                dve.wait_ge(ld_w1[s], 16 * EX)
                dve.wait_ge(ex_out[s], 2)
                for p in range(2):
                    place(p, p)

                def keep_turned(p, n):
                    dve.wait_ge(ex_tp[s], n + 1)
                    for c in range(CK):
                        part = bank[p][0:CP, 128 * c:128 * c + 128]
                        if s == 0:
                            ins = dve.tensor_scalar(xsT[p][:, c, :], part, vec96[:, 2, c:c + 1],
                                                    vec96[:, 3, c:c + 1], ALU.mult, ALU.add)
                        else:
                            ins = dve.tensor_copy(xsT[p][:, c, :], part)
                    ins.then_inc(ex_xT[s], 1)

                def keep_out(p, n, turn):
                    dve.wait_ge(ex_y[s], n + 1)
                    dve.wait_ge(st_y[s][p], turn)
                    dve.tensor_copy(yout[p], bank[6 + p][:, 0:C]).then_inc(ex_out[s], 1)

                for p in range(2):
                    keep_turned(p, p)
                weights_of_tokens()
                with dve.Fori(0, SLOTS[s] // 2 - 1) as it:
                    dve.wait_ge(ex_hid[s], it * 4 + 2)
                    place(0, it * 2 + 2)
                    dve.wait_ge(ex_hid[s], it * 4 + 4)
                    for p in range(2):
                        keep_turned(p, it * 2 + (p + 2))
                    place(1, it * 2 + 3)
                    for p in range(2):
                        keep_out(p, it * 2 + p, it * 16 + 16)
                for p in range(2):
                    keep_out(p, SLOTS[s] - 2 + p, SLOTS[s] // 2 * 16)
                for t in range(TT):
                    ps = take(("b2", s, t))
                    dve.tensor_tensor(h[:, t, :], h[:, t, :], ps[0:CP, 0:C], ALU.add).then_inc(dve_evac, 1)
                dve.wait_ge(dve_evac, free_at[("b2", s, TT - 1)])

            def combine(s, b, weights):
                dve.wait_ge(gathered[s][b], 16 * CHOICES[s])
                for c in range(CHOICES[s]):
                    for t in three(b):
                        ins = dve.scalar_tensor_tensor(out=h[:, t, :], in0=back[c][:, t, :],
                                                       scalar=weights[c][:, t:t + 1], in1=h[:, t, :],
                                                       op0=ALU.mult, op1=ALU.add)
                    if c < CHOICES[s] - 1:
                        link(ins)
                ins.then_inc(h_part, 1)

            for b in range(B):
                ps = take(("gate", 0, b))
                dve.tensor_tensor(lg[:, NT * b:NT * b + NT, :],
                                  ps[0:CP, 0:NT * EX].rearrange("p (t e) -> p t e", t=NT),
                                  row[0:CP, R_GB:R_GB + EX].unsqueeze(1).to_broadcast([CP, NT, EX]),
                                  ALU.add).then_inc(dve_evac, 1)
            dve.wait_ge(dve_evac, free_at[("gate", 0, B - 1)])
            experts_of_tokens()
            dve.tensor_tensor(s12[:, :], top[:, :, 1], top[:, :, 0], ALU.subtract).then_inc(gate_e, 1)
            route(0)

            def weights_of_two():
                dve.tensor_tensor(h[:, :, :], h[:, :, :], z[:, :, :], ALU.add)
                one_hot(oh, 1)
                one_hot(cw, 0)
                dve.wait_ge(gate_x, 1)
                link(dve.tensor_scalar(s12b[:, :], s12[:, :], 1.0, None, ALU.add))
                link(dve.reciprocal(s12b[:, :], s12b[:, :]))
                link(dve.tensor_tensor(s12[:, :], s12[:, :], s12b[:, :], ALU.mult))
                link(dve.tensor_tensor(cw[:, :, :], cw[:, :, :], bcast(s12b[:, :]), ALU.mult))
                link(dve.tensor_tensor(oh[:, :, :], oh[:, :, :], bcast(s12[:, :]), ALU.mult))
                dve.tensor_tensor(cw[:, :, :], cw[:, :, :], oh[:, :, :], ALU.add).then_inc(cw_ready, 1)
                dve.wait_ge(cw_ready, 1)

            add_experts(0, weights_of_two)
            def moments(b):
                dve.wait_ge(ln_y, B * 9 + b + 1)
                for t in three(b):
                    ins = dve.bn_stats(st[0:CP, t, :], z[:, t, :])
                link(ins)
                link(dve.bn_aggr(bstat[:, b, :], st[0:CP, NT * b:NT * b + NT, :]))
                dve.tensor_copy(ms[:, 2 * b:2 * b + 1], bstat[:, b, 0:1])
                link(dve.tensor_tensor(ms[:, 2 * b + 1:2 * b + 2], bstat[:, b, 0:1], bstat[:, b, 0:1], ALU.mult))
                dve.tensor_tensor(ms[:, 2 * b + 1:2 * b + 2], ms[:, 2 * b + 1:2 * b + 2], bstat[:, b, 1:2],
                                  ALU.add).then_inc(bn_stat, 1)

            def joint_variance(b):
                ps = take(("moments", b))
                dve.tensor_scalar(msm[:, 2 * b:2 * b + 2], ps[0:CP, 0:2], 1.0 / CP, None, ALU.mult)\
                    .then_inc(dve_evac, 1)
                dve.wait_ge(dve_evac, free_at[("moments", b)])
                v = bve[:, b:b + 1]
                link(dve.tensor_tensor(v, msm[:, 2 * b:2 * b + 1], msm[:, 2 * b:2 * b + 1], ALU.mult))
                link(dve.tensor_tensor(v, msm[:, 2 * b + 1:2 * b + 2], v, ALU.subtract))
                dve.tensor_scalar(v, v, EPS, None, ALU.add).then_inc(bn_var, 1)

            def normalise_jointly(b):
                dve.wait_ge(bn_rstd, b + 1)
                dve.tensor_scalar(y96[:, NT * b:NT * b + NT, :], z[:, NT * b:NT * b + NT, :],
                                  msm[:, 2 * b:2 * b + 1], brs[:, b:b + 1], ALU.subtract, ALU.mult)\
                    .then_inc(bn_y, 1)

            for k in range(B + 1):
                if k < B:
                    combine(0, k, [s12b, s12])
                    dve.wait_ge(h_part, k + 1)
                    ln_stats(h, three(k), CP)
                if k == B:
                    for b in range(B - 2):
                        normalise_jointly(b)
                if k >= 1:
                    ln_apply(9, k - 1, h, z, three(k - 1), CP)
                    moments(k - 1)
                    joint_variance(k - 1)
            for b in range(B - 2, B):
                normalise_jointly(b)
            keys_values(10, lambda t: v1[:, t, :].rearrange("p (h d) -> p h d", h=H))
            for t in range(TT):
                ps = take(("s", t))
                dve.tensor_reduce(nm1[:, t:t + 1], ps[0:CP, 0:N], AX.X, ALU.max, negate=True).then_inc(sa_max, 1)
            dve.wait_ge(act_evac, free_at[("s", TT - 1)])
            link(dve.reciprocal(rec1[:, :], sum1[:, :]))
            for b in range(B):
                for t in three(b):
                    ps = take(("a", t))
                    dve.scalar_tensor_tensor(out=h[:, t, :], in0=ps[0:CP, 0:C], scalar=rec1[:, t:t + 1],
                                             in1=h[:, t, :], op0=ALU.mult, op1=ALU.add).then_inc(dve_evac, 1)
                dve.wait_ge(dve_evac, free_at[("a", NT * b + NT - 1)])
                ln_stats(h, three(b), CP)
                if b:
                    ln_apply(11, b - 1, h, y96, three(b - 1), CP)
            ln_apply(11, B - 1, h, y96, three(B - 1), CP)
            for b in range(B):
                ps = take(("gate", 1, b))
                dve.tensor_copy(lg[:, NT * b:NT * b + NT, :],
                                ps[0:CP, 0:NT * EX].rearrange("p (t e) -> p t e", t=NT)).then_inc(dve_evac, 1)
            dve.wait_ge(dve_evac, free_at[("gate", 1, B - 1)])
            experts_of_tokens()
            route(1)

            def weight_of_one():
                one_hot(cw, 0)
                dve.tensor_tensor(lg[:, :, :], lg[:, :, :], bcast(top[:, :, 0]), ALU.subtract).then_inc(gate_e, 1)
                dve.wait_ge(gate_x, 2)
                link(dve.tensor_reduce(s12[:, :], lg[:, :, :], AX.X, ALU.add))
                link(dve.reciprocal(s12b[:, :], s12[:, :]))
                dve.tensor_tensor(cw[:, :, :], cw[:, :, :], bcast(s12b[:, :]), ALU.mult).then_inc(cw_ready, 1)
                dve.wait_ge(cw_ready, 2)

            add_experts(1, weight_of_one)
            for b in range(B):
                combine(1, b, [s12b])

        @block.gpsimd
        def _(pool):
            pool.memset(ident[:, :], 0.0).then_inc(pool_step, 1)
            pool.memset(mhalf[:, :], -0.5)
            pool.wait_ge(pool_step, 1)
            pool.affine_select(out=ident[:, :], in_=ident[:, :], compare_op=ALU.not_equal, fill=1.0, base=0,
                               pattern=[[-1, 128]], channel_multiplier=1).then_inc(consts_ready, 1)
            pool.wait_ge(consts_ready, 1)
            zeros = z[0:64, 0, :]
            pool.memset(zeros, 0.0).then_inc(zeros_ready, 1)
            pool.wait_ge(zeros_ready, 1)
            for s in range(2):
                for p in range(2):
                    r0 = ROWS[s] - 128 + 64 * p
                    pool.dma_start(tokens[s][r0:r0 + 64, :], zeros).then_inc(st_y[s][p], 16)
            def power(n, tiles, rows):
                pool.wait_ge(ln_var, n + 1)
                t0, t1 = tiles[0], tiles[-1] + 1
                pool.tensor_tensor(rstd[0:rows, t0:t1], ve[0:rows, t0:t1], mhalf[0:rows, t0:t1], ALU.pow)\
                    .then_inc(ln_rstd, 1)

            for n in range(2 * L + 1):
                if n == 1:
                    pool.memset(ctxT, 0.0).then_inc(ctx_zeroed, 1)
                for b in range(B):
                    power(B * n + b, range(2 * b, 2 * b + 2), 128)
            
            pool.wait_ge(act_evac, free_at[("yT", 2 * L, B - 1)])
            pool.memset(vpad[0:CP, :, :, HD:HP], 0.0).then_inc(pool_step, 1)
            pool.wait_ge(pool_step, 2)
            pool.memset(kT[CP:CP + 1, 1, :], 1.0).then_inc(pool_step, 1)
            pool.wait_ge(pool_step, 3)
            pool.memset(ones[:, :], 1.0)
            for i in range(4):
                pool.memset(pt[i][:, :], 1.0)
                pool.memset(rs[i][:, :], 1.0)
            pool.iota(iota8[:, :], [[1, EX]], base=0, channel_multiplier=0, allow_small_or_imprecise_dtypes=True)\
                .then_inc(fused_consts, 1)
            for b in range(B):
                power(B * 5 + b, range(NT * b, NT * b + NT), CP)

            pool.wait_ge(act_evac, free_at[("qk", 5, B - 1, 0, CK - 1)])
            pool.wait_ge(ld_fused, LD_FUSED)

            def mixed_queries(u, n0):
                pool.tensor_tensor(
                    qg[u][0:CP, :, :].rearrange("p k (h n) -> p k h n", h=H),
                    qT[0:CP, :, bass.ds(n0, RT)].unsqueeze(2).to_broadcast([CP, CK, H, RT]),
                    wlT[:, :, :].unsqueeze(3).to_broadcast([CP, CK, H, RT]), ALU.mult).then_inc(tk_q, 1)

            for u in range(4):
                mixed_queries(u, RT * u)
            for b in range(B):
                with pool.Fori(JT // 4 * b if b else 1, JT // 4 * (b + 1)) as it:
                    for u in range(4):
                        pool.wait_ge(tk_s, it * 4 + (u - 3))
                        mixed_queries(u, it * (4 * RT) + RT * u)
                if b:
                    for i in range(2):
                        power(B * 6 + 2 * (b - 1) + i, range(NT * (b - 1), NT * b), CP)
            for i in range(2):
                power(B * 6 + 2 * (B - 1) + i, range(TT - NT, TT), CP)
            pool.wait_ge(act_evac, free_at[("qk", 7, B - 1, 0, CK - 1)])
            pool.wait_ge(dve_evac, free_at[("v", 7, TT - 1)])

            def four_heads(G, b, first):
                k = b + B * G
                for j in range(4):
                    o, r = divmod(4 * G + j, H // CK)
                    if not first:
                        pool.wait_ge(mh_s, k * 12 + (NT * (j + 1) - 12))
                        pool.nop(nofuse=True)
                    pool.tensor_tensor(qh4[j][:, :], qT[0:CP, o, bass.ds(b * N, N)],
                                       hmask[:, o, r:r + 1].to_broadcast([CP, N]), ALU.mult).then_inc(mh_q, 1)
                if not first:
                    pool.wait_ge(mh_o, k + 0)
                    pool.nop(nofuse=True)
                for j in range(4):
                    ins = pool.tensor_copy(vh4[j][:, :, :], vpad[0:CP, bass.ds(b * NT, NT), 4 * G + j, :])
                ins.then_inc(mh_v, 1)

            four_heads(0, 0, True)
            for G in range(HG):
                with pool.Fori(0 if G else 1, B) as b:
                    four_heads(G, b, False)
            def mixture(s):
                for p in range(2):
                    pool.wait_ge(st_y[s][p], 16)
                pool.wait_ge(ex_out[s], 2)
                pool.wait_ge(tokens_out[s], 16 * CHOICES[s])

                def gather(n):
                    if n >= 2:
                        pool.wait_ge(ex_tp[s], n - 1)
                    pool.indirect_dma_start(xin[n % 2], None, tokens[s],
                                            bass.IndirectOffsetOnAxis(ap=slot_row[s][:, n:n + 1], axis=0))\
                        .then_inc(ld_x[n % 2], 16)

                def scatter(n):
                    pool.wait_ge(ex_out[s], n + 3)
                    if n:
                        pool.wait_ge(st_y[s][(n - 1) % 2], 16 + 16 * ((n + 1) // 2))
                    pool.indirect_dma_start(results[s],
                                            bass.IndirectOffsetOnAxis(ap=slot_row[s][:, n:n + 1], axis=0),
                                            yout[n % 2], None).then_inc(st_y[s][n % 2], 16)

                for n in range(4):
                    gather(n)
                for n in range(0, SLOTS[s], 2):
                    if n + 4 < SLOTS[s]:
                        gather(n + 4)
                        gather(n + 5)
                    scatter(n)
                    scatter(n + 1)

            for b in range(B):
                power(B * 8 + b, range(NT * b, NT * b + NT), CP)
            mixture(0)
            def joint_power(b):
                pool.wait_ge(bn_var, b + 1)
                pool.tensor_tensor(brs[:, b:b + 1], bve[:, b:b + 1], mhalf[0:CP, 0:1], ALU.pow).then_inc(bn_rstd, 1)

            for b in range(B - 1):
                power(B * 9 + b, range(NT * b, NT * b + NT), CP)
            for b in range(B - 2):
                joint_power(b)
            power(B * 9 + B - 1, range(TT - NT, TT), CP)
            for b in range(B - 2, B):
                joint_power(b)
            for b in range(B):
                power(B * 10 + b, range(NT * b, NT * b + NT), CP)
            mixture(1)

        @block.sync
        def _(sp):
            sp.dma_start(convw, a["conv_w"]).then_inc(ld_conv, 16)
            sp.dma_start(vec[:, :], a["vec"]).then_inc(ld_row, 16)
            sp.dma_start(row[:, :], a["row"].to_broadcast([128, R_END])).then_inc(ld_row, 16)
            for i in range(8):
                sp.dma_start(patches[:, 2 * i:2 * i + 2, :], a["patches"][:, 2 * i:2 * i + 2, :])\
                    .then_inc(ld_patch[i], 16)
            for l in range(L):
                sp.dma_start(wqkv[l], a["qkv_w"][l]).then_inc(ld_layer[l], 16)
                sp.dma_start(wout[l], a["out_w"][l]).then_inc(ld_layer[l], 16)
                sp.dma_start(wff1[l], a["ff1_w"][l]).then_inc(ld_layer[l], 16)
                sp.dma_start(wff2[l], a["ff2_w"][l]).then_inc(ld_layer[l], 16)
            sp.dma_start(headw[:, :], a["head_w"]).then_inc(ld_head, 16)
            for b in range(B):
                sp.dma_start(h[64:CP, NT * b + 2, :], a["txt"][b]).then_inc(ld_head, 16)
            
            sp.dma_start(consts[:, :], a["consts"]).then_inc(ld_fused, 16)
            for i in range(3):
                sp.dma_start(wqkv96[i][:, :, :], a["qkv96"][i]).then_inc(ld_fused, 16)
            sp.dma_start(wlT[:, :, :], a["wlT"]).then_inc(ld_fused, 16)
            sp.dma_start(wmix[:, :], a["wmix"]).then_inc(ld_fused, 16)
            sp.dma_start(wdelta[:, :], a["wdelta"]).then_inc(ld_fused, 16)
            sp.dma_start(lam[:, :], a["lam"]).then_inc(ld_fused, 16)
            for i in range(4):
                sp.dma_start(qg[i][CP:CP + 1, 1, :], a["bl"]).then_inc(ld_fused, 16)
            sp.dma_start(hmask[:, :, :], a["hmask"]).then_inc(ld_fused, 16)
            sp.dma_start(vec96[:, :, :], a["vec96"]).then_inc(ld_fused, 16)
            for i in range(2):
                sp.dma_start(gate_w[i][:, :, :], a["gate_w"][i]).then_inc(ld_fused, 16)
                sp.dma_start(b2[i][:, :], a["b2"][i]).then_inc(ld_fused, 16)
                sp.dma_start(wproj[i][:, :, :], a["wproj"][i]).then_inc(ld_fused, 16)
            def load_w1(s):
                for e in range(EX):
                    sp.dma_start(w1all[:, e, :], a["ew1"][s, e].rearrange("p k f -> p (k f)")).then_inc(ld_w1[s], 16)

            def load_w2(s, experts):
                for e in experts:
                    sp.dma_start(w2all[:, e, :], a["ew2"][s, e]).then_inc(ld_w2[s], 16)

            past_values = [e for e in range(EX) if W2_AT + WE * e >= 2 * CK * T + TT * H * HP]
            sp.wait_ge(dve_evac, free_at[("h", B - 1, NT - 1)])
            load_w2(0, past_values)
            for s in range(2):
                if s == 0:
                    sp.wait_ge(dve_evac, free_at[("proj", R_P1, B - 1, NT - 1)])
                    load_w1(0)
                    sp.wait_ge(ln_y, B * 8 + B)
                else:
                    sp.wait_ge(ex_hid[0], 2 * SLOTS[0])
                    load_w1(1)
                    sp.wait_ge(dve_evac, free_at[("a", TT - 1)])
                    load_w2(1, range(EX // 2))
                    sp.wait_ge(ln_y, B * 10 + B)
                for c in range(CHOICES[s]):
                    sp.dma_start(tokens[s][T * c:T * (c + 1), :].rearrange("(t p) c -> p t c", p=CP), y96)\
                        .then_inc(tokens_out[s], 16)
                load_w2(s, range(EX // 2, EX) if s else [e for e in range(EX) if e not in past_values])
                for p in range(2):
                    sp.wait_ge(st_y[s][p], 16 + 16 * (SLOTS[s] // 2))
                for b in range(B):
                    for c in range(CHOICES[s]):
                        r0 = T * c + N * b
                        sp.dma_start(back[c][:, NT * b:NT * b + NT, :],
                                     results[s][r0:r0 + N, :].rearrange("(t p) c -> p t c", p=CP))\
                            .then_inc(gathered[s][b], 16)
            for b in range(B):
                sp.wait_ge(h_part, B + b + 1)
                sp.dma_start(out[b].rearrange("(i p) c -> p i c", p=CP), h[:, NT * b:NT * b + NT, :])\
                    .then_inc(stored, 16)
            sp.wait_ge(stored, 16 * B)



def lay_out(i):
    import numpy as np

    def g(name):
        return np.asarray(i[name])

    def cols(v):
        return v.reshape(-1, 128).T

    def cols96(v):
        return v.reshape(CK, CP).T

    def rows_to_tiles(w, p):
        return w.reshape(w.shape[0] // p, p, w.shape[1]).transpose(1, 0, 2)

    t = "L0_tok_"
    o = {}
    im = g("x").reshape(B, 32, 16, 8, 16, 8)
    o["patches"] = im.transpose(1, 3, 5, 0, 2, 4).reshape(KC, 128, TI).transpose(1, 0, 2)
    o["conv_w"] = rows_to_tiles(g(t + "conv_w").reshape(D, 2048).T, 128)
    o["qkv_w"] = g(t + "qkv_w")
    o["out_w"] = np.stack([rows_to_tiles(w, 128) for w in g(t + "out_w")])
    o["ff1_w"] = g(t + "ff1_w")
    o["ff2_w"] = np.stack([rows_to_tiles(w, 128) for w in g(t + "ff2_w")])
    o["head_w"] = g(t + "head_w")
    o["txt"] = g("txt")
    o["vec"] = np.concatenate([cols(g(t + n)) for n in ("conv_b", "ln1_g", "ln1_b", "ln2_g", "ln2_b",
                                                        "lnf_g", "lnf_b", "ff1_b")]
                              + [(1.0 + T * r + np.arange(128, dtype=np.float32))[:, None] for r in CHOICES],
                              axis=1).astype(np.float32)
    o["row"] = np.concatenate([g(n).reshape(-1) for n in (
        t + "out_b", t + "ff2_b", t + "head_b", "L0_attn_b_proj", "L0_ffn_proj_b", "L0_attn_lamb",
        "L0_ffn_gate_b")])[None]
    
    o["consts"] = np.concatenate([
        np.triu(np.ones((CP, CP), np.float32), 1),
        np.tile(np.tril(np.ones((EX, EX), np.float32)).reshape(1, -1), (CP, 1)),
        np.tile(np.arange(NB, dtype=np.float32)[None] * 128, (CP, 1)),
        np.tile(np.arange(max(SLOTS) + 2, dtype=np.float32)[None], (CP, 1)),
        np.tile(np.arange(GMAX, dtype=np.float32)[None], (CP, 1)),
        1.0 + np.arange(CP, dtype=np.float32)[:, None],
        np.tile(np.arange(-128, 0, dtype=np.float32)[None], (CP, 1))], axis=1).astype(np.float32)
    s = "L0_attn_"
    f = "L0_ffn_"
    o["qkv96"] = np.stack([rows_to_tiles(w, CP) for w in (
        g(s + "W_qkv"), g(f + "qkv_w").T,
        np.concatenate([g("L1_attn_W" + n).T for n in "qkv"], axis=1))])
    o["wlT"] = np.repeat(g(s + "W_l"), HD, axis=0).reshape(CK, CP, H).transpose(1, 0, 2)
    o["wmix"] = np.concatenate([np.repeat(np.repeat(g(s + "W_w"), RT, axis=0), RT, axis=1),
                                np.repeat(g(s + "b_w"), RT)[None]])
    o["wdelta"] = np.concatenate([np.tile(np.eye(RT, dtype=np.float32), (H, H)), np.ones((1, MR), np.float32)])
    o["lam"] = np.repeat(g(s + "lamb").reshape(HG, 4), HP, axis=1).T
    o["bl"] = np.repeat(g(s + "b_l"), RT)[None]
    o["hmask"] = np.repeat(np.eye(H // CK, dtype=np.float32), HD, axis=0)[:, None].repeat(CK, axis=1)
    o["vec96"] = np.stack([cols96(g(f + n)) for n in ("ln1_g", "ln1_b", "ln2_g", "ln2_b")], axis=1)

    def by_column_tile(w):
        p = np.zeros((4, HP, HG, C), np.float32)
        p[:, 0:HD] = w.reshape(HG, 4, HD, C).transpose(1, 2, 0, 3)
        return p.reshape(128, HG, C)

    o["wproj"] = np.stack([by_column_tile(w) for w in (g(s + "W_proj"), g(f + "proj_w").T)])
    o["gate_w"] = np.stack([rows_to_tiles(w, CP) for w in (g(f + "gate_w").T, g("L1_ffn_Wg"))])
    o["b2"] = np.stack([g(f + "b2"), g("L1_ffn_b2")])
    w1 = [g(f + "w1").transpose(0, 2, 1), g("L1_ffn_W1")]
    w2 = [g(f + "w2").transpose(0, 2, 1), g("L1_ffn_W2")]
    b1 = [g(f + "b1"), g("L1_ffn_b1")]
    o["ew1"] = np.stack([w.reshape(EX, CK, CP, F).transpose(0, 2, 1, 3) for w in w1])
    o["ew2"] = np.concatenate([
        np.stack([w.reshape(EX, FC, 128, C).transpose(0, 2, 1, 3).reshape(EX, 128, FC * C) for w in w2]),
        np.stack([v.reshape(EX, FC, 128).transpose(0, 2, 1) for v in b1])], axis=3)
    return {n: np.ascontiguousarray(v) for n, v in o.items()}


def kernel(**inputs):
    import concourse.bacc as bacc
    from concourse import mybir as mb
    from concourse.bass_utils import run_bass_kernel_spmd

    nc = bacc.Bacc("TRN2", target_bir_lowering=False, num_devices=1)
    arrays = lay_out(inputs)
    aps = {n: nc.dram_tensor("in_" + n, v.shape, mb.dt.from_np(v.dtype), kind="ExternalInput").ap()
           for n, v in arrays.items()}
    out = nc.dram_tensor("out_h", (B, N, C), F32, kind="ExternalOutput").ap()
    build(nc, aps, out)
    r = run_bass_kernel_spmd(nc, [{"in_" + n: v for n, v in arrays.items()}], core_ids=[0])
    return r.results[0]["out_h"]
```
